# Optimizing a Trainium2 kernel written in Bass

```python
import numpy as np
import jax
import jax.numpy as jnp

def _softmax(x, axis=-1):
    return jax.nn.softmax(x, axis=axis)

def _gelu(x):
    return jax.nn.gelu(x, approximate=True)

def _silu(x):
    return jax.nn.silu(x)

def _sigmoid(x):
    return jax.nn.sigmoid(x)

def _layernorm(x, axis=-1, eps=1e-05):
    m = jnp.mean(x, axis=axis, keepdims=True)
    v = jnp.var(x, axis=axis, keepdims=True)
    return (x - m) / jnp.sqrt(v + eps)

def _scatter_add(tgt, idx, src, axis=0):
    return tgt.at[idx].add(src)

def _segment_sum(src, seg, n):
    return jax.ops.segment_sum(src, seg, n)
kernel_name = 'mk_xattn_ffn_d2_seqx_r8_80cbb8'

def setup_inputs(seed: int=0):
    np.random.seed(seed)
    _w = jnp.asarray

    def _rec_inputs():
        import jax
        import jax.numpy as jnp
        _rk = jax.random.key(seed)
        x = -0.000125 + 0.9999 * jax.random.normal(jax.random.fold_in(_rk, 1), (32, 64, 256), jnp.float32)
        _lenS = 64 - jax.random.randint(jax.random.fold_in(_rk, 7), (32,), 0, max(1, 64 // 4) + 1, jnp.int32)
        _lenS2 = 64 - jax.random.randint(jax.random.fold_in(_rk, 8), (32,), 0, max(1, 64 // 4) + 1, jnp.int32)
        _ctx_2048P = jax.random.normal(jax.random.fold_in(_rk, 11), (32, 16, 256), jnp.float32)
        _ctx_2048c = jax.random.dirichlet(jax.random.fold_in(_rk, 511), 0.3 * jnp.ones((16,), jnp.float32), (32, 64))
        _ctx_2048t = jnp.einsum('bsk,bkd->bsd', _ctx_2048c, _ctx_2048P)
        _ctx_2048t = _ctx_2048t * jax.lax.rsqrt(jnp.mean(jnp.square(_ctx_2048t)) + 1e-12) * 0.953939
        ctx_2048 = -1.52775e-05 + 0.999936 * (_ctx_2048t + 0.3 * jax.random.normal(jax.random.fold_in(_rk, 611), (32, 64, 256), jnp.float32))
        _validS = jnp.arange(64)[None, :] < _lenS[:, None]
        _validS2 = jnp.arange(64)[None, :] < _lenS2[:, None]
        _causal = jnp.tril(jnp.ones((64, 64), dtype=bool))
        mask_BxS2_ik0 = jnp.where(jnp.broadcast_to(_validS2[:, :], (32, 64)), 0, 1).astype(jnp.int32)
        return (x, ctx_2048, mask_BxS2_ik0)
    x, ctx_2048, mask_BxS2_ik0 = _rec_inputs()

    def _L0_xattn_setup():
        import jax, jax.numpy as jnp
        import numpy as np
        EPS = 1e-06
        NUM_HEADS = 16

        def _feature_map(x):
            return jnp.where(x > 0, x + 1.0, jnp.exp(x))
        key = jax.random.key(seed)
        ks = jax.random.split(key, 7)
        B, L, S, D = (4, 512, 512, 256)
        sc = 1.0 / np.sqrt(D)
        return {'query': jax.random.normal(ks[0], (B, L, D), jnp.float32), 'kv': jax.random.normal(ks[1], (B, S, D), jnp.float32), 'Wq': jax.random.normal(ks[2], (D, D), jnp.float32) * sc, 'Wg': jax.random.normal(ks[3], (D, D), jnp.float32) * sc, 'bg': jnp.ones((D,), jnp.float32), 'Wkv': jax.random.normal(ks[4], (2 * D, D), jnp.float32) * sc, 'Wo': jax.random.normal(ks[5], (D, D), jnp.float32) * sc}
    _L0_xattn_all = _L0_xattn_setup()
    _L0_xattn_in = {k: v for k, v in _L0_xattn_all.items() if k in ('Wq', 'Wg', 'bg', 'Wkv', 'Wo')}
    del _L0_xattn_all

    def _L0_ffn_setup():
        import jax, jax.numpy as jnp
        import numpy as np
        N_EXPERTS = 8
        TOP_K = 2
        C = 256
        H = 128
        HS = 256
        B, T = (1, 64)
        SCALE = 0.02
        key = jax.random.key(seed)
        ks = jax.random.split(key, 10)
        x = jax.random.normal(ks[0], (B, T, C), dtype=jnp.float32)
        gate_w = jax.random.normal(ks[1], (N_EXPERTS, C), dtype=jnp.float32) * SCALE
        w_gate = jax.random.normal(ks[2], (N_EXPERTS, H, C), dtype=jnp.float32) * SCALE
        w_up = jax.random.normal(ks[3], (N_EXPERTS, H, C), dtype=jnp.float32) * SCALE
        w_down = jax.random.normal(ks[4], (N_EXPERTS, C, H), dtype=jnp.float32) * SCALE
        sh_gate = jax.random.normal(ks[5], (HS, C), dtype=jnp.float32) * SCALE
        sh_up = jax.random.normal(ks[6], (HS, C), dtype=jnp.float32) * SCALE
        sh_down = jax.random.normal(ks[7], (C, HS), dtype=jnp.float32) * SCALE
        se_gate_w = jax.random.normal(ks[8], (1, C), dtype=jnp.float32) * SCALE
        return {'x': x, 'gate_w': gate_w, 'w_gate': w_gate, 'w_up': w_up, 'w_down': w_down, 'sh_gate': sh_gate, 'sh_up': sh_up, 'sh_down': sh_down, 'se_gate_w': se_gate_w}
    _L0_ffn_all = _L0_ffn_setup()
    _L0_ffn_in = {k: v for k, v in _L0_ffn_all.items() if k in ('gate_w', 'w_gate', 'w_up', 'w_down', 'sh_gate', 'sh_up', 'sh_down', 'se_gate_w')}
    del _L0_ffn_all

    def _L1_xattn_setup():
        import jax, jax.numpy as jnp
        import numpy as np
        import math
        H = 256
        NH = 16
        HD = H // NH
        EPS_LN = 1e-05
        RES_SCALE_MAX = 0.3

        def _nan_clean(x, lim=10000.0):
            return jnp.nan_to_num(x, nan=0.0, posinf=lim, neginf=-lim)
        key = jax.random.key(seed)
        ks = jax.random.split(key, 12)
        B, S, T = (4, 256, 32)
        std = 1.0 / math.sqrt(H)
        return {'hidden_states': jax.random.normal(ks[0], (B, S, H), jnp.float32), 'audio_tokens': jax.random.normal(ks[1], (B, T, H), jnp.float32), 'attention_mask': jax.random.randint(ks[2], (B, T), 0, 2, jnp.int32), 'Wq': jax.random.normal(ks[3], (H, H), jnp.float32) * std, 'bq': jnp.zeros((H,), jnp.float32), 'Wk': jax.random.normal(ks[4], (H, H), jnp.float32) * std, 'bk': jnp.zeros((H,), jnp.float32), 'Wv': jax.random.normal(ks[5], (H, H), jnp.float32) * std, 'bv': jnp.zeros((H,), jnp.float32), 'Wo': jax.random.normal(ks[6], (H, H), jnp.float32) * std, 'bo': jnp.zeros((H,), jnp.float32), 'ln_gamma': jnp.ones((H,), jnp.float32), 'ln_beta': jnp.zeros((H,), jnp.float32), 'residual_scale': jnp.float32(0.05)}
    _L1_xattn_all = _L1_xattn_setup()
    _L1_xattn_in = {k: v for k, v in _L1_xattn_all.items() if k in ('Wq', 'bq', 'Wk', 'bk', 'Wv', 'bv', 'Wo', 'bo', 'ln_gamma', 'ln_beta', 'residual_scale')}
    del _L1_xattn_all

    def _L1_ffn_setup():
        import jax, jax.numpy as jnp
        import numpy as np
        key = jax.random.key(seed)
        k1, k2, k3, k4, k5 = jax.random.split(key, 5)
        B, L, H, N = (2, 256, 256, 1024)
        x = jax.random.normal(k1, (B, L, H), dtype=jnp.float32)
        W0 = jax.random.normal(k2, (N, H), dtype=jnp.float32) * (1.0 / np.sqrt(H))
        bias0 = jax.random.normal(k3, (N,), dtype=jnp.float32) * 0.02
        W1 = jax.random.normal(k4, (H, N), dtype=jnp.float32) * (1.0 / np.sqrt(N))
        bias1 = jax.random.normal(k5, (H,), dtype=jnp.float32) * 0.02
        return {'x': x, 'W0': W0, 'bias0': bias0, 'W1': W1, 'bias1': bias1}
    _L1_ffn_all = _L1_ffn_setup()
    _L1_ffn_in = {k: v for k, v in _L1_ffn_all.items() if k in ('W0', 'bias0', 'W1', 'bias1')}
    del _L1_ffn_all
    return {'x': x, 'ctx_2048': ctx_2048, 'mask_BxS2_ik0': mask_BxS2_ik0, 'L0_xattn_Wq': _L0_xattn_in['Wq'], 'L0_xattn_Wg': _L0_xattn_in['Wg'], 'L0_xattn_bg': _L0_xattn_in['bg'], 'L0_xattn_Wkv': _L0_xattn_in['Wkv'], 'L0_xattn_Wo': _L0_xattn_in['Wo'], 'L0_ffn_gate_w': _L0_ffn_in['gate_w'], 'L0_ffn_w_gate': _L0_ffn_in['w_gate'], 'L0_ffn_w_up': _L0_ffn_in['w_up'], 'L0_ffn_w_down': _L0_ffn_in['w_down'], 'L0_ffn_sh_gate': _L0_ffn_in['sh_gate'], 'L0_ffn_sh_up': _L0_ffn_in['sh_up'], 'L0_ffn_sh_down': _L0_ffn_in['sh_down'], 'L0_ffn_se_gate_w': _L0_ffn_in['se_gate_w'], 'L1_xattn_Wq': _L1_xattn_in['Wq'], 'L1_xattn_bq': _L1_xattn_in['bq'], 'L1_xattn_Wk': _L1_xattn_in['Wk'], 'L1_xattn_bk': _L1_xattn_in['bk'], 'L1_xattn_Wv': _L1_xattn_in['Wv'], 'L1_xattn_bv': _L1_xattn_in['bv'], 'L1_xattn_Wo': _L1_xattn_in['Wo'], 'L1_xattn_bo': _L1_xattn_in['bo'], 'L1_xattn_ln_gamma': _L1_xattn_in['ln_gamma'], 'L1_xattn_ln_beta': _L1_xattn_in['ln_beta'], 'L1_xattn_residual_scale': _L1_xattn_in['residual_scale'], 'L1_ffn_W0': _L1_ffn_in['W0'], 'L1_ffn_bias0': _L1_ffn_in['bias0'], 'L1_ffn_W1': _L1_ffn_in['W1'], 'L1_ffn_bias1': _L1_ffn_in['bias1']}

def reference(x, ctx_2048, mask_BxS2_ik0, L0_xattn_Wq, L0_xattn_Wg, L0_xattn_bg, L0_xattn_Wkv, L0_xattn_Wo, L0_ffn_gate_w, L0_ffn_w_gate, L0_ffn_w_up, L0_ffn_w_down, L0_ffn_sh_gate, L0_ffn_sh_up, L0_ffn_sh_down, L0_ffn_se_gate_w, L1_xattn_Wq, L1_xattn_bq, L1_xattn_Wk, L1_xattn_bk, L1_xattn_Wv, L1_xattn_bv, L1_xattn_Wo, L1_xattn_bo, L1_xattn_ln_gamma, L1_xattn_ln_beta, L1_xattn_residual_scale, L1_ffn_W0, L1_ffn_bias0, L1_ffn_W1, L1_ffn_bias1):
    import jax
    import jax.numpy as jnp

    def _L0_xattn_ref(query, kv, Wq, Wg, bg, Wkv, Wo):
        import jax, jax.numpy as jnp
        import numpy as np
        EPS = 1e-06
        NUM_HEADS = 16

        def _feature_map(x):
            return jnp.where(x > 0, x + 1.0, jnp.exp(x))
        B, L, D = query.shape
        S = kv.shape[1]
        H = NUM_HEADS
        hd = D // H
        q = query @ Wq.T
        gate = jax.nn.sigmoid(query @ Wg.T + bg)
        kvp = kv @ Wkv.T
        k, v = jnp.split(kvp, 2, axis=-1)
        q = _feature_map(q.reshape(B, L, H, hd).transpose(0, 2, 1, 3))
        k = _feature_map(k.reshape(B, S, H, hd).transpose(0, 2, 1, 3))
        v = v.reshape(B, S, H, hd).transpose(0, 2, 1, 3)
        kv_summary = jnp.einsum('bhsd,bhse->bhde', k, v)
        k_sum = k.sum(axis=-2)
        z = 1.0 / (jnp.einsum('bhld,bhd->bhl', q, k_sum)[..., None] + EPS)
        attn = jnp.einsum('bhld,bhde->bhle', q, kv_summary) * z
        attn = attn.transpose(0, 2, 1, 3).reshape(B, L, D)
        out = attn * gate @ Wo.T
        return out

    def _L0_ffn_ref(x, gate_w, w_gate, w_up, w_down, sh_gate, sh_up, sh_down, se_gate_w):
        import jax, jax.numpy as jnp
        import numpy as np
        N_EXPERTS = 8
        TOP_K = 2
        C = 256
        H = 128
        HS = 256
        B, T = (1, 64)
        SCALE = 0.02
        Bb, Tt, Cc = x.shape
        xf = x.reshape(-1, Cc)
        scores = xf @ gate_w.T
        ew, ei = jax.lax.top_k(scores, TOP_K)
        ew = jax.nn.softmax(ew, axis=-1)
        x1 = jax.nn.silu(jnp.einsum('td,ehd->teh', xf, w_gate))
        x3 = jnp.einsum('td,ehd->teh', xf, w_up)
        expert_out = jnp.einsum('teh,edh->ted', x1 * x3, w_down)
        onehot = jax.nn.one_hot(ei, N_EXPERTS, dtype=ew.dtype)
        comb = jnp.einsum('ta,tae->te', ew, onehot)
        routed = jnp.einsum('te,ted->td', comb, expert_out)
        shared = jax.nn.silu(xf @ sh_gate.T) * (xf @ sh_up.T) @ sh_down.T
        sgate = jax.nn.sigmoid(xf @ se_gate_w.T)
        return (routed + sgate * shared).reshape(Bb, Tt, Cc)

    def _L1_xattn_ref(hidden_states, audio_tokens, attention_mask, Wq, bq, Wk, bk, Wv, bv, Wo, bo, ln_gamma, ln_beta, residual_scale):
        import jax, jax.numpy as jnp
        import numpy as np
        import math
        H = 256
        NH = 16
        HD = H // NH
        EPS_LN = 1e-05
        RES_SCALE_MAX = 0.3

        def _nan_clean(x, lim=10000.0):
            return jnp.nan_to_num(x, nan=0.0, posinf=lim, neginf=-lim)
        B, S, _ = hidden_states.shape
        T = audio_tokens.shape[1]
        hs = _nan_clean(hidden_states).astype(jnp.float32)
        at = _nan_clean(audio_tokens).astype(jnp.float32)

        def proj(x, W, b, L):
            y = x @ W.T + b
            return y.reshape(B, L, NH, HD).transpose(0, 2, 1, 3)
        q = _nan_clean(proj(hs, Wq, bq, S))
        k = _nan_clean(proj(at, Wk, bk, T))
        v = _nan_clean(proj(at, Wv, bv, T))
        scale = max(math.sqrt(HD), 1e-08)
        scores = jnp.einsum('bhsd,bhtd->bhst', q, k) / scale
        scores = jnp.clip(scores, -50.0, 50.0)
        scores = jnp.nan_to_num(scores, nan=0.0, posinf=50.0, neginf=-50.0)
        attend = (attention_mask.astype(jnp.float32) > 0.5)[:, None, None, :]
        scores = jnp.where(attend, scores, -10000.0)
        scores = jnp.clip(scores, -50.0, 50.0)
        probs = jax.nn.softmax(scores, axis=-1)
        probs = jnp.nan_to_num(probs, nan=0.0, posinf=1.0, neginf=0.0)
        probs = probs / (probs.sum(axis=-1, keepdims=True) + 1e-08)
        ctx = jnp.einsum('bhst,bhtd->bhsd', probs, v)
        ctx = ctx.transpose(0, 2, 1, 3).reshape(B, S, H)
        delta = _nan_clean(ctx @ Wo.T + bo)
        rs = jnp.clip(residual_scale, 0.0, RES_SCALE_MAX)
        delta = rs * delta
        mu = delta.mean(axis=-1, keepdims=True)
        var = jnp.mean((delta - mu) ** 2, axis=-1, keepdims=True)
        delta = (delta - mu) / jnp.sqrt(var + EPS_LN) * ln_gamma + ln_beta
        return delta

    def _L1_ffn_ref(x, W0, bias0, W1, bias1):
        import jax, jax.numpy as jnp
        import numpy as np
        B, L, H = x.shape
        X = x.reshape(-1, H).astype(jnp.float16)
        D = jnp.dot(X.astype(jnp.float32), W0.T) + bias0
        D = jax.nn.gelu(D, approximate=False).astype(jnp.float16)
        E = jnp.dot(D.astype(jnp.float32), W1.T) + bias1
        return E.astype(jnp.float16).reshape(B, L, H)
    x = x + _L0_xattn_ref(_layernorm(x, axis=-1), ctx_2048, L0_xattn_Wq, L0_xattn_Wg, L0_xattn_bg, L0_xattn_Wkv, L0_xattn_Wo)
    x = x + _L0_ffn_ref(_layernorm(x, axis=-1), L0_ffn_gate_w, L0_ffn_w_gate, L0_ffn_w_up, L0_ffn_w_down, L0_ffn_sh_gate, L0_ffn_sh_up, L0_ffn_sh_down, L0_ffn_se_gate_w)
    x = x + _L1_xattn_ref(_layernorm(x, axis=-1), ctx_2048, mask_BxS2_ik0, L1_xattn_Wq, L1_xattn_bq, L1_xattn_Wk, L1_xattn_bk, L1_xattn_Wv, L1_xattn_bv, L1_xattn_Wo, L1_xattn_bo, L1_xattn_ln_gamma, L1_xattn_ln_beta, L1_xattn_residual_scale)
    x = x + _L1_ffn_ref(_layernorm(x, axis=-1), L1_ffn_W0, L1_ffn_bias0, L1_ffn_W1, L1_ffn_bias1)
    return x

_drawn_inputs = setup_inputs


def setup_inputs(seed=0):
    import zlib

    import numpy as np

    out = dict(_drawn_inputs(seed))
    spreads = {'L0_xattn_bg': (1.0, 0.6),
     'L1_xattn_bq': (0.0, 1.919),
     'L1_xattn_bk': (0.0, 2.0),
     'L1_xattn_bv': (0.0, 0.525),
     'L1_xattn_bo': (0.0, 0.517),
     'L1_xattn_ln_gamma': (1.0, 0.6),
     'L1_xattn_ln_beta': (0.0, 0.75)}
    factors = {'L0_xattn_Wq': 4.887,
     'L0_ffn_gate_w': 8.0,
     'L0_ffn_w_gate': 8.0,
     'L0_ffn_w_up': 8.0,
     'L0_ffn_w_down': 8.0,
     'L0_ffn_sh_gate': 8.0,
     'L0_ffn_sh_up': 8.0,
     'L0_ffn_sh_down': 8.0,
     'L0_ffn_se_gate_w': 8.0,
     'L1_ffn_bias0': 40.454,
     'L1_ffn_bias1': 28.317}
    for name, (base, spread) in spreads.items():
        noise = np.random.default_rng([zlib.crc32(name.encode()), seed]).standard_normal(out[name].shape)
        drawn = base * np.exp(spread * noise) if base else spread * noise
        out[name] = jnp.asarray(drawn.astype(out[name].dtype))
    for name, factor in factors.items():
        out[name] = (out[name] * factor).astype(out[name].dtype)
    return out
```

```python
from contextlib import ExitStack

import numpy as np

import concourse.bass as bass
from concourse import mybir

F32 = mybir.dt.float32
F32R = mybir.dt.float32r
F16 = mybir.dt.float16
I32 = mybir.dt.int32
U32 = mybir.dt.uint32
ALU = mybir.AluOpType
ACT = mybir.ActivationFunctionType

P = 128
BATCHES, SEQ, D = 32, 64, 256
TOKENS = BATCHES * SEQ
TILES = TOKENS // P
PER_TILE = P // SEQ
KC = D // P
HEADS, HD = 16, 16
HPC = P // HD
PAIRS = HEADS // 2
PPC = P // (2 * HD)
EXPERTS, EH = 8, 128
SH = 256
FF = 1024
NFF = FF // P
GROUPS = TILES // 2
VC = P + HPC
PVC = 2 * HD + 2

L0_KV, L0_Q, L0_G, L0_O = 0, 2 * 512, 2 * 512 + 2 * D, 2 * 512 + 4 * D
L0_COLS = L0_O + 2 * D
W1_COLS = 2 * EXPERTS * EH + 2 * SH + EXPERTS + 2
FFN_USED = KC * W1_COLS + (EXPERTS + SH // P) * D
FFN_CHUNK = -(-FFN_USED // TILES // 2) * 2
FFN_COLS = FFN_CHUNK * TILES
L1_Q, L1_K, L1_V, L1_O = 0, 2 * D, 4 * D, 6 * D
L1_W0 = 8 * D
L1_W1 = L1_W0 + KC * FF
L1_COLS = L1_W1 + NFF * D
L1_CHUNK = L1_COLS // TILES

ARENA_R = 5120
ARENA_F = 6784

B_T, B_QG, B_KV, B_A, B_O, B_S, B_TA = 0, 1, 2, 3, 4, 5, 7
F_T, F_G0, F_U0, F_G1, F_U1, F_O, F_H = 0, 1, 2, 3, 4, 5, 6
X_T, X_QK, X_VO, X_C, X_S = 0, 1, 2, 3, 4
M_T, M_H, M_O = 0, 1, 5


class Slot:

    def __init__(self, at, ring, count):
        self.at, self.ring, self.count = at, ring, count

    def tile(self, ahead):
        t = self.at + ahead
        if isinstance(t, int) and not 0 <= t < self.count:
            return None
        return t, (self.ring + ahead) % 2


def slots(eng, count, first, last, body, low=4):
    high = (count - 1) // 2 * 2
    for s in range(first, low):
        body(Slot(s, s % 2, count))
    with eng.Fori(low // 2, high // 2) as i:
        body(Slot(i * 2, 0, count))
        body(Slot(i * 2 + 1, 1, count))
    for s in range(high, last + 1):
        body(Slot(s, s % 2, count))


def after(eng, sem, t, back=0, base=0, per=1, extra=0):
    if isinstance(t, int) and t - back < 0:
        if base:
            eng.wait_ge(sem, base)
        return
    eng.wait_ge(sem, t * per + (base + per * (1 - back) + extra))


def after_plain(eng, held, sem, t, base=0):
    value = t + (base + 1)
    if not isinstance(t, int):
        value = eng.to_reg(value)
    eng.wait_ge(*held)
    eng.wait_ge(sem, value)


def build(nc, A, out):
    with ExitStack() as ctx:
        def sb(name, shape, dt=F32):
            return ctx.enter_context(nc.sbuf_tensor(name, shape, dt))

        def sem(name):
            return ctx.enter_context(nc.semaphore(name))

        x = sb("x", [P, TILES, D])
        raw = sb("raw", [P, L0_COLS])
        w0h, w0l = sb("w0h", [P, L0_COLS], F32R), sb("w0l", [P, L0_COLS], F32R)
        wfh, wfl = sb("wfh", [P, FFN_COLS], F32R), sb("wfl", [P, FFN_COLS], F32R)
        w1h, w1l = sb("w1h", [P, L1_COLS], F32R), sb("w1l", [P, L1_COLS], F32R)
        ar = sb("arena_r", [P, ARENA_R], F32R)
        af = sb("arena_f", [P, ARENA_F])
        ctx_raw = sb("ctx_raw", [P, 2, D])
        ident = sb("ident", [P, P])
        ident16 = sb("ident16", [P, P], F16)
        blockmask = sb("blockmask", [P, 2 * VC])
        pairmask = sb("pairmask", [P, 2])
        iota8 = sb("iota8", [P, EXPERTS])
        rows = sb("rows", [P, 5, D])
        bo_rs = rows[:, 1, :]
        cols = sb("cols", [P, 2 * KC + NFF])
        bkm = sb("bkm", [P, KC, 2])
        rs = sb("rs", [P, 1])
        bg_raw = sb("bg_raw", [1, D])
        bgh, bgl = sb("bgh", [1, D], F32R), sb("bgl", [1, D], F32R)
        one_raw = sb("one_raw", [1, P])
        one_row = sb("one_row", [1, P], F32R)
        mask_i = sb("mask_i", [P, BATCHES], I32)
        lim = sb("lim", [P, BATCHES])
        st = sb("st", [P, 2, 6])
        mv = sb("mv", [P, 2, 2])
        ve = sb("ve", [P, 2])
        rstd = sb("rstd", [P, 2])
        st2 = sb("st2", [P, 2, 6])
        mv2 = sb("mv2", [P, 2, 2])
        ve2 = sb("ve2", [P, 2])
        rstd2 = sb("rstd2", [P, 2])
        mhalf = sb("mhalf", [P, 1])
        eps = sb("eps", [P, 1])
        tiny = sb("tiny", [P, 2, 80])
        tinyi = sb("tinyi", [P, 2, 8], U32)
        PS = ctx.enter_context(nc.psum_tensor("PS", [P, 8, 512], F32))

        def carve(arena, sizes):
            at, parts = 0, []
            for n in sizes:
                parts.append(arena[:, at:at + n])
                at += n
            assert at <= arena.shape[1], at
            return parts

        def ring(ap):
            return ap.rearrange("p (r n) -> p r n", r=2)

        xTh, xTl, cTh, cTl, aTh, aTl = map(ring, carve(ar, [512] * 6))
        fTh, fTl = carve(ar, [1024, 1280, 1280])[1:]
        mX, mD = map(ring, carve(ar, [1024, 4096]))
        (xn,) = map(ring, carve(af, [512]))
        _, ek, rk, eq, rq, kk, qq, thg, ag, vx, smat, az = carve(af, [512] * 9 + [2 * 2 * VC, 4 * 2 * VC, D])
        ek, rk, eq, rq, kk, qq, thg, ag, vx = map(ring, (ek, rk, eq, rq, kk, qq, thg, ag, vx))
        vx = [vx[:, r, :].rearrange("p (c n) -> p c n", c=2) for r in range(2)]
        smat = smat.rearrange("p (r b n) -> p r b n", r=2, b=2)
        _, fth, fa, fh = carve(af, [512, 1280, 1280, 1280])
        _, q1, kb, vb, pp, cn, dl, dn = map(ring, carve(af, [512, 512, 1024, 4 * PAIRS * PVC, 2048, 512, 512, 512]))
        kb = [kb[:, r, :].rearrange("p (c b h k) -> p c b h k", c=KC, b=2, h=2) for r in range(2)]
        vb = [vb[:, r, :].rearrange("p (b g n) -> p b g n", b=2, g=PAIRS) for r in range(2)]
        pp = [pp[:, r, :].rearrange("p (b j n) -> p b j n", b=2, j=PPC) for r in range(2)]
        mx16, md16, me16, mo = carve(af, [256, 2048, 256, 1024])
        mx16 = mx16.bitcast(F16).rearrange("p (r n) -> p r n", r=2)
        md16 = md16.bitcast(F16).rearrange("p (r n t) -> p r n t", r=2, n=NFF)
        me16 = me16.bitcast(F16).rearrange("p (k n) -> p k n", k=2)
        mo = mo.rearrange("p (r k n) -> p r k n", r=2, k=2)
        mX = [mX[:, r, :].rearrange("p (c t) -> p c t", c=KC) for r in range(2)]
        mD = [mD[:, r, :].rearrange("p (n t) -> p n t", n=NFF) for r in range(2)]

        def wmat(h, l, at, k, n):
            return [w[:, at:at + k * n].rearrange("p (k n) -> p k n", k=k) for w in (h, l)]

        kvw, qw, gw, ow = (wmat(w0h, w0l, at, KC, n) for at, n in ((L0_KV, 512), (L0_Q, D), (L0_G, D), (L0_O, D)))
        f1w = wmat(wfh, wfl, 0, KC, W1_COLS)
        f2w = wmat(wfh, wfl, KC * W1_COLS, EXPERTS + SH // P, D)
        q1w, k1w, v1w, o1w = (wmat(w1h, w1l, at, KC, D) for at in (L1_Q, L1_K, L1_V, L1_O))
        m0w = wmat(w1h, w1l, L1_W0, KC, FF)
        m1w = wmat(w1h, w1l, L1_W1, NFF, D)

        x_in = [sem("x_in_first"), sem("x_in_rest")]
        const_in, late_in = sem("const_in"), sem("late_in")
        w0_in = [sem(f"w0_in{i}") for i in range(3)]
        w0_hi, w0_lo = sem("w0_hi"), sem("w0_lo")
        ctx_in = [sem("ctx_in0"), sem("ctx_in1")]
        w_in = [sem("w_in0"), sem("w_in1")]
        setup_v, setup_p = sem("setup_vector"), sem("setup_pool")
        w_hi, w_lo = sem("weights_hi"), sem("weights_lo")
        ln_stats, ln_aggr, ln_var, ln_rstd = sem("ln_stats"), sem("ln_aggr"), sem("ln_var"), sem("ln_rstd")
        xn_ready, xT_psum, xT_hi, xT_lo = sem("xn_ready"), sem("xT_psum"), sem("xT_hi"), sem("xT_lo")
        ctx_hi, ctx_lo = sem("ctx_hi"), sem("ctx_lo")
        x_done = [sem(f"x_done{i}") for i in range(3)]

        block = ctx.enter_context(nc.Block())

        def product(out_ap, left, right, first=True, last=True):
            (lh, ll), (rh, rl) = left, right
            nc.tensor.matmul(out_ap, lh, rh, start=first, stop=False)
            nc.tensor.matmul(out_ap, lh, rl, start=False, stop=False)
            return nc.tensor.matmul(out_ap, ll, rh, start=False, stop=last)

        def ln_stats_step(dve, stage, t, r):
            base = TILES * stage
            after(dve, ln_var, t, 2, base)
            after(dve, xn_ready, t, 2, base)
            nc.vector.bn_stats(st[:, r, :], x[:, t, :]).then_inc(ln_stats, 1)
            after_plain(dve, (x_in[0], 16), ln_stats, t, base)
            nc.vector.bn_aggr(mv[:, r, :], st[:, r, :]).then_inc(ln_aggr, 1)

        def ln_rstd_step(pool, stage, t, r):
            base = TILES * stage
            after(pool, ln_aggr, t, 0, base)
            nc.gpsimd.tensor_tensor(ve[:, r:r + 1], mv[:, r, 1:2], eps[:, 0:1], ALU.add).then_inc(ln_var, 1)
            after(pool, ln_var, t, 0, base)
            after(pool, xn_ready, t, 2, base)
            nc.gpsimd.tensor_tensor(rstd[:, r:r + 1], ve[:, r:r + 1], mhalf[:, 0:1], ALU.pow).then_inc(ln_rstd, 1)

        def ln_norm_step(dve, stage, t, r, dst):
            base = TILES * stage
            after(dve, ln_rstd, t, 0, base)
            after(dve, ln_aggr, t, 0, base)
            after(dve, xT_psum, t, 2, base)
            nc.vector.tensor_scalar(dst[:, r, :], x[:, t, :], mv[:, r, 0:1], rstd[:, r:r + 1],
                                    ALU.subtract, ALU.mult).then_inc(xn_ready, 1)

        def transpose_x(pe, stage, t, r, bank):
            base = TILES * stage
            after(pe, xn_ready, t, 0, base)
            after(pe, xT_lo, t, 1, base)
            for c in range(KC):
                last = nc.tensor.transpose(PS[:, bank, c * P:(c + 1) * P], xn[:, r, c * P:(c + 1) * P], ident[:, :])
            last.then_inc(xT_psum, 1)

        def xT_hi_step(act, stage, t, r, bank, used):
            base = TILES * stage
            after(act, xT_psum, t, 0, base)
            after(act, used[0], t, 2, per=used[1])
            after(act, xT_lo, t, 2, base)
            nc.scalar.activation(xTh[:, r, :], PS[:, bank, 0:D], ACT.Copy).then_inc(xT_hi, 1)

        def xT_lo_step(dve, stage, t, r, bank, used):
            base = TILES * stage
            after(dve, xT_hi, t, 0, base)
            after(dve, used[0], t, 2, per=used[1])
            nc.vector.tensor_tensor(xTl[:, r, :], PS[:, bank, 0:D], xTh[:, r, :].bitcast(F32),
                                    ALU.subtract).then_inc(xT_lo, 1)

        def xT(r, c):
            return [w[:, r, c * P:(c + 1) * P] for w in (xTh, xTl)]

        def cT(r, c):
            return [w[:, r, c * P:(c + 1) * P] for w in (cTh, cTl)]

        def aT(r, c):
            return [w[:, r, c * P:(c + 1) * P] for w in (aTh, aTl)]

        def in_ring(eng, sems, t, r, before=0):
            eng.wait_ge(sems[r], t * 8 + (16 - 8 * r + 16 * before))

        def ctx_hi_step(act, turn, t, r, used):
            base = TILES * turn
            in_ring(act, ctx_in, t, r, 8 * turn)
            after(act, used, t, 2)
            after(act, ctx_lo, t, 2, base)
            nc.scalar.activation(cTh[:, r, :], ctx_raw[:, r, :], ACT.Copy).then_inc(ctx_hi, 1)

        def ctx_lo_step(pool, turn, t, r, used):
            after(pool, ctx_hi, t, 0, TILES * turn)
            after(pool, used, t, 2)
            nc.gpsimd.tensor_tensor(cTl[:, r, :], ctx_raw[:, r, :], cTh[:, r, :].bitcast(F32),
                                    ALU.subtract).then_inc(ctx_lo, 1)

        def weights_hi_step(act, turn, t, r):
            wh, n = ((wfh, FFN_CHUNK), (w1h, L1_CHUNK))[turn]
            in_ring(act, w_in, t, r, 8 * turn)
            nc.scalar.activation(wh[:, bass.ts(t, n)], raw[:, r * FFN_CHUNK:r * FFN_CHUNK + n],
                                 ACT.Copy).then_inc(w_hi, 1)

        def weights_lo_step(dve, turn, t, r):
            wh, wl, n = ((wfh, wfl, FFN_CHUNK), (w1h, w1l, L1_CHUNK))[turn]
            after(dve, w_hi, t, 0, TILES * turn)
            nc.vector.tensor_tensor(wl[:, bass.ts(t, n)], raw[:, r * FFN_CHUNK:r * FFN_CHUNK + n],
                                    wh[:, bass.ts(t, n)].bitcast(F32), ALU.subtract).then_inc(w_lo, 1)

        S0 = {n: sem("s0_" + n) for n in (
            "kv_psum", "gq_psum", "k_exp", "k_relu", "v_ready", "q_exp", "q_relu", "gate_tanh", "k_ready", "q_ready",
            "ktv_psum", "s_ready", "attn_psum", "den", "z", "az", "ag_ready", "agT_psum", "agT_hi", "agT_lo",
            "o_psum")}
        S1 = {n: sem("s1_" + n) for n in (
            "router_psum", "scores", "top", "index", "gap", "gap_exp", "denom", "weights", "w2", "indexf", "pick1",
            "pick2", "comb", "g_psum", "tanh", "a", "h", "hT_psum", "hT_hi", "hT_lo", "down")}
        S2 = {n: sem("s2_" + n) for n in (
            "qk_psum", "v_psum", "q_ready", "kb_ready", "vb_ready", "scores_psum", "clipped", "probs", "pv_psum",
            "r1", "s1", "s2", "s3", "r2", "cn_ready", "cnT_psum", "cnT_hi", "cnT_lo", "o_psum", "delta", "d_stats",
            "d_aggr", "d_var", "d_rstd", "dn", "scaled", "shifted")}
        S3 = {n: sem("s3_" + n) for n in (
            "x_ready", "h_psum", "gelu", "d_ready", "o_psum", "e16", "o_ready")}
        stored = [sem("stored0"), sem("stored1")]

        @block.sync
        def _(sp):
            def load(dst, src, s):
                sp.dma_start(dst, src).then_inc(s, 16)

            x_d = A["x"].rearrange("(t p) d -> p t d", p=P)
            load(x[:, 0:2, :], x_d[:, 0:2, :], x_in[0])
            load(ctx_raw[:, 0, :], A["ctxT"][0], ctx_in[0])
            load(ident[:, :], A["ident"], const_in)
            load(raw[:, 0:L0_Q], A["w_l0"][:, 0:L0_Q], w0_in[0])
            load(raw[:, L0_Q:L0_O], A["w_l0"][:, L0_Q:L0_O], w0_in[1])
            load(ctx_raw[:, 1, :], A["ctxT"][1], ctx_in[1])
            load(raw[:, L0_O:], A["w_l0"][:, L0_O:], w0_in[2])
            load(bg_raw[:, :], A["bg"], const_in)
            load(blockmask[:, :], A["blockmask"], const_in)
            load(x[:, 2:TILES, :], x_d[:, 2:TILES, :], x_in[1])
            for dst, name in ((pairmask, "pairmask"), (iota8, "iota8"), (cols, "cols"), (rs, "rs"), (mask_i, "mask")):
                load(dst[:, :], A[name], late_in)
            load(rows[:, :, :], A["rows"], late_in)

            def load_ctx(turn, t, r):
                after(sp, ctx_lo, t, 2, TILES * turn)
                load(ctx_raw[:, r, :], A["ctxT"][t], ctx_in[r])

            def load_w(turn, t, r):
                src, n = ((A["w_ffn"], FFN_CHUNK), (A["w_l1"], L1_CHUNK))[turn]
                after(sp, w_lo, t, 2, TILES * turn)
                load(raw[:, r * FFN_CHUNK:r * FFN_CHUNK + n], src[t], w_in[r])

            sp.wait_ge(w0_lo, 3)
            for t in range(2):
                load_w(0, t, t)
            with sp.Fori(1, TILES // 2) as i:
                for r in range(2):
                    load_ctx(0, i * 2 + r, r)
                    load_w(0, i * 2 + r, r)
            for t in range(2):
                load_ctx(1, t, t)
            for t in range(2):
                load_w(1, t, t)
            with sp.Fori(1, TILES // 2) as i:
                for r in range(2):
                    load_w(1, i * 2 + r, r)
            with sp.Fori(1, TILES // 2) as i:
                for r in range(2):
                    load_ctx(1, i * 2 + r, r)

            out_d = out.rearrange("(g k p) d -> g p k d", p=P, k=2)
            with sp.Fori(0, GROUPS // 2) as i:
                for r in range(2):
                    sp.wait_ge(S3["o_ready"], i * 2 + (r + 1))
                    load(out_d[i * 2 + r], mo[:, r, :, :], stored[r])
            for r in range(2):
                sp.wait_ge(stored[r], 16 * GROUPS // 2)

        @block.gpsimd
        def _(pool):
            nc.gpsimd.memset(mhalf[:, :], -0.5).then_inc(setup_p, 1)
            nc.gpsimd.memset(eps[:, :], 1e-5).then_inc(setup_p, 1)
            nc.gpsimd.memset(one_raw[:, :], 1.0).then_inc(setup_p, 1)
            for r in range(2):
                nc.gpsimd.memset(vx[r][:, :, P:VC], 1.0).then_inc(setup_p, 1)

            def slot0(s):
                if tile := s.tile(1):
                    ctx_lo_step(pool, 0, *tile, S0["kv_psum"])
                    ln_rstd_step(pool, 0, *tile)

            slots(pool, TILES, -1, TILES - 2, slot0)

            pool.wait_ge(x_done[0], TILES)

            def slot1(s):
                if tile := s.tile(1):
                    ln_rstd_step(pool, 1, *tile)

            slots(pool, TILES, -1, TILES - 2, slot1, low=2)

            pool.wait_ge(x_done[1], TILES)
            for r in range(2):
                nc.gpsimd.memset(vb[r][:, :, :, :], 0.0).then_inc(setup_p, 1)
            pool.wait_ge(setup_p, 7)
            for r in range(2):
                for h in range(2):
                    nc.gpsimd.memset(vb[r][SEQ * h:SEQ * (h + 1), :, :, 2 * HD + h:2 * HD + h + 1],
                                     1.0).then_inc(setup_p, 1)
            pool.wait_ge(setup_p, 11)

            def slot2(s):
                if tile := s.tile(1):
                    ctx_lo_step(pool, 1, *tile, S2["v_psum"])
                    ln_rstd_step(pool, 2, *tile)
                if tile := s.tile(-2):
                    t, r = tile
                    after(pool, S2["d_aggr"], t)
                    nc.gpsimd.tensor_tensor(ve2[:, r:r + 1], mv2[:, r, 1:2], eps[:, 0:1], ALU.add).then_inc(S2["d_var"], 1)
                    after(pool, S2["d_var"], t)
                    after(pool, S2["dn"], t, 2)
                    nc.gpsimd.tensor_tensor(rstd2[:, r:r + 1], ve2[:, r:r + 1], mhalf[:, 0:1],
                                            ALU.pow).then_inc(S2["d_rstd"], 1)
                    after(pool, S2["dn"], t)
                    nc.gpsimd.tensor_tensor(dn[:, r, :], dn[:, r, :], rows[:, 2, :], ALU.mult).then_inc(S2["scaled"], 1)
                    after(pool, S2["scaled"], t)
                    nc.gpsimd.tensor_tensor(dn[:, r, :], dn[:, r, :], rows[:, 3, :], ALU.add).then_inc(S2["shifted"], 1)
                    after(pool, S2["shifted"], t)
                    nc.gpsimd.tensor_tensor(x[:, t, :], x[:, t, :], dn[:, r, :], ALU.add).then_inc(x_done[2], 1)

            slots(pool, TILES, -1, TILES + 1, slot2)

            def slot3(s):
                if tile := s.tile(1):
                    for k in range(2):
                        ln_rstd_step(pool, 3, tile[0] * 2 + k, k)

            slots(pool, GROUPS, -1, GROUPS - 2, slot3, low=2)

        @block.scalar
        def _(act):
            for i, (a, b) in enumerate(((L0_KV, L0_Q), (L0_Q, L0_O), (L0_O, L0_COLS))):
                act.wait_ge(w0_in[i], 16)
                nc.scalar.activation(w0h[:, a:b], raw[:, a:b], ACT.Copy).then_inc(w0_hi, 1)

            def slot0(s):
                if tile := s.tile(0):
                    t, r = tile
                    after(act, S0["kv_psum"], t)
                    after(act, S0["k_ready"], t, 2)
                    nc.scalar.activation(ek[:, r, :], PS[:, B_KV, 0:D], ACT.Exp).then_inc(S0["k_exp"], 1)
                    nc.scalar.activation(rk[:, r, :], PS[:, B_KV, 0:D], ACT.Relu).then_inc(S0["k_relu"], 1)
                    after(act, S0["ktv_psum"], t, 2)
                    act.wait_ge(setup_p, 5)
                    nc.scalar.activation(vx[r][:, :, 0:P], PS[:, B_KV, D:2 * D].rearrange("p (c n) -> p c n", c=2),
                                         ACT.Copy).then_inc(S0["v_ready"], 1)
                    after(act, S0["gq_psum"], t)
                    after(act, S0["q_ready"], t, 2)
                    nc.scalar.activation(eq[:, r, :], PS[:, B_QG, 0:D], ACT.Exp).then_inc(S0["q_exp"], 1)
                    nc.scalar.activation(rq[:, r, :], PS[:, B_QG, 0:D], ACT.Relu).then_inc(S0["q_relu"], 1)
                    after(act, S0["ag_ready"], t, 2)
                    nc.scalar.activation(thg[:, r, :], PS[:, B_QG, D:2 * D], ACT.Tanh,
                                         scale=0.5).then_inc(S0["gate_tanh"], 1)
                if tile := s.tile(1):
                    ctx_hi_step(act, 0, *tile, S0["kv_psum"])
                    xT_hi_step(act, 0, *tile, B_T, (S0["gq_psum"], 1))
                if tile := s.tile(0):
                    weights_hi_step(act, 0, *tile)
                if tile := s.tile(-1):
                    t, r = tile
                    after(act, S0["agT_psum"], t)
                    after(act, S0["o_psum"], t, 2)
                    after(act, S0["agT_lo"], t, 2)
                    nc.scalar.activation(aTh[:, r, :], PS[:, B_TA, 0:D], ACT.Copy).then_inc(S0["agT_hi"], 1)

            slots(act, TILES, -1, TILES, slot0)

            act.wait_ge(x_done[0], TILES)
            down = S1["down"]

            def slot1(s):
                if tile := s.tile(-1):
                    t, r = tile
                    after(act, S1["hT_psum"], t, per=3)
                    after(act, down, t, 1, per=3)
                    nc.scalar.activation(fTh[:, 1024:1280], PS[:, F_H, 0:256], ACT.Copy).then_inc(S1["hT_hi"], 1)
                if tile := s.tile(0):
                    t, r = tile
                    after(act, S1["gap"], t)
                    after(act, S1["w2"], t, 2)
                    nc.scalar.activation(tiny[:, r, 34:36], tiny[:, r, 32:34], ACT.Exp).then_inc(S1["gap_exp"], 1)
                    for g, bank in enumerate((F_G0, F_G1)):
                        after(act, S1["g_psum"], t, per=3, extra=g - 2)
                        after(act, S1["a"], t, 1, per=3, extra=g - 2)
                        nc.scalar.activation(fth[:, 512 * g:512 * (g + 1)], PS[:, bank, :], ACT.Tanh,
                                             scale=0.5).then_inc(S1["tanh"], 1)
                        if g == 0:
                            weights_hi_step(act, 1, t, r)
                        else:
                            after(act, S1["hT_psum"], t, per=3, extra=-2)
                            after(act, down, t, 1, per=3, extra=-2)
                            nc.scalar.activation(fTh[:, 0:512], PS[:, F_H, :], ACT.Copy).then_inc(S1["hT_hi"], 1)
                    after(act, S1["g_psum"], t, per=3)
                    after(act, S1["a"], t, 1, per=3)
                    nc.scalar.activation(fth[:, 1024:1280], PS[:, F_G0, 0:256], ACT.Tanh,
                                         scale=0.5).then_inc(S1["tanh"], 1)
                    after(act, S1["hT_psum"], t, per=3, extra=-1)
                    after(act, down, t, 1, per=3, extra=-1)
                    nc.scalar.activation(fTh[:, 512:1024], PS[:, F_H + 1, :], ACT.Copy).then_inc(S1["hT_hi"], 1)
                if tile := s.tile(1):
                    xT_hi_step(act, 1, *tile, F_T, (S1["g_psum"], 3))

            slots(act, TILES, -1, TILES, slot1, low=2)

            act.wait_ge(x_done[1], TILES)
            act.wait_ge(setup_v, 6)

            def slot2(s):
                if tile := s.tile(-1):
                    t, r = tile
                    after(act, S2["clipped"], t, per=2)
                    flat = pp[r].rearrange("p b j n -> p (b j n)")
                    nc.scalar.activation(flat, flat, ACT.Exp).then_inc(S2["probs"], 1)
                if tile := s.tile(0):
                    t, r = tile
                    after(act, S2["qk_psum"], t)
                    after(act, S2["scores_psum"], t, 2)
                    for c in range(KC):
                        nc.scalar.activation(q1[:, r, c * P:(c + 1) * P], PS[:, X_QK, c * P:(c + 1) * P], ACT.Identity,
                                             bias=cols[:, c:c + 1]).then_inc(S2["q_ready"], 1)
                        for h in range(2):
                            nc.scalar.activation(
                                kb[r][:, c, :, h, :],
                                PS[:, X_QK, D + c * P:D + (c + 1) * P].rearrange("p (b k) -> p b k", b=2),
                                ACT.Identity, bias=bkm[:, c, h:h + 1], scale=pairmask[:, h:h + 1],
                            ).then_inc(S2["kb_ready"], 1)
                if tile := s.tile(1):
                    ctx_hi_step(act, 1, *tile, S2["v_psum"])
                    xT_hi_step(act, 2, *tile, X_T, (S2["qk_psum"], 1))
                if tile := s.tile(-1):
                    t, r = tile
                    after(act, S2["cnT_psum"], t)
                    after(act, S2["o_psum"], t, 2)
                    after(act, S2["cnT_lo"], t, 2)
                    nc.scalar.activation(aTh[:, r, :], PS[:, X_T, D:2 * D], ACT.Copy).then_inc(S2["cnT_hi"], 1)

            slots(act, TILES, -1, TILES, slot2)

            act.wait_ge(x_done[2], TILES)

            def slot3(s):
                if tile := s.tile(0):
                    g, r = tile
                    for n in range(NFF):
                        if n % 2 == 0:
                            after(act, S3["h_psum"], g, per=4, extra=n // 2 - 3)
                            after(act, S3["d_ready"], g, 2, per=4, extra=n // 2 - 3)
                        nc.scalar.activation(md16[:, r, n, :], PS[:, M_H + n // 2, (n % 2) * D:(n % 2 + 1) * D],
                                             ACT.Gelu, bias=cols[:, 2 * KC + n:2 * KC + n + 1]).then_inc(S3["gelu"], 1)
                if tile := s.tile(1):
                    g, r = tile
                    after(act, xT_psum, g, per=2, base=3 * TILES)
                    after(act, S3["h_psum"], g, 2, per=4)
                    for k in range(2):
                        src = PS[:, M_T, k * P:(k + 1) * P].bitcast(F16).rearrange("p (c t) -> p c t", c=KC)
                        nc.scalar.activation(mX[r][:, :, k * P:(k + 1) * P], src, ACT.Copy).then_inc(S3["x_ready"], 1)

            slots(act, GROUPS, -1, GROUPS - 1, slot3, low=2)

        @block.vector
        def _(dve):
            def split_w0(i, a, b):
                dve.wait_ge(w0_hi, i + 1)
                nc.vector.tensor_tensor(w0l[:, a:b], raw[:, a:b], w0h[:, a:b].bitcast(F32),
                                        ALU.subtract).then_inc(w0_lo, 1)

            def setup():
                dve.wait_ge(const_in, 16 * 3)
                dve.wait_ge(setup_p, 3)
                nc.vector.tensor_copy(bgh[:, :], bg_raw[:, :]).then_inc(setup_v, 1)
                nc.vector.tensor_copy(one_row[:, :], one_raw[:, :])
                dve.wait_ge(setup_v, 1)
                nc.vector.tensor_tensor(bgl[:, :], bg_raw[:, :], bgh[:, :].bitcast(F32),
                                        ALU.subtract).then_inc(setup_v, 1)

            def setup_late():
                dve.wait_ge(late_in, 16 * 6)
                nc.vector.tensor_copy(ident16[:, :], ident[:, :]).then_inc(setup_v, 1)
                for c in range(KC):
                    nc.vector.tensor_scalar(bkm[:, c, :], pairmask[:, :], cols[:, KC + c:KC + c + 1], None, ALU.mult)
                nc.vector.tensor_scalar(rs[:, :], rs[:, :], 0.0, 0.3, ALU.max, ALU.min).then_inc(setup_v, 1)
                nc.vector.tensor_scalar(lim[:, :], mask_i[:, :], 0.5, 100.0, ALU.is_gt, ALU.mult).then_inc(setup_v, 1)
                dve.wait_ge(setup_v, 5)
                nc.vector.tensor_scalar(rows[:, 1, :], rows[:, 1, :], rs[:, 0:1], None, ALU.mult)
                nc.vector.tensor_scalar(lim[:, :], lim[:, :], -50.0, None, ALU.add).then_inc(setup_v, 1)

            split_w0(0, L0_KV, L0_Q)
            setup()

            def slot0(s):
                if tile := s.tile(1):
                    t, r = tile
                    if isinstance(t, int) and t in (0, 2):
                        dve.wait_ge(x_in[t // 2], 16)
                    ln_stats_step(dve, 0, t, r)
                if isinstance(s.at, int) and s.at == -1:
                    split_w0(1, L0_Q, L0_O)
                if tile := s.tile(0):
                    t, r = tile
                    after(dve, S0["k_exp"], t)
                    after(dve, S0["k_relu"], t)
                    after(dve, S0["ktv_psum"], t, 2)
                    nc.vector.scalar_tensor_tensor(out=kk[:, r, :], in0=ek[:, r, :], scalar=1.0, in1=rk[:, r, :],
                                                   op0=ALU.min, op1=ALU.add).then_inc(S0["k_ready"], 1)
                if tile := s.tile(1):
                    ln_norm_step(dve, 0, *tile, xn)
                if isinstance(s.at, int) and s.at == -1:
                    split_w0(2, L0_O, L0_COLS)
                if tile := s.tile(-2):
                    t, r = tile
                    after(dve, S0["o_psum"], t)
                    nc.vector.tensor_tensor(x[:, t, :], PS[:, B_O, 0:D], x[:, t, :], ALU.add).then_inc(x_done[0], 1)
                if tile := s.tile(0):
                    t, r = tile
                    after(dve, S0["q_exp"], t)
                    after(dve, S0["q_relu"], t)
                    after(dve, S0["attn_psum"], t, 2)
                    nc.vector.scalar_tensor_tensor(out=qq[:, r, :], in0=eq[:, r, :], scalar=1.0, in1=rq[:, r, :],
                                                   op0=ALU.min, op1=ALU.add).then_inc(S0["q_ready"], 1)
                if tile := s.tile(-1):
                    t, r = tile
                    at = PS[:, B_A, 0:2 * VC].rearrange("p (c n) -> p c n", c=2)
                    den, hz = (tiny[:, r, a:a + HEADS].rearrange("p (c h) -> p c h", c=2) for a in (0, HEADS))
                    after(dve, S0["attn_psum"], t)
                    nc.vector.tensor_scalar(den, at[:, :, P:VC], 1e-6, 2.0, ALU.add, ALU.mult).then_inc(S0["den"], 1)
                    after(dve, S0["den"], t)
                    nc.vector.reciprocal(hz, den).then_inc(S0["z"], 1)
                    after(dve, S0["z"], t)
                    nc.vector.tensor_tensor(
                        az.rearrange("p (c h e) -> p c h e", c=2, h=HPC),
                        at[:, :, 0:P].rearrange("p c (h e) -> p c h e", h=HPC),
                        hz.unsqueeze(3).to_broadcast([P, 2, HPC, HD]), ALU.mult).then_inc(S0["az"], 1)
                    after(dve, S0["az"], t)
                    after(dve, S0["gate_tanh"], t)
                    after(dve, S0["agT_psum"], t, 2)
                    nc.vector.scalar_tensor_tensor(out=ag[:, r, :], in0=thg[:, r, :], scalar=1.0, in1=az,
                                                   op0=ALU.add, op1=ALU.mult).then_inc(S0["ag_ready"], 1)
                if tile := s.tile(1):
                    xT_lo_step(dve, 0, *tile, B_T, (S0["gq_psum"], 1))
                if tile := s.tile(0):
                    t, r = tile
                    after(dve, S0["ktv_psum"], t)
                    after(dve, S0["attn_psum"], t, 2)
                    for b in range(2):
                        last = nc.vector.tensor_tensor(smat[:, r, b, :], PS[:, B_S + b, 0:2 * VC], blockmask[:, :],
                                                       ALU.mult)
                    last.then_inc(S0["s_ready"], 1)
                    weights_lo_step(dve, 0, t, r)
                if tile := s.tile(-1):
                    t, r = tile
                    after(dve, S0["agT_hi"], t)
                    after(dve, S0["o_psum"], t, 2)
                    nc.vector.tensor_tensor(aTl[:, r, :], PS[:, B_TA, 0:D], aTh[:, r, :].bitcast(F32),
                                            ALU.subtract).then_inc(S0["agT_lo"], 1)

            slots(dve, TILES, -1, TILES + 1, slot0)
            dve.wait_ge(x_done[0], TILES)
            setup_late()

            def residual_1(t):
                after(dve, S1["down"], t, per=3)
                nc.vector.tensor_tensor(x[:, t, :], PS[:, F_O, 0:D], x[:, t, :], ALU.add).then_inc(x_done[1], 1)

            def slot1(s):
                if tile := s.tile(1):
                    ln_stats_step(dve, 1, *tile)
                if tile := s.tile(-1):
                    t, r = tile
                    after(dve, S1["hT_hi"], t, per=3)
                    nc.vector.tensor_tensor(fTl[:, 1024:1280], PS[:, F_H, 0:256], fTh[:, 1024:1280].bitcast(F32),
                                            ALU.subtract).then_inc(S1["hT_lo"], 1)
                if tile := s.tile(0):
                    t, r = tile
                    sc, mx8, gap, e2, w3, c1, c2, comb, dn2, ixf = (
                        tiny[:, r, a:a + n] for a, n in (
                            (0, 10), (16, 8), (32, 2), (34, 2), (36, 3), (40, 8), (48, 8), (56, 8), (64, 2), (66, 2)))
                    ix = tinyi[:, r, :]
                    after(dve, S1["router_psum"], t)
                    nc.vector.tensor_copy(sc, PS[:, F_T, D:D + 10]).then_inc(S1["scores"], 1)
                    after_plain(dve, (late_in, 16 * 6), S1["scores"], t)
                    nc.vector.max(mx8, sc[:, 0:8]).then_inc(S1["top"], 1)
                    nc.vector.tensor_scalar(gap[:, 1:2], sc[:, 8:9], -1.0, None, ALU.mult)
                    after(dve, S1["top"], t)
                    nc.vector.tensor_tensor(gap[:, 0:1], mx8[:, 1:2], mx8[:, 0:1], ALU.subtract).then_inc(S1["gap"], 1)
                    nc.vector.max_index(ix, mx8, sc[:, 0:8]).then_inc(S1["index"], 1)
                    after(dve, S1["index"], t)
                    nc.vector.tensor_copy(ixf, ix[:, 0:2]).then_inc(S1["indexf"], 1)
                    after(dve, S1["gap_exp"], t)
                    nc.vector.tensor_scalar(dn2, e2, 2.0, 2.0, ALU.mult, ALU.add).then_inc(S1["denom"], 1)
                    after(dve, S1["denom"], t)
                    nc.vector.reciprocal(w3[:, 0:2], dn2).then_inc(S1["weights"], 1)
                    after(dve, S1["weights"], t)
                    nc.vector.tensor_tensor(w3[:, 2:3], w3[:, 0:1], e2[:, 0:1], ALU.mult).then_inc(S1["w2"], 1)
                    after(dve, S1["indexf"], t)
                    nc.vector.tensor_scalar(c1, iota8[:, :], ixf[:, 0:1], w3[:, 0:1], ALU.is_equal,
                                            ALU.mult).then_inc(S1["pick1"], 1)
                    after(dve, S1["w2"], t)
                    nc.vector.tensor_scalar(c2, iota8[:, :], ixf[:, 1:2], w3[:, 2:3], ALU.is_equal,
                                            ALU.mult).then_inc(S1["pick2"], 1)
                    after(dve, S1["pick1"], t)
                    after(dve, S1["pick2"], t)
                    nc.vector.tensor_tensor(comb, c1, c2, ALU.add).then_inc(S1["comb"], 1)
                    ln = s.tile(1)
                    for g, (gb, ub) in enumerate(((F_G0, F_U0), (F_G1, F_U1))):
                        at = slice(512 * g, 512 * (g + 1))
                        after(dve, S1["tanh"], t, per=3, extra=g - 2)
                        nc.vector.scalar_tensor_tensor(out=fa[:, at], in0=fth[:, at], scalar=1.0, in1=PS[:, gb, :],
                                                       op0=ALU.add, op1=ALU.mult).then_inc(S1["a"], 1)
                        before = s.tile(-1)
                        if g == 1 and before:
                            residual_1(before[0])
                        after(dve, S1["a"], t, per=3, extra=g - 2)
                        if g == 0:
                            after(dve, S1["comb"], t)
                        after(dve, S1["hT_psum"], t, 1, per=3, extra=g - 2)
                        for e in range(4):
                            c = slice(512 * g + 128 * e, 512 * g + 128 * (e + 1))
                            last = nc.vector.scalar_tensor_tensor(
                                out=fh[:, c], in0=fa[:, c], scalar=comb[:, 4 * g + e:4 * g + e + 1],
                                in1=PS[:, ub, 128 * e:128 * (e + 1)], op0=ALU.mult, op1=ALU.mult)
                        last.then_inc(S1["h"], 1)
                        if g == 0:
                            if ln:
                                ln_norm_step(dve, 1, *ln, xn)
                            weights_lo_step(dve, 1, t, r)
                        if g == 1:
                            after(dve, S1["hT_hi"], t, per=3, extra=-2)
                            nc.vector.tensor_tensor(fTl[:, 0:512], PS[:, F_H, :], fTh[:, 0:512].bitcast(F32),
                                                    ALU.subtract).then_inc(S1["hT_lo"], 1)
                    at = slice(1024, 1280)
                    after(dve, S1["tanh"], t, per=3)
                    nc.vector.scalar_tensor_tensor(out=fa[:, at], in0=fth[:, at], scalar=1.0, in1=PS[:, F_G0, 0:256],
                                                   op0=ALU.add, op1=ALU.mult).then_inc(S1["a"], 1)
                    after(dve, S1["a"], t, per=3)
                    after(dve, S1["hT_psum"], t, 1, per=3)
                    nc.vector.scalar_tensor_tensor(out=fh[:, at], in0=fa[:, at], scalar=w3[:, 1:2],
                                                   in1=PS[:, F_G0, 256:512], op0=ALU.mult,
                                                   op1=ALU.mult).then_inc(S1["h"], 1)
                    after(dve, S1["hT_hi"], t, per=3, extra=-1)
                    nc.vector.tensor_tensor(fTl[:, 512:1024], PS[:, F_H + 1, :], fTh[:, 512:1024].bitcast(F32),
                                            ALU.subtract).then_inc(S1["hT_lo"], 1)
                else:
                    if tile := s.tile(1):
                        ln_norm_step(dve, 1, *tile, xn)
                    if tile := s.tile(-1):
                        residual_1(tile[0])
                if tile := s.tile(1):
                    xT_lo_step(dve, 1, *tile, F_T, (S1["g_psum"], 3))

            slots(dve, TILES, -1, TILES, slot1, low=2)
            dve.wait_ge(x_done[1], TILES)

            def slot2(s):
                if tile := s.tile(1):
                    ln_stats_step(dve, 2, *tile)
                if tile := s.tile(0):
                    t, r = tile
                    after(dve, S2["v_psum"], t)
                    after(dve, S2["pv_psum"], t, 2)
                    dve.wait_ge(setup_p, 11)

                    def heads(ap, b, h):
                        return ap[SEQ * b:SEQ * (b + 1)].rearrange("p (g h e) -> p g h e", g=PAIRS, h=2)[:, :, h, :]

                    for b in range(2):
                        for h in range(2):
                            last = nc.vector.tensor_tensor(
                                vb[r][SEQ * h:SEQ * (h + 1), b, :, HD * h:HD * (h + 1)],
                                heads(PS[:, X_VO, 0:D], b, h), heads(rows[:, 0, :], b, h), ALU.add)
                    last.then_inc(S2["vb_ready"], 1)
                if tile := s.tile(1):
                    ln_norm_step(dve, 2, *tile, xn)
                if tile := s.tile(-2):
                    t, r = tile
                    after(dve, S2["o_psum"], t)
                    after(dve, S2["dn"], t, 2)
                    nc.vector.scalar_tensor_tensor(out=dl[:, r, :], in0=PS[:, X_VO, D:2 * D], scalar=rs[:, 0:1],
                                                   in1=bo_rs, op0=ALU.mult, op1=ALU.add).then_inc(S2["delta"], 1)
                    after(dve, S2["delta"], t)
                    after(dve, S2["d_var"], t, 2)
                    nc.vector.bn_stats(st2[:, r, :], dl[:, r, :]).then_inc(S2["d_stats"], 1)
                    after_plain(dve, (x_in[0], 16), S2["d_stats"], t)
                    nc.vector.bn_aggr(mv2[:, r, :], st2[:, r, :]).then_inc(S2["d_aggr"], 1)
                if tile := s.tile(-1):
                    t, r = tile
                    cx = PS[:, X_C, 0:PAIRS * PVC].rearrange("p (g n) -> p g n", g=PAIRS)
                    sums = cx[:, :, 2 * HD:PVC]
                    r1, s1, s2, s3, r2 = (tiny[:, r, a:a + HEADS].rearrange("p (g h) -> p g h", h=2)
                                      for a in (0, 16, 32, 48, 64))
                    after(dve, S2["pv_psum"], t)
                    nc.vector.reciprocal(r1, sums).then_inc(S2["r1"], 1)
                    after(dve, S2["r1"], t)
                    nc.vector.tensor_tensor(s1, sums, r1, ALU.mult).then_inc(S2["s1"], 1)
                    after(dve, S2["s1"], t)
                    nc.vector.tensor_scalar(s2, s1, 1e-8, None, ALU.add).then_inc(S2["s2"], 1)
                    after(dve, S2["s2"], t)
                    nc.vector.reciprocal(s3, s2).then_inc(S2["s3"], 1)
                    after(dve, S2["s3"], t)
                    nc.vector.tensor_tensor(r2, s3, r1, ALU.mult).then_inc(S2["r2"], 1)
                    after(dve, S2["r2"], t)
                    after(dve, S2["cnT_psum"], t, 2)
                    nc.vector.tensor_tensor(
                        cn[:, r, :].rearrange("p (g h e) -> p g h e", g=PAIRS, h=2),
                        cx[:, :, 0:2 * HD].rearrange("p g (h e) -> p g h e", h=2),
                        r2.unsqueeze(3).to_broadcast([P, PAIRS, 2, HD]), ALU.mult).then_inc(S2["cn_ready"], 1)
                if tile := s.tile(1):
                    xT_lo_step(dve, 2, *tile, X_T, (S2["qk_psum"], 1))
                if tile := s.tile(-2):
                    t, r = tile
                    after(dve, S2["d_rstd"], t)
                    after(dve, x_done[2], t, 2)
                    nc.vector.tensor_scalar(dn[:, r, :], dl[:, r, :], mv2[:, r, 0:1], rstd2[:, r:r + 1],
                                            ALU.subtract, ALU.mult).then_inc(S2["dn"], 1)
                if tile := s.tile(0):
                    t, r = tile
                    after(dve, S2["scores_psum"], t)
                    after(dve, S2["pv_psum"], t, 2)
                    for b in range(2):
                        nc.vector.tensor_scalar(pp[r][:, b, :, :], PS[:, X_S:X_S + 4, b * P:(b + 1) * P], -50.0,
                                                lim[:, bass.ds(t * 2 + b, 1)], ALU.max,
                                                ALU.min).then_inc(S2["clipped"], 1)
                if tile := s.tile(-1):
                    t, r = tile
                    after(dve, S2["cnT_hi"], t)
                    after(dve, S2["o_psum"], t, 2)
                    nc.vector.tensor_tensor(aTl[:, r, :], PS[:, X_T, D:2 * D], aTh[:, r, :].bitcast(F32),
                                            ALU.subtract).then_inc(S2["cnT_lo"], 1)

            slots(dve, TILES, -1, TILES + 1, slot2)
            dve.wait_ge(x_done[2], TILES)

            def slot3(s):
                if tile := s.tile(1):
                    for k in range(2):
                        ln_stats_step(dve, 3, tile[0] * 2 + k, k)
                    for k in range(2):
                        ln_norm_step(dve, 3, tile[0] * 2 + k, k, mx16)
                if tile := s.tile(0):
                    g, r = tile
                    for i in range(4):
                        after(dve, S3["gelu"], g, per=8, extra=2 * i - 6)
                        after(dve, S3["o_psum"], g, 2)
                        nc.vector.tensor_copy(mD[r][:, 2 * i:2 * i + 2, :],
                                              md16[:, r, 2 * i:2 * i + 2, :]).then_inc(S3["d_ready"], 1)
                if tile := s.tile(-1):
                    g, r = tile
                    after(dve, S3["o_psum"], g)
                    after(dve, S3["o_ready"], g, 1)
                    nc.vector.tensor_tensor(me16, PS[:, M_O, :].rearrange("p (k n) -> p k n", k=2),
                                            rows[:, 4, :].unsqueeze(1).to_broadcast([P, 2, D]),
                                            ALU.add).then_inc(S3["e16"], 1)
                    after(dve, S3["e16"], g)
                    if not (isinstance(g, int) and g < 2):
                        dve.wait_ge(stored[r], g * 8 + (-8 * r))
                    nc.vector.tensor_tensor(mo[:, r, :, :], x[:, bass.ds(g * 2, 2), :], me16,
                                            ALU.add).then_inc(S3["o_ready"], 1)

            slots(dve, GROUPS, -1, GROUPS, slot3)

        @block.tensor
        def _(pe):
            pe.wait_ge(const_in, 16 * 3)

            def slot0(s):
                if tile := s.tile(0):
                    t, r = tile
                    after(pe, ctx_lo, t)
                    after(pe, ctx_hi, t)
                    if isinstance(t, int) and t == 0:
                        pe.wait_ge(w0_lo, 1)
                    after(pe, S0["v_ready"], t, 1)
                    for c in range(KC):
                        last = product(PS[:, B_KV, :], cT(r, c), [w[:, c, :] for w in kvw], c == 0, c == KC - 1)
                    last.then_inc(S0["kv_psum"], 1)
                if tile := s.tile(-2):
                    t, r = tile
                    after(pe, S0["agT_lo"], t)
                    after(pe, x_done[0], t, 1)
                    for c in range(KC):
                        last = product(PS[:, B_O, 0:D], aT(r, c), [w[:, c, :] for w in ow], c == 0, c == KC - 1)
                    last.then_inc(S0["o_psum"], 1)
                if tile := s.tile(0):
                    t, r = tile
                    after(pe, xT_lo, t)
                    if isinstance(t, int) and t == 0:
                        pe.wait_ge(w0_lo, 3)
                        pe.wait_ge(setup_v, 2)
                    after(pe, S0["gate_tanh"], t, 1)
                    for m in range(KC):
                        for c in range(KC):
                            product(PS[:, B_QG, m * P:(m + 1) * P], [w[:, c, m * P:(m + 1) * P] for w in qw], xT(r, c),
                                    c == 0, c == KC - 1)
                    for c in range(KC):
                        product(PS[:, B_QG, D:2 * D], xT(r, c), [w[:, c, :] for w in gw], c == 0, False)
                    nc.tensor.matmul(PS[:, B_QG, D:2 * D], one_row[:, :], bgh[:, :], start=False, stop=False)
                    nc.tensor.matmul(PS[:, B_QG, D:2 * D], one_row[:, :], bgl[:, :], start=False,
                                     stop=True).then_inc(S0["gq_psum"], 1)
                if tile := s.tile(-1):
                    t, r = tile
                    after(pe, S0["q_ready"], t)
                    after(pe, S0["s_ready"], t)
                    after(pe, S0["az"], t, 1)
                    for b in range(2):
                        for c in range(KC):
                            last = nc.tensor.matmul(PS[SEQ * b:SEQ * (b + 1), B_A, c * VC:(c + 1) * VC],
                                                    qq[:, r, c * P + SEQ * b:c * P + SEQ * (b + 1)],
                                                    smat[:, r, b, c * VC:(c + 1) * VC], start=True, stop=True)
                    last.then_inc(S0["attn_psum"], 1)
                if tile := s.tile(1):
                    transpose_x(pe, 0, *tile, B_T)
                if tile := s.tile(0):
                    t, r = tile
                    after(pe, S0["k_ready"], t)
                    after(pe, S0["v_ready"], t)
                    after(pe, S0["s_ready"], t, 1)
                    for b in range(2):
                        for c in range(KC):
                            last = nc.tensor.matmul(PS[:, B_S + b, c * VC:(c + 1) * VC],
                                                    kk[SEQ * b:SEQ * (b + 1), r, c * P:(c + 1) * P],
                                                    vx[r][SEQ * b:SEQ * (b + 1), c, :], start=True, stop=True)
                    last.then_inc(S0["ktv_psum"], 1)
                if tile := s.tile(-1):
                    t, r = tile
                    after(pe, S0["ag_ready"], t)
                    after(pe, S0["agT_lo"], t, 1)
                    for c in range(KC):
                        last = nc.tensor.transpose(PS[:, B_TA, c * P:(c + 1) * P], ag[:, r, c * P:(c + 1) * P],
                                                   ident[:, :])
                    last.then_inc(S0["agT_psum"], 1)

            slots(pe, TILES, -1, TILES + 1, slot0)

            pe.wait_ge(x_done[0], TILES)
            pe.wait_ge(w_lo, TILES)
            R0 = 2 * EXPERTS * EH + 2 * SH

            def expert_in(t, r, bank, at):
                for c in range(KC):
                    last = product(PS[:, bank, :], xT(r, c), [w[:, c, at:at + 512] for w in f1w], c == 0, c == KC - 1)
                return last

            def hidden_T(first, n, bank):
                for i in range(n):
                    last = nc.tensor.transpose(PS[:, bank, i * P:(i + 1) * P],
                                               fh[:, (first + i) * P:(first + i + 1) * P], ident[:, :])
                last.then_inc(S1["hT_psum"], 1)

            def expert_out(first, n, start, stop):
                for i in range(first, first + n):
                    last = product(PS[:, F_O, 0:D], [w[:, i * P:(i + 1) * P] for w in (fTh, fTl)],
                                   [w[:, i, :] for w in f2w], start and i == first, stop and i == first + n - 1)
                last.then_inc(S1["down"], 1)
                return last

            def slot1(s):
                if tile := s.tile(0):
                    t, r = tile
                    after(pe, xT_lo, t, base=TILES)
                    for c in range(KC):
                        last = product(PS[:, F_T, D:D + 10], xT(r, c), [w[:, c, R0:R0 + 10] for w in f1w], c == 0,
                                       c == KC - 1)
                    last.then_inc(S1["router_psum"], 1)
                    after(pe, S1["h"], t, 1, per=3)
                    expert_in(t, r, F_G0, 0)
                    expert_in(t, r, F_U0, 512).then_inc(S1["g_psum"], 1)
                if tile := s.tile(-1):
                    t, r = tile
                    after(pe, S1["h"], t, per=3)
                    after(pe, S1["hT_lo"], t, per=3, extra=-2)
                    hidden_T(8, 2, F_H)
                    after(pe, S1["hT_lo"], t, per=3, extra=-1)
                    expert_out(4, 4, False, False)
                if tile := s.tile(0):
                    t, r = tile
                    after(pe, S1["h"], t, 1, per=3, extra=-1)
                    expert_in(t, r, F_G1, 1024)
                    expert_in(t, r, F_U1, 1536).then_inc(S1["g_psum"], 1)
                if tile := s.tile(-1):
                    after(pe, S1["hT_lo"], tile[0], per=3)
                    expert_out(8, 2, False, True)
                if tile := s.tile(0):
                    t, r = tile
                    after(pe, S1["h"], t, per=3, extra=-2)
                    after(pe, S1["hT_lo"], t, 1, per=3)
                    hidden_T(0, 4, F_H)
                    expert_in(t, r, F_G0, 2048).then_inc(S1["g_psum"], 1)
                    after(pe, S1["hT_lo"], t, per=3, extra=-2)
                    after(pe, x_done[1], t, 1)
                    expert_out(0, 4, True, False)
                    after(pe, S1["h"], t, per=3, extra=-1)
                    hidden_T(4, 4, F_H + 1)
                if tile := s.tile(1):
                    if before := s.tile(0):
                        after(pe, S1["scores"], before[0])
                    transpose_x(pe, 1, *tile, F_T)

            slots(pe, TILES, -1, TILES, slot1, low=2)

            pe.wait_ge(x_done[1], TILES)
            pe.wait_ge(w_lo, 2 * TILES)

            def slot2(s):
                if tile := s.tile(0):
                    t, r = tile
                    after(pe, xT_lo, t, base=2 * TILES)
                    after(pe, ctx_lo, t, base=TILES)
                    after(pe, S2["kb_ready"], t, 1, per=4)
                    after(pe, S2["q_ready"], t, 1, per=2)
                    for m in range(KC):
                        for c in range(KC):
                            product(PS[:, X_QK, m * P:(m + 1) * P], [w[:, c, m * P:(m + 1) * P] for w in q1w],
                                    xT(r, c), c == 0, c == KC - 1)
                    for m in range(KC):
                        for c in range(KC):
                            last = product(PS[:, X_QK, D + m * P:D + (m + 1) * P],
                                           [w[:, c, m * P:(m + 1) * P] for w in k1w], cT(r, c), c == 0, c == KC - 1)
                    last.then_inc(S2["qk_psum"], 1)
                    after(pe, S2["vb_ready"], t, 1)
                    after(pe, S2["delta"], t, 3)
                    for c in range(KC):
                        last = product(PS[:, X_VO, 0:D], cT(r, c), [w[:, c, :] for w in v1w], c == 0, c == KC - 1)
                    last.then_inc(S2["v_psum"], 1)
                if tile := s.tile(-1):
                    t, r = tile
                    after(pe, S2["probs"], t)
                    after(pe, S2["vb_ready"], t)
                    after(pe, S2["cn_ready"], t, 1)
                    for b in range(2):
                        for g in range(PAIRS):
                            c, j = divmod(g, PPC)
                            last = nc.tensor.matmul(PS[SEQ * b:SEQ * (b + 1), X_C, g * PVC:(g + 1) * PVC],
                                                    pp[r][:, b, j, c * SEQ:(c + 1) * SEQ], vb[r][:, b, g, :],
                                                    start=True, stop=True)
                    last.then_inc(S2["pv_psum"], 1)
                if tile := s.tile(1):
                    if before := s.tile(-2):
                        after(pe, S2["cnT_lo"], before[0])
                    transpose_x(pe, 2, *tile, X_T)
                if tile := s.tile(-2):
                    t, r = tile
                    after(pe, S2["cnT_lo"], t)
                    if here := s.tile(0):
                        after(pe, S2["vb_ready"], here[0])
                    for c in range(KC):
                        last = product(PS[:, X_VO, D:2 * D], aT(r, c), [w[:, c, :] for w in o1w], c == 0, c == KC - 1)
                    last.then_inc(S2["o_psum"], 1)
                if tile := s.tile(0):
                    t, r = tile
                    after(pe, S2["kb_ready"], t, per=4)
                    after(pe, S2["q_ready"], t, per=2)
                    after(pe, S2["clipped"], t, 1, per=2)
                    for b in range(2):
                        for c in range(KC):
                            for j in range(PPC):
                                f = slice(2 * HD * j, 2 * HD * (j + 1))
                                last = nc.tensor.matmul(
                                    PS[:, X_S + j, (b * KC + c) * SEQ:(b * KC + c + 1) * SEQ],
                                    kb[r][f, c, b, :, :].rearrange("p h k -> p (h k)"),
                                    q1[f, r, c * P + SEQ * b:c * P + SEQ * (b + 1)], start=True, stop=True)
                    last.then_inc(S2["scores_psum"], 1)
                if tile := s.tile(-1):
                    t, r = tile
                    after(pe, S2["cn_ready"], t)
                    if ahead := s.tile(1):
                        after(pe, xT_lo, ahead[0], base=2 * TILES)
                    for c in range(KC):
                        last = nc.tensor.transpose(PS[:, X_T, D + c * P:D + (c + 1) * P], cn[:, r, c * P:(c + 1) * P],
                                                   ident[:, :])
                    last.then_inc(S2["cnT_psum"], 1)

            slots(pe, TILES, -1, TILES + 1, slot2)

            pe.wait_ge(x_done[2], TILES)
            pe.wait_ge(setup_v, 6)

            def slot3(s):
                if tile := s.tile(0):
                    g, r = tile
                    after(pe, S3["x_ready"], g, per=2)
                    for n in range(NFF):
                        if n % 2 == 0:
                            after(pe, S3["gelu"], g, 1, per=8, extra=n - 6)
                        for c in range(KC):
                            for w in range(2):
                                last = nc.tensor.matmul(PS[:, M_H + n // 2, (n % 2) * D:(n % 2 + 1) * D],
                                                        m0w[w][:, c, n * P:(n + 1) * P], mX[r][:, c, :],
                                                        start=c + w == 0, stop=c + w == 2)
                        if n % 2:
                            last.then_inc(S3["h_psum"], 1)
                if tile := s.tile(-1):
                    g, r = tile
                    after(pe, S3["d_ready"], g, per=4)
                    after(pe, S3["e16"], g, 1)
                    for k in range(2):
                        for n in range(NFF):
                            for w in range(2):
                                last = nc.tensor.matmul(PS[:, M_O, k * D:(k + 1) * D],
                                                        mD[r][:, n, k * P:(k + 1) * P], m1w[w][:, n, :],
                                                        start=n + w == 0, stop=n + w == NFF)
                    last.then_inc(S3["o_psum"], 1)
                if tile := s.tile(1):
                    g, r = tile
                    after(pe, S3["x_ready"], g, 1, per=2)
                    for k in range(2):
                        after(pe, xn_ready, g, per=2, base=3 * TILES, extra=k - 1)
                        for c in range(KC):
                            last = nc.tensor.transpose(
                                PS[:, M_T, k * P + c * SEQ:k * P + (c + 1) * SEQ].bitcast(F16),
                                mx16[:, k, c * P:(c + 1) * P], ident16[:, :])
                        last.then_inc(xT_psum, 1)

            slots(pe, GROUPS, -1, GROUPS, slot3, low=2)


def by_contraction(w):
    n, k = w.shape
    return np.ascontiguousarray(w.T.reshape(k // P, P, n).transpose(1, 0, 2)).reshape(P, -1)


def laid_out(i):
    i = {k: np.asarray(v) for k, v in i.items()}
    f = np.float32
    lane = np.arange(P)
    a = {"x": i["x"].reshape(TOKENS, D)}
    a["ctxT"] = i["ctx_2048"].reshape(TILES, P, KC, P).transpose(0, 3, 2, 1).reshape(TILES, P, D)
    a["w_l0"] = np.concatenate([by_contraction(i["L0_xattn_" + n]) for n in ("Wkv", "Wq", "Wg", "Wo")], 1)
    gates, ups = (i["L0_ffn_" + n].reshape(2, 4 * EH, D) for n in ("w_gate", "w_up"))
    w1 = np.concatenate([gates[0], ups[0], gates[1], ups[1], i["L0_ffn_sh_gate"], i["L0_ffn_sh_up"],
                         i["L0_ffn_gate_w"], i["L0_ffn_se_gate_w"], np.zeros((1, D), f)])
    ffn = np.concatenate([by_contraction(w1), i["L0_ffn_w_down"].transpose(2, 0, 1).reshape(P, -1),
                          by_contraction(i["L0_ffn_sh_down"]), np.zeros((P, FFN_COLS - FFN_USED), f)], 1)
    a["w_ffn"] = ffn.reshape(P, TILES, FFN_CHUNK).transpose(1, 0, 2)
    l1 = np.concatenate([by_contraction(i[n]) for n in ("L1_xattn_Wq", "L1_xattn_Wk", "L1_xattn_Wv", "L1_xattn_Wo",
                                                        "L1_ffn_W0", "L1_ffn_W1")], 1)
    a["w_l1"] = l1.reshape(P, TILES, L1_CHUNK).transpose(1, 0, 2)
    a["rows"] = np.broadcast_to(np.stack([i[n] for n in ("L1_xattn_bv", "L1_xattn_bo", "L1_xattn_ln_gamma",
                                                         "L1_xattn_ln_beta", "L1_ffn_bias1")]), (P, 5, D))
    a["cols"] = np.concatenate([i[n].reshape(-1, P).T for n in ("L1_xattn_bq", "L1_xattn_bk", "L1_ffn_bias0")], 1)
    a["bg"] = i["L0_xattn_bg"].reshape(1, D)
    a["rs"] = np.broadcast_to(i["L1_xattn_residual_scale"].reshape(1, 1), (P, 1))
    mask = i["mask_BxS2_ik0"].T
    a["mask"] = np.concatenate([mask, mask], 0)
    a["ident"] = np.eye(P, dtype=f)
    own = (lane[:, None] // HD == np.arange(VC)[None, :] // HD)
    own[:, P:] = lane[:, None] // HD == np.arange(HPC)[None, :]
    a["blockmask"] = np.concatenate([own, own], 1).astype(f)
    a["pairmask"] = (0.25 * (lane[:, None] % (2 * HD) // HD == np.arange(2)[None, :])).astype(f)
    a["iota8"] = np.tile(np.arange(EXPERTS, dtype=f), (P, 1))
    return {k: np.ascontiguousarray(v) for k, v in a.items()}


def kernel(**inputs):
    import concourse.bacc as _bacc
    from concourse.bass_utils import run_bass_kernel_spmd as _run

    nc = _bacc.Bacc("TRN2", target_bir_lowering=False, num_devices=1, dynamic_dma_scratch_size=2048)
    arrays = laid_out(inputs)
    args = {n: nc.dram_tensor("in_" + n, a.shape, mybir.dt.from_np(a.dtype), kind="ExternalInput").ap()
            for n, a in arrays.items()}
    out = nc.dram_tensor("out", (TOKENS, D), F32, kind="ExternalOutput").ap()
    build(nc, args, out)
    r = _run(nc, [{"in_" + n: a for n, a in arrays.items()}], core_ids=[0])
    return r.results[0]["out"].reshape(BATCHES, SEQ, D)
```

```python
from contextlib import ExitStack

import numpy as np

import concourse.bass as bass
from concourse import mybir

F32 = mybir.dt.float32
F32R = mybir.dt.float32r
F16 = mybir.dt.float16
I32 = mybir.dt.int32
U32 = mybir.dt.uint32
ALU = mybir.AluOpType
ACT = mybir.ActivationFunctionType

P = 128
BATCHES, SEQ, D = 32, 64, 256
TOKENS = BATCHES * SEQ
TILES = TOKENS // P
PER_TILE = P // SEQ
KC = D // P
HEADS, HD = 16, 16
HPC = P // HD
PAIRS = HEADS // 2
PPC = P // (2 * HD)
EXPERTS, EH = 8, 128
SH = 256
FF = 1024
NFF = FF // P
GROUPS = TILES // 2
VC = P + HPC
PVC = 2 * HD + 2

L0_KV, L0_Q, L0_G, L0_O = 0, 2 * 512, 2 * 512 + 2 * D, 2 * 512 + 4 * D
L0_COLS = L0_O + 2 * D
W1_COLS = 2 * EXPERTS * EH + 2 * SH + EXPERTS + 2
FFN_USED = KC * W1_COLS + (EXPERTS + SH // P) * D
FFN_CHUNK = -(-FFN_USED // TILES // 2) * 2
FFN_COLS = FFN_CHUNK * TILES
L1_Q, L1_K, L1_V, L1_O = 0, 2 * D, 4 * D, 6 * D
L1_W0 = 8 * D
L1_W1 = L1_W0 + KC * FF
L1_COLS = L1_W1 + NFF * D
L1_CHUNK = L1_COLS // TILES

GROUP_A, GROUP_B, GROUP_C = slice(0, 512), slice(512, 1024), slice(1024, 1280)

ARENA_R = 5120
ARENA_F = 6784

B_T, B_Q, B_GO, B_KV, B_A, B_S, B_TA = 0, 1, 2, 3, 4, 5, 7
F_T, F_G0, F_U0, F_G1, F_U1, F_O, F_H = 0, 1, 2, 3, 4, 5, 6
X_T, X_Q, X_K, X_V, X_O, X_C, X_S = 0, 1, 2, 3, 4, 5, 6
M_T, M_H, M_O = 0, 1, 5


class Slot:

    def __init__(self, at, ring, count, pair=None):
        self.at, self.ring, self.count = at, ring, count
        self.pair = at // 2 if isinstance(at, int) else pair

    def tile(self, ahead):
        t = self.at + ahead
        if isinstance(t, int) and not 0 <= t < self.count:
            return None
        return t, (self.ring + ahead) % 2


def slots(eng, count, first, last, body, low=4):
    high = (count - 1) // 2 * 2
    for s in range(first, low):
        body(Slot(s, s % 2, count))
    with eng.Fori(low // 2, high // 2) as i:
        body(Slot(i * 2, 0, count, i))
        body(Slot(i * 2 + 1, 1, count, i))
    for s in range(high, last + 1):
        body(Slot(s, s % 2, count))


def after(eng, sem, t, back=0, base=0, per=1, extra=0):
    if isinstance(t, int) and t - back < 0:
        if base:
            eng.wait_ge(sem, base)
        return
    eng.wait_ge(sem, t * per + (base + per * (1 - back) + extra))


def after_plain(eng, held, sem, t, base=0):
    value = t + (base + 1)
    if not isinstance(t, int):
        value = eng.to_reg(value)
    eng.wait_ge(*held)
    eng.wait_ge(sem, value)


def build(nc, A, out):
    with ExitStack() as ctx:
        def sb(name, shape, dt=F32):
            return ctx.enter_context(nc.sbuf_tensor(name, shape, dt))

        def sem(name):
            return ctx.enter_context(nc.semaphore(name))

        x = sb("x", [P, TILES, D])
        raw = sb("raw", [P, L0_COLS])
        w0h, w0l = sb("w0h", [P, L0_COLS], F32R), sb("w0l", [P, L0_COLS], F32R)
        wfh, wfl = sb("wfh", [P, FFN_COLS], F32R), sb("wfl", [P, FFN_COLS], F32R)
        w1h, w1l = sb("w1h", [P, L1_COLS], F32R), sb("w1l", [P, L1_COLS], F32R)
        ar = sb("arena_r", [P, ARENA_R], F32R)
        af = sb("arena_f", [P, ARENA_F])
        ctx_raw = sb("ctx_raw", [P, 2, D])
        ident = sb("ident", [P, P])
        ident16 = sb("ident16", [P, P], F16)
        blockmask = sb("blockmask", [P, 2 * VC])
        headmask = sb("headmask", [P, 4])
        iota8 = sb("iota8", [P, EXPERTS])
        rows = sb("rows", [P, 5, D])
        bo_rs = rows[:, 1, :]
        cols = sb("cols", [P, 2 * KC + NFF])
        bkm, bqm = sb("bkm", [P, KC, 2]), sb("bqm", [P, KC, 2])
        rs = sb("rs", [P, 1])
        bg_raw = sb("bg_raw", [1, D])
        bgh, bgl = sb("bgh", [1, D], F32R), sb("bgl", [1, D], F32R)
        one_raw = sb("one_raw", [1, P])
        one_row = sb("one_row", [1, P], F32R)
        mask_i = sb("mask_i", [P, BATCHES], I32)
        lim = sb("lim", [P, BATCHES])
        st = sb("st", [P, 2, 6])
        mv = sb("mv", [P, 2, 2])
        ve = sb("ve", [P, 2])
        rstd = sb("rstd", [P, 2])
        st2 = sb("st2", [P, 2, 6])
        mv2 = sb("mv2", [P, 2, 2])
        ve2 = sb("ve2", [P, 2])
        rstd2 = sb("rstd2", [P, 2])
        mhalf = sb("mhalf", [P, 1])
        eps = sb("eps", [P, 1])
        tiny = sb("tiny", [P, 2, 80])
        tinyi = sb("tinyi", [P, 2, 8], U32)
        PS = ctx.enter_context(nc.psum_tensor("PS", [P, 8, 512], F32))

        def carve(arena, sizes):
            at, parts = 0, []
            for n in sizes:
                parts.append(arena[:, at:at + n])
                at += n
            assert at <= arena.shape[1], at
            return parts

        def ring(ap):
            return ap.rearrange("p (r n) -> p r n", r=2)

        xTh, xTl, cTh, cTl, aTh, aTl = map(ring, carve(ar, [512] * 6))
        fTh, fTl = carve(ar, [1024, 1280, 1280])[1:]
        mX, mD = map(ring, carve(ar, [1024, 4096]))
        (xn,) = map(ring, carve(af, [512]))
        _, ek, rk, eq, rq, kk, qq, thg, ag, vx, smat, az = carve(af, [512] * 9 + [2 * 2 * VC, 4 * 2 * VC, D])
        ek, rk, kk, thg, ag, vx = map(ring, (ek, rk, kk, thg, ag, vx))
        vx = [vx[:, r, :].rearrange("p (c n) -> p c n", c=2) for r in range(2)]
        smat = smat.rearrange("p (r b n) -> p r b n", r=2, b=2)
        _, fth, fa, fh = carve(af, [512, 1280, 1280, 1280])
        _, kb, vb, pp, cn, dl, dn = map(ring, carve(af, [512, 1024, 4 * PAIRS * PVC, 2048, 512, 512, 512]))
        assert 2 * FFN_CHUNK <= 1024 <= L0_COLS - 1024
        qb = raw[:, 1024:2048]
        qb = qb.rearrange("p (r c b j q) -> p r c b j q", r=2, c=KC, b=2, j=2)
        kb = kb.rearrange("p r (c b h k) -> p r c b h k", c=KC, b=2, h=2)
        vb = [vb[:, r, :].rearrange("p (b g n) -> p b g n", b=2, g=PAIRS) for r in range(2)]
        pp = [pp[:, r, :].rearrange("p (b i n) -> p b i n", b=2, i=2) for r in range(2)]
        mx16, md16, me16, mo = carve(af, [256, 2048, 256, 1024])
        mx16 = mx16.bitcast(F16).rearrange("p (r n) -> p r n", r=2)
        md16 = md16.bitcast(F16).rearrange("p (r n t) -> p r n t", r=2, n=NFF)
        me16 = me16.bitcast(F16).rearrange("p (k n) -> p k n", k=2)
        mo = mo.rearrange("p (r k n) -> p r k n", r=2, k=2)
        mX = [mX[:, r, :].rearrange("p (c t) -> p c t", c=KC) for r in range(2)]
        mD = [mD[:, r, :].rearrange("p (n t) -> p n t", n=NFF) for r in range(2)]

        def wmat(h, l, at, k, n):
            return [w[:, at:at + k * n].rearrange("p (k n) -> p k n", k=k) for w in (h, l)]

        kvw, qw, gw, ow = (wmat(w0h, w0l, at, KC, n) for at, n in ((L0_KV, 512), (L0_Q, D), (L0_G, D), (L0_O, D)))
        f1w = wmat(wfh, wfl, 0, KC, W1_COLS)
        f2w = wmat(wfh, wfl, KC * W1_COLS, EXPERTS + SH // P, D)
        q1w, k1w, v1w, o1w = (wmat(w1h, w1l, at, KC, D) for at in (L1_Q, L1_K, L1_V, L1_O))
        m0w = wmat(w1h, w1l, L1_W0, KC, FF)
        m1w = wmat(w1h, w1l, L1_W1, NFF, D)

        x_in = [sem("x_in_first"), sem("x_in_rest")]
        const_in, late_in = sem("const_in"), sem("late_in")
        w0_in = [sem(f"w0_in{i}") for i in range(3)]
        w0_hi, w0_lo = sem("w0_hi"), sem("w0_lo")
        ctx_in = [sem("ctx_in0"), sem("ctx_in1")]
        w_in = [sem("w_in0"), sem("w_in1")]
        setup_v, setup_p = sem("setup_vector"), sem("setup_pool")
        w_hi, w_lo = sem("weights_hi"), sem("weights_lo")
        ln_stats, ln_aggr, ln_var, ln_rstd = sem("ln_stats"), sem("ln_aggr"), sem("ln_var"), sem("ln_rstd")
        xn_ready, xT_psum, xT_hi, xT_lo = sem("xn_ready"), sem("xT_psum"), sem("xT_hi"), sem("xT_lo")
        ctx_hi, ctx_lo = sem("ctx_hi"), sem("ctx_lo")
        x_done = [sem(f"x_done{i}") for i in range(3)]

        block = ctx.enter_context(nc.Block())

        def product(out_ap, left, right, first=True, last=True):
            (lh, ll), (rh, rl) = left, right
            nc.tensor.matmul(out_ap, lh, rh, start=first, stop=False)
            nc.tensor.matmul(out_ap, lh, rl, start=False, stop=False)
            return nc.tensor.matmul(out_ap, ll, rh, start=False, stop=last)

        def ln_stats_step(dve, stage, t, r):
            base = TILES * stage
            after(dve, ln_var, t, 2, base)
            after(dve, xn_ready, t, 2, base)
            nc.vector.bn_stats(st[:, r, :], x[:, t, :]).then_inc(ln_stats, 1)
            after_plain(dve, (x_in[0], 16), ln_stats, t, base)
            nc.vector.bn_aggr(mv[:, r, :], st[:, r, :]).then_inc(ln_aggr, 1)

        def ln_rstd_step(pool, stage, t, r):
            base = TILES * stage
            after(pool, ln_aggr, t, 0, base)
            nc.gpsimd.tensor_tensor(ve[:, r:r + 1], mv[:, r, 1:2], eps[:, 0:1], ALU.add).then_inc(ln_var, 1)
            after(pool, ln_var, t, 0, base)
            after(pool, xn_ready, t, 2, base)
            nc.gpsimd.tensor_tensor(rstd[:, r:r + 1], ve[:, r:r + 1], mhalf[:, 0:1], ALU.pow).then_inc(ln_rstd, 1)

        def ln_norm_step(dve, stage, t, r, dst):
            base = TILES * stage
            after(dve, ln_rstd, t, 0, base)
            after(dve, ln_aggr, t, 0, base)
            after(dve, xT_psum, t, 2, base)
            nc.vector.tensor_scalar(dst[:, r, :], x[:, t, :], mv[:, r, 0:1], rstd[:, r:r + 1],
                                    ALU.subtract, ALU.mult).then_inc(xn_ready, 1)

        def transpose_x(pe, stage, t, r, bank):
            base = TILES * stage
            after(pe, xn_ready, t, 0, base)
            after(pe, xT_lo, t, 1, base)
            for c in range(KC):
                last = nc.tensor.transpose(PS[:, bank, c * P:(c + 1) * P], xn[:, r, c * P:(c + 1) * P], ident[:, :])
            last.then_inc(xT_psum, 1)

        def xT_hi_step(act, stage, t, r, bank):
            base = TILES * stage
            after(act, xT_psum, t, 0, base)
            after(act, xT_lo, t, 2, base)
            nc.scalar.activation(xTh[:, :, r * P:(r + 1) * P], PS[:, bank, 0:D].rearrange("p (c t) -> p c t", c=KC),
                                 ACT.Copy).then_inc(xT_hi, 1)

        def xT_lo_step(dve, stage, t, r, bank):
            after(dve, xT_hi, t, 0, TILES * stage)
            at = slice(r * P, (r + 1) * P)
            nc.vector.tensor_tensor(xTl[:, :, at], PS[:, bank, 0:D].rearrange("p (c t) -> p c t", c=KC),
                                    xTh[:, :, at].bitcast(F32), ALU.subtract).then_inc(xT_lo, 1)

        def xT(r, c):
            return [w[:, c, r * P:(r + 1) * P] for w in (xTh, xTl)]

        def cT(r, c):
            return [w[:, c, r * P:(r + 1) * P] for w in (cTh, cTl)]

        def pair(parts, c):
            return [w[:, c, :] for w in parts]

        def aT(r, c):
            return [w[:, r, c * P:(c + 1) * P] for w in (aTh, aTl)]

        def in_ring(eng, sems, t, r, before=0):
            eng.wait_ge(sems[r], t * 8 + (16 - 8 * r + 16 * before))

        def ctx_hi_step(act, turn, t, r, used):
            base = TILES * turn
            in_ring(act, ctx_in, t, r, 8 * turn)
            after(act, used, t, 2)
            after(act, ctx_lo, t, 2, base)
            nc.scalar.activation(cTh[:, :, r * P:(r + 1) * P], ctx_raw[:, r, :].rearrange("p (c t) -> p c t", c=KC),
                                 ACT.Copy).then_inc(ctx_hi, 1)

        def ctx_lo_step(pool, turn, t, r, used):
            after(pool, ctx_hi, t, 0, TILES * turn)
            after(pool, used, t, 2)
            at = slice(r * P, (r + 1) * P)
            nc.gpsimd.tensor_tensor(cTl[:, :, at], ctx_raw[:, r, :].rearrange("p (c t) -> p c t", c=KC),
                                    cTh[:, :, at].bitcast(F32), ALU.subtract).then_inc(ctx_lo, 1)

        def weights_hi_step(act, turn, t, r):
            wh, n = ((wfh, FFN_CHUNK), (w1h, L1_CHUNK))[turn]
            in_ring(act, w_in, t, r, 8 * turn)
            nc.scalar.activation(wh[:, bass.ts(t, n)], raw[:, r * FFN_CHUNK:r * FFN_CHUNK + n],
                                 ACT.Copy).then_inc(w_hi, 1)

        def weights_lo_step(dve, turn, t, r):
            wh, wl, n = ((wfh, wfl, FFN_CHUNK), (w1h, w1l, L1_CHUNK))[turn]
            after(dve, w_hi, t, 0, TILES * turn)
            nc.vector.tensor_tensor(wl[:, bass.ts(t, n)], raw[:, r * FFN_CHUNK:r * FFN_CHUNK + n],
                                    wh[:, bass.ts(t, n)].bitcast(F32), ALU.subtract).then_inc(w_lo, 1)

        S0 = {n: sem("s0_" + n) for n in (
            "kv_psum", "q_psum", "g_psum", "k_exp", "k_relu", "v_ready", "q_exp", "q_relu", "gate_tanh", "k_ready", "q_ready",
            "ktv_psum", "s_ready", "attn_psum", "den", "z", "az", "ag_ready", "agT_psum", "agT_hi", "agT_lo",
            "o_psum")}
        S1 = {n: sem("s1_" + n) for n in (
            "router_psum", "scores", "top", "index", "gap", "gap_exp", "denom", "weights", "w2", "indexf", "pick1",
            "pick2", "comb", "g_psum", "tanh", "a", "h", "hT_psum", "hT_hi", "hT_lo", "down")}
        S2 = {n: sem("s2_" + n) for n in (
            "q_psum", "k_psum", "v_psum", "q_ready", "kb_ready", "vb_ready", "scores_psum", "clipped", "probs", "pv_psum",
            "guard", "den", "rden", "cn_ready", "cnT_psum", "cnT_hi", "cnT_lo", "o_psum", "delta", "d_stats",
            "d_aggr", "d_var", "d_rstd", "dn", "scaled", "shifted")}
        S3 = {n: sem("s3_" + n) for n in (
            "x_ready", "h_psum", "gelu", "d_ready", "o_psum", "e16", "o_ready")}
        stored = [sem("stored0"), sem("stored1")]

        @block.sync
        def _(sp):
            def load(dst, src, s):
                sp.dma_start(dst, src).then_inc(s, 16)

            x_d = A["x"].rearrange("(t p) d -> p t d", p=P)
            load(x[:, 0:2, :], x_d[:, 0:2, :], x_in[0])
            load(ctx_raw[:, 0, :], A["ctxT"][0], ctx_in[0])
            load(ident[:, :], A["ident"], const_in)
            load(raw[:, 0:L0_Q], A["w_l0"][:, 0:L0_Q], w0_in[0])
            load(raw[:, L0_Q:L0_O], A["w_l0"][:, L0_Q:L0_O], w0_in[1])
            load(ctx_raw[:, 1, :], A["ctxT"][1], ctx_in[1])
            load(raw[:, L0_O:], A["w_l0"][:, L0_O:], w0_in[2])
            load(bg_raw[:, :], A["bg"], const_in)
            load(blockmask[:, :], A["blockmask"], const_in)
            load(x[:, 2:TILES, :], x_d[:, 2:TILES, :], x_in[1])
            for dst, name in ((headmask, "headmask"), (iota8, "iota8"), (cols, "cols"), (rs, "rs"), (mask_i, "mask")):
                load(dst[:, :], A[name], late_in)
            load(rows[:, :, :], A["rows"], late_in)

            def load_ctx(turn, t, r):
                after(sp, ctx_lo, t, 2, TILES * turn)
                load(ctx_raw[:, r, :], A["ctxT"][t], ctx_in[r])

            def load_w(turn, t, r):
                src, n = ((A["w_ffn"], FFN_CHUNK), (A["w_l1"], L1_CHUNK))[turn]
                after(sp, w_lo, t, 2, TILES * turn)
                load(raw[:, r * FFN_CHUNK:r * FFN_CHUNK + n], src[t], w_in[r])

            sp.wait_ge(w0_lo, 3)
            for t in range(2):
                load_w(0, t, t)
            with sp.Fori(1, TILES // 2) as i:
                for r in range(2):
                    load_ctx(0, i * 2 + r, r)
                    load_w(0, i * 2 + r, r)
            for t in range(2):
                load_ctx(1, t, t)
            for t in range(2):
                load_w(1, t, t)
            with sp.Fori(1, TILES // 2) as i:
                for r in range(2):
                    load_w(1, i * 2 + r, r)
            with sp.Fori(1, TILES // 2) as i:
                for r in range(2):
                    load_ctx(1, i * 2 + r, r)

            out_d = out.rearrange("(g k p) d -> g p k d", p=P, k=2)
            with sp.Fori(0, GROUPS // 2) as i:
                for r in range(2):
                    sp.wait_ge(S3["o_ready"], i * 2 + (r + 1))
                    load(out_d[i * 2 + r], mo[:, r, :, :], stored[r])
            for r in range(2):
                sp.wait_ge(stored[r], 16 * GROUPS // 2)

        @block.gpsimd
        def _(pool):
            nc.gpsimd.memset(mhalf[:, :], -0.5).then_inc(setup_p, 1)
            nc.gpsimd.memset(eps[:, :], 1e-5).then_inc(setup_p, 1)
            nc.gpsimd.memset(one_raw[:, :], 1.0).then_inc(setup_p, 1)
            for r in range(2):
                nc.gpsimd.memset(vx[r][:, :, P:VC], 1.0).then_inc(setup_p, 1)

            def slot0(s):
                if tile := s.tile(2):
                    ln_rstd_step(pool, 0, *tile)
                    ctx_lo_step(pool, 0, *tile, S0["kv_psum"])

            slots(pool, TILES, -2, TILES - 1, slot0)

            pool.wait_ge(x_done[0], TILES)

            def slot1(s):
                if tile := s.tile(2):
                    ln_rstd_step(pool, 1, *tile)

            slots(pool, TILES, -2, TILES - 3, slot1, low=2)

            pool.wait_ge(x_done[1], TILES)
            for r in range(2):
                nc.gpsimd.memset(vb[r][:, :, :, :], 0.0).then_inc(setup_p, 1)
            pool.wait_ge(setup_p, 7)
            for r in range(2):
                for h in range(2):
                    nc.gpsimd.memset(vb[r][SEQ * h:SEQ * (h + 1), :, :, 2 * HD + h:2 * HD + h + 1],
                                     1.0).then_inc(setup_p, 1)
            pool.wait_ge(setup_p, 11)

            def slot2(s):
                if tile := s.tile(2):
                    ln_rstd_step(pool, 2, *tile)
                    ctx_lo_step(pool, 1, *tile, S2["v_psum"])
                if tile := s.tile(-2):
                    t, r = tile
                    after(pool, S2["d_aggr"], t)
                    nc.gpsimd.tensor_tensor(ve2[:, r:r + 1], mv2[:, r, 1:2], eps[:, 0:1], ALU.add).then_inc(S2["d_var"], 1)
                    after(pool, S2["d_var"], t)
                    after(pool, S2["dn"], t, 2)
                    nc.gpsimd.tensor_tensor(rstd2[:, r:r + 1], ve2[:, r:r + 1], mhalf[:, 0:1],
                                            ALU.pow).then_inc(S2["d_rstd"], 1)
                    after(pool, S2["dn"], t)
                    nc.gpsimd.tensor_tensor(dn[:, r, :], dn[:, r, :], rows[:, 2, :], ALU.mult).then_inc(S2["scaled"], 1)
                    after(pool, S2["scaled"], t)
                    nc.gpsimd.tensor_tensor(dn[:, r, :], dn[:, r, :], rows[:, 3, :], ALU.add).then_inc(S2["shifted"], 1)
                    after(pool, S2["shifted"], t)
                    nc.gpsimd.tensor_tensor(x[:, t, :], x[:, t, :], dn[:, r, :], ALU.add).then_inc(x_done[2], 1)

            slots(pool, TILES, -2, TILES + 1, slot2)

            def slot3(s):
                if tile := s.tile(1):
                    for k in range(2):
                        ln_rstd_step(pool, 3, tile[0] * 2 + k, k)

            slots(pool, GROUPS, -1, GROUPS - 2, slot3, low=2)

        @block.scalar
        def _(act):
            for i, (a, b) in enumerate(((L0_KV, L0_Q), (L0_Q, L0_O), (L0_O, L0_COLS))):
                act.wait_ge(w0_in[i], 16)
                nc.scalar.activation(w0h[:, a:b], raw[:, a:b], ACT.Copy).then_inc(w0_hi, 1)

            def slot0(s):
                if tile := s.tile(0):
                    t, r = tile
                    after(act, S0["kv_psum"], t)
                    after(act, S0["k_ready"], t, 2)
                    nc.scalar.activation(ek[:, r, :], PS[:, B_KV, 0:D], ACT.Exp).then_inc(S0["k_exp"], 1)
                    nc.scalar.activation(rk[:, r, :], PS[:, B_KV, 0:D], ACT.Relu).then_inc(S0["k_relu"], 1)
                    after(act, S0["ktv_psum"], t, 2)
                    act.wait_ge(setup_p, 5)
                    nc.scalar.activation(vx[r][:, :, 0:P], PS[:, B_KV, D:2 * D].rearrange("p (c n) -> p c n", c=2),
                                         ACT.Copy).then_inc(S0["v_ready"], 1)
                if tile := s.tile(2):
                    ctx_hi_step(act, 0, *tile, S0["kv_psum"])
                if s.ring == 0 and s.tile(0):
                    after(act, S0["q_psum"], s.pair)
                    after(act, S0["q_ready"], s.pair, 1)
                    nc.scalar.activation(eq, PS[:, B_Q, :], ACT.Exp).then_inc(S0["q_exp"], 1)
                    nc.scalar.activation(rq, PS[:, B_Q, :], ACT.Relu).then_inc(S0["q_relu"], 1)
                if tile := s.tile(0):
                    t, r = tile
                    after(act, S0["g_psum"], t)
                    after(act, S0["ag_ready"], t, 2)
                    nc.scalar.activation(thg[:, r, :], PS[:, B_GO, 0:D], ACT.Tanh,
                                         scale=0.5).then_inc(S0["gate_tanh"], 1)
                if tile := s.tile(2):
                    after(act, S0["g_psum"], tile[0], 2)
                    xT_hi_step(act, 0, *tile, B_T)
                if tile := s.tile(0):
                    weights_hi_step(act, 0, *tile)
                if tile := s.tile(-1):
                    t, r = tile
                    after(act, S0["agT_psum"], t)
                    after(act, S0["o_psum"], t, 2)
                    after(act, S0["agT_lo"], t, 2)
                    nc.scalar.activation(aTh[:, r, :], PS[:, B_TA, 0:D], ACT.Copy).then_inc(S0["agT_hi"], 1)

            slots(act, TILES, -2, TILES, slot0)

            act.wait_ge(x_done[0], TILES)
            down = S1["down"]

            def hidden_hi(t, group, at, bank):
                after(act, S1["hT_psum"], t, per=3, extra=group - 2)
                after(act, down, t, 1, per=3, extra=group - 2)
                nc.scalar.activation(fTh[:, at], PS[:, bank, 0:at.stop - at.start], ACT.Copy).then_inc(S1["hT_hi"], 1)

            def gate_tanh(t, group, at, bank):
                after(act, S1["g_psum"], t, per=3, extra=group - 2)
                after(act, S1["a"], t, 1, per=3, extra=group - 2)
                nc.scalar.activation(fth[:, at], PS[:, bank, 0:at.stop - at.start], ACT.Tanh,
                                     scale=0.5).then_inc(S1["tanh"], 1)

            def slot1(s):
                here, before, ahead = s.tile(0), s.tile(-1), s.tile(1)
                if before:
                    hidden_hi(before[0], 1, GROUP_B, F_H + 1)
                if here:
                    t, r = here
                    after(act, S1["gap"], t)
                    after(act, S1["w2"], t, 2)
                    nc.scalar.activation(tiny[:, r, 34:36], tiny[:, r, 32:34], ACT.Exp).then_inc(S1["gap_exp"], 1)
                    gate_tanh(t, 0, GROUP_A, F_G0)
                if before:
                    hidden_hi(before[0], 2, GROUP_C, F_H)
                if ahead:
                    after(act, S1["g_psum"], ahead[0], 2, per=3)
                    xT_hi_step(act, 1, *ahead, F_T)
                if here:
                    weights_hi_step(act, 1, t, r)
                    hidden_hi(t, 0, GROUP_A, F_H)
                    gate_tanh(t, 1, GROUP_B, F_G1)
                    gate_tanh(t, 2, GROUP_C, F_G0)

            slots(act, TILES, -1, TILES, slot1, low=2)

            act.wait_ge(x_done[1], TILES)
            act.wait_ge(setup_v, 6)

            def exp_scores(t, r):
                after(act, S2["clipped"], t, per=2)
                flat = pp[r].rearrange("p b i n -> p (b i n)")
                nc.scalar.activation(flat, flat, ACT.Exp).then_inc(S2["probs"], 1)

            def slot2(s):
                if s.ring == 0 and s.tile(0):
                    after(act, S2["k_psum"], s.pair)
                    after(act, S2["scores_psum"], s.at, 1)
                    for c in range(KC):
                        for h in range(2):
                            nc.scalar.activation(
                                kb[:, :, c, :, h, :],
                                PS[:, X_K, c * 2 * P:(c + 1) * 2 * P].rearrange("p (r b k) -> p r b k", r=2, b=2),
                                ACT.Identity, bias=bkm[:, c, h:h + 1], scale=headmask[:, h:h + 1],
                            ).then_inc(S2["kb_ready"], 1)
                if tile := s.tile(-2):
                    t, r = tile
                    after(act, S2["cnT_psum"], t)
                    after(act, S2["o_psum"], t, 2)
                    after(act, S2["cnT_lo"], t, 2)
                    nc.scalar.activation(aTh[:, r, :], PS[:, X_T, D:2 * D], ACT.Copy).then_inc(S2["cnT_hi"], 1)
                if s.ring == 1 and s.tile(-1):
                    exp_scores(*s.tile(-1))
                if s.ring == 0 and s.tile(0):
                    after(act, S2["q_psum"], s.pair)
                    after(act, S2["scores_psum"], s.at, 1)
                    for c in range(KC):
                        for j in range(2):
                            nc.scalar.activation(
                                qb[:, :, c, :, j, :],
                                PS[:, X_Q, c * 2 * P:(c + 1) * 2 * P].rearrange("p (r b q) -> p r b q", r=2, b=2),
                                ACT.Identity, bias=bqm[:, c, j:j + 1], scale=headmask[:, 2 + j:3 + j],
                            ).then_inc(S2["q_ready"], 1)
                if tile := s.tile(2):
                    ctx_hi_step(act, 1, *tile, S2["v_psum"])
                    after(act, S2["q_psum"], s.pair)
                    xT_hi_step(act, 2, *tile, X_T)
                if s.ring == 1 and s.tile(0):
                    exp_scores(*s.tile(0))

            slots(act, TILES, -2, TILES + 1, slot2)

            act.wait_ge(x_done[2], TILES)

            def slot3(s):
                if tile := s.tile(0):
                    g, r = tile
                    for n in range(NFF):
                        if n % 2 == 0:
                            after(act, S3["h_psum"], g, per=4, extra=n // 2 - 3)
                            after(act, S3["d_ready"], g, 2, per=4, extra=n // 2 - 3)
                        nc.scalar.activation(md16[:, r, n, :], PS[:, M_H + n // 2, (n % 2) * D:(n % 2 + 1) * D],
                                             ACT.Gelu, bias=cols[:, 2 * KC + n:2 * KC + n + 1]).then_inc(S3["gelu"], 1)
                if tile := s.tile(1):
                    g, r = tile
                    after(act, xT_psum, g, per=2, base=3 * TILES)
                    after(act, S3["h_psum"], g, 2, per=4)
                    for k in range(2):
                        src = PS[:, M_T, k * P:(k + 1) * P].bitcast(F16).rearrange("p (c t) -> p c t", c=KC)
                        nc.scalar.activation(mX[r][:, :, k * P:(k + 1) * P], src, ACT.Copy).then_inc(S3["x_ready"], 1)

            slots(act, GROUPS, -1, GROUPS - 1, slot3, low=2)

        @block.vector
        def _(dve):
            def split_w0(i, a, b):
                dve.wait_ge(w0_hi, i + 1)
                nc.vector.tensor_tensor(w0l[:, a:b], raw[:, a:b], w0h[:, a:b].bitcast(F32),
                                        ALU.subtract).then_inc(w0_lo, 1)

            def setup():
                dve.wait_ge(const_in, 16 * 3)
                dve.wait_ge(setup_p, 3)
                nc.vector.tensor_copy(bgh[:, :], bg_raw[:, :]).then_inc(setup_v, 1)
                nc.vector.tensor_copy(one_row[:, :], one_raw[:, :])
                dve.wait_ge(setup_v, 1)
                nc.vector.tensor_tensor(bgl[:, :], bg_raw[:, :], bgh[:, :].bitcast(F32),
                                        ALU.subtract).then_inc(setup_v, 1)

            def setup_late():
                dve.wait_ge(late_in, 16 * 6)
                nc.vector.tensor_copy(ident16[:, :], ident[:, :]).then_inc(setup_v, 1)
                for c in range(KC):
                    nc.vector.tensor_scalar(bqm[:, c, :], headmask[:, 2:4], cols[:, c:c + 1], None, ALU.mult)
                    nc.vector.tensor_scalar(bkm[:, c, :], headmask[:, 0:2], cols[:, KC + c:KC + c + 1], None, ALU.mult)
                nc.vector.tensor_scalar(rs[:, :], rs[:, :], 0.0, 0.3, ALU.max, ALU.min).then_inc(setup_v, 1)
                nc.vector.tensor_scalar(lim[:, :], mask_i[:, :], 0.5, 100.0, ALU.is_gt, ALU.mult).then_inc(setup_v, 1)
                dve.wait_ge(setup_v, 5)
                nc.vector.tensor_scalar(rows[:, 1, :], rows[:, 1, :], rs[:, 0:1], None, ALU.mult)
                nc.vector.tensor_scalar(lim[:, :], lim[:, :], -50.0, None, ALU.add).then_inc(setup_v, 1)

            split_w0(0, L0_KV, L0_Q)
            setup()

            def slot0(s):
                if tile := s.tile(2):
                    t, r = tile
                    if isinstance(t, int) and t in (0, 2):
                        dve.wait_ge(x_in[t // 2], 16)
                    ln_stats_step(dve, 0, t, r)
                if isinstance(s.at, int) and s.at == -2:
                    split_w0(1, L0_Q, L0_O)
                if tile := s.tile(-2):
                    t, r = tile
                    after(dve, S0["o_psum"], t)
                    nc.vector.tensor_tensor(x[:, t, :], PS[:, B_GO, D:2 * D], x[:, t, :], ALU.add).then_inc(x_done[0], 1)
                if tile := s.tile(0):
                    t, r = tile
                    after(dve, S0["k_exp"], t)
                    after(dve, S0["k_relu"], t)
                    after(dve, S0["ktv_psum"], t, 2)
                    nc.vector.scalar_tensor_tensor(out=kk[:, r, :], in0=ek[:, r, :], scalar=1.0, in1=rk[:, r, :],
                                                   op0=ALU.min, op1=ALU.add).then_inc(S0["k_ready"], 1)
                if tile := s.tile(2):
                    ln_norm_step(dve, 0, *tile, xn)
                if isinstance(s.at, int) and s.at == -2:
                    split_w0(2, L0_O, L0_COLS)
                if tile := s.tile(-1):
                    t, r = tile
                    at = PS[:, B_A, 0:2 * VC].rearrange("p (c n) -> p c n", c=2)
                    den, hz = (tiny[:, r, a:a + HEADS].rearrange("p (c h) -> p c h", c=2) for a in (0, HEADS))
                    after(dve, S0["attn_psum"], t)
                    nc.vector.tensor_scalar(den, at[:, :, P:VC], 1e-6, 2.0, ALU.add, ALU.mult).then_inc(S0["den"], 1)
                    after(dve, S0["den"], t)
                    nc.vector.reciprocal(hz, den).then_inc(S0["z"], 1)
                    after(dve, S0["z"], t)
                    nc.vector.tensor_tensor(
                        az.rearrange("p (c h e) -> p c h e", c=2, h=HPC),
                        at[:, :, 0:P].rearrange("p c (h e) -> p c h e", h=HPC),
                        hz.unsqueeze(3).to_broadcast([P, 2, HPC, HD]), ALU.mult).then_inc(S0["az"], 1)
                    after(dve, S0["az"], t)
                    after(dve, S0["gate_tanh"], t)
                    after(dve, S0["agT_psum"], t, 2)
                    nc.vector.scalar_tensor_tensor(out=ag[:, r, :], in0=thg[:, r, :], scalar=1.0, in1=az,
                                                   op0=ALU.add, op1=ALU.mult).then_inc(S0["ag_ready"], 1)
                if s.ring == 0 and s.tile(0):
                    after(dve, S0["q_exp"], s.pair)
                    after(dve, S0["q_relu"], s.pair)
                    after(dve, S0["attn_psum"], s.at, 1)
                    nc.vector.scalar_tensor_tensor(out=qq, in0=eq, scalar=1.0, in1=rq,
                                                   op0=ALU.min, op1=ALU.add).then_inc(S0["q_ready"], 1)
                if tile := s.tile(2):
                    xT_lo_step(dve, 0, *tile, B_T)
                if tile := s.tile(0):
                    t, r = tile
                    after(dve, S0["ktv_psum"], t)
                    after(dve, S0["attn_psum"], t, 2)
                    for b in range(2):
                        last = nc.vector.tensor_tensor(smat[:, r, b, :], PS[:, B_S + b, 0:2 * VC], blockmask[:, :],
                                                       ALU.mult)
                    last.then_inc(S0["s_ready"], 1)
                if tile := s.tile(-1):
                    t, r = tile
                    after(dve, S0["agT_hi"], t)
                    after(dve, S0["o_psum"], t, 2)
                    nc.vector.tensor_tensor(aTl[:, r, :], PS[:, B_TA, 0:D], aTh[:, r, :].bitcast(F32),
                                            ALU.subtract).then_inc(S0["agT_lo"], 1)
                if tile := s.tile(0):
                    weights_lo_step(dve, 0, *tile)

            slots(dve, TILES, -2, TILES + 1, slot0)
            dve.wait_ge(x_done[0], TILES)
            setup_late()

            def router(t, r):
                sc, mx8, gap, e2, w3, c1, c2, comb, dn2, ixf = (
                    tiny[:, r, a:a + n] for a, n in (
                        (0, 10), (16, 8), (32, 2), (34, 2), (36, 3), (40, 8), (48, 8), (56, 8), (64, 2), (66, 2)))
                ix = tinyi[:, r, :]
                after(dve, S1["router_psum"], t)
                nc.vector.tensor_copy(sc, PS[:, F_T, D:D + 10]).then_inc(S1["scores"], 1)
                after_plain(dve, (late_in, 16 * 6), S1["scores"], t)
                nc.vector.max(mx8, sc[:, 0:8]).then_inc(S1["top"], 1)
                nc.vector.tensor_scalar(gap[:, 1:2], sc[:, 8:9], -1.0, None, ALU.mult)
                after(dve, S1["top"], t)
                nc.vector.tensor_tensor(gap[:, 0:1], mx8[:, 1:2], mx8[:, 0:1], ALU.subtract).then_inc(S1["gap"], 1)
                nc.vector.max_index(ix, mx8, sc[:, 0:8]).then_inc(S1["index"], 1)
                after(dve, S1["index"], t)
                nc.vector.tensor_copy(ixf, ix[:, 0:2]).then_inc(S1["indexf"], 1)
                after(dve, S1["gap_exp"], t)
                nc.vector.tensor_scalar(dn2, e2, 2.0, 2.0, ALU.mult, ALU.add).then_inc(S1["denom"], 1)
                after(dve, S1["denom"], t)
                nc.vector.reciprocal(w3[:, 0:2], dn2).then_inc(S1["weights"], 1)
                after(dve, S1["weights"], t)
                nc.vector.tensor_tensor(w3[:, 2:3], w3[:, 0:1], e2[:, 0:1], ALU.mult).then_inc(S1["w2"], 1)
                after(dve, S1["indexf"], t)
                nc.vector.tensor_scalar(c1, iota8[:, :], ixf[:, 0:1], w3[:, 0:1], ALU.is_equal,
                                        ALU.mult).then_inc(S1["pick1"], 1)
                after(dve, S1["w2"], t)
                nc.vector.tensor_scalar(c2, iota8[:, :], ixf[:, 1:2], w3[:, 2:3], ALU.is_equal,
                                        ALU.mult).then_inc(S1["pick2"], 1)
                after(dve, S1["pick1"], t)
                after(dve, S1["pick2"], t)
                nc.vector.tensor_tensor(comb, c1, c2, ALU.add).then_inc(S1["comb"], 1)
                return comb, w3[:, 1:2]

            def hidden_lo(t, group, at, bank):
                after(dve, S1["hT_hi"], t, per=3, extra=group - 2)
                nc.vector.tensor_tensor(fTl[:, at], PS[:, bank, 0:at.stop - at.start], fTh[:, at].bitcast(F32),
                                        ALU.subtract).then_inc(S1["hT_lo"], 1)

            def gate_factor(t, group, at, bank):
                after(dve, S1["tanh"], t, per=3, extra=group - 2)
                nc.vector.scalar_tensor_tensor(out=fa[:, at], in0=fth[:, at], scalar=1.0,
                                               in1=PS[:, bank, 0:at.stop - at.start],
                                               op0=ALU.add, op1=ALU.mult).then_inc(S1["a"], 1)

            def hidden(t, group, parts, bank, first):
                after(dve, S1["a"], t, per=3, extra=group - 2)
                after(dve, S1["comb"], t)
                after(dve, S1["hT_psum"], t, 1, per=3, extra=group - 2)
                for c, weight in parts:
                    u = first + c.start - parts[0][0].start
                    last = nc.vector.scalar_tensor_tensor(
                        out=fh[:, c], in0=fa[:, c], scalar=weight, in1=PS[:, bank, u:u + c.stop - c.start],
                        op0=ALU.mult, op1=ALU.mult)
                last.then_inc(S1["h"], 1)

            def slot1(s):
                here, before, ahead = s.tile(0), s.tile(-1), s.tile(1)
                if before:
                    hidden_lo(before[0], 1, GROUP_B, F_H + 1)
                if here:
                    t, r = here
                    comb, shared_gate = router(t, r)
                    experts = [(slice(EH * e, EH * (e + 1)), comb[:, e:e + 1]) for e in range(EXPERTS)]
                if here:
                    gate_factor(t, 0, GROUP_A, F_G0)
                    hidden(t, 0, experts[:4], F_U0, 0)
                if before:
                    hidden_lo(before[0], 2, GROUP_C, F_H)
                if ahead:
                    xT_lo_step(dve, 1, *ahead, F_T)
                if here:
                    weights_lo_step(dve, 1, t, r)
                if tile := s.tile(2):
                    ln_stats_step(dve, 1, *tile)
                    ln_norm_step(dve, 1, *tile, xn)
                if here:
                    hidden_lo(t, 0, GROUP_A, F_H)
                if before:
                    after(dve, S1["down"], before[0], per=3)
                    nc.vector.tensor_tensor(x[:, before[0], :], PS[:, F_O, 0:D], x[:, before[0], :],
                                            ALU.add).then_inc(x_done[1], 1)
                if here:
                    gate_factor(t, 1, GROUP_B, F_G1)
                    hidden(t, 1, experts[4:], F_U1, 0)
                    gate_factor(t, 2, GROUP_C, F_G0)
                    hidden(t, 2, [(GROUP_C, shared_gate)], F_G0, SH)

            slots(dve, TILES, -2, TILES, slot1, low=2)
            dve.wait_ge(x_done[1], TILES)

            def values(t, r):
                after(dve, S2["v_psum"], t)
                after(dve, S2["pv_psum"], t, 2)
                dve.wait_ge(setup_p, 11)

                def heads(ap, b, h):
                    return ap[SEQ * b:SEQ * (b + 1)].rearrange("p (g h e) -> p g h e", g=PAIRS, h=2)[:, :, h, :]

                for b in range(2):
                    for h in range(2):
                        last = nc.vector.tensor_tensor(
                            vb[r][SEQ * h:SEQ * (h + 1), b, :, HD * h:HD * (h + 1)],
                            heads(PS[:, X_V, 0:D], b, h), heads(rows[:, 0, :], b, h), ALU.add)
                last.then_inc(S2["vb_ready"], 1)

            def delta(t, r):
                after(dve, S2["o_psum"], t)
                after(dve, S2["dn"], t, 2)
                nc.vector.scalar_tensor_tensor(out=dl[:, r, :], in0=PS[:, X_O, 0:D], scalar=rs[:, 0:1],
                                               in1=bo_rs, op0=ALU.mult, op1=ALU.add).then_inc(S2["delta"], 1)
                after(dve, S2["delta"], t)
                after(dve, S2["d_var"], t, 2)
                nc.vector.bn_stats(st2[:, r, :], dl[:, r, :]).then_inc(S2["d_stats"], 1)
                after_plain(dve, (x_in[0], 16), S2["d_stats"], t)
                nc.vector.bn_aggr(mv2[:, r, :], st2[:, r, :]).then_inc(S2["d_aggr"], 1)

            def normalise(t, r):
                cx = PS[:, X_C, 0:PAIRS * PVC].rearrange("p (g n) -> p g n", g=PAIRS)
                sums = cx[:, :, 2 * HD:PVC]
                guard, den, rden = (tiny[:, r, a:a + HEADS].rearrange("p (g h) -> p g h", h=2) for a in (0, 16, 32))
                after(dve, S2["pv_psum"], t)
                nc.vector.tensor_scalar(guard, sums, 1e-8, None, ALU.mult).then_inc(S2["guard"], 1)
                after(dve, S2["guard"], t)
                nc.vector.tensor_tensor(den, sums, guard, ALU.add).then_inc(S2["den"], 1)
                after(dve, S2["den"], t)
                nc.vector.reciprocal(rden, den).then_inc(S2["rden"], 1)
                after(dve, S2["rden"], t)
                after(dve, S2["cnT_psum"], t, 2)
                nc.vector.tensor_tensor(
                    cn[:, r, :].rearrange("p (g h e) -> p g h e", g=PAIRS, h=2),
                    cx[:, :, 0:2 * HD].rearrange("p g (h e) -> p g h e", h=2),
                    rden.unsqueeze(3).to_broadcast([P, PAIRS, 2, HD]), ALU.mult).then_inc(S2["cn_ready"], 1)

            def clip(t, r):
                after(dve, S2["scores_psum"], t)
                after(dve, S2["pv_psum"], t, 2)
                for b in range(2):
                    nc.vector.tensor_scalar(pp[r][:, b, :, :], PS[:, X_S:X_S + 2, b * 2 * P:(b + 1) * 2 * P],
                                            -50.0, lim[:, bass.ds(t * 2 + b, 1)], ALU.max,
                                            ALU.min).then_inc(S2["clipped"], 1)

            def slot2(s):
                if s.ring == 1 and s.tile(-1):
                    clip(*s.tile(-1))
                if tile := s.tile(2):
                    ln_stats_step(dve, 2, *tile)
                if tile := s.tile(-2):
                    t, r = tile
                    after(dve, S2["cnT_hi"], t)
                    after(dve, S2["o_psum"], t, 2)
                    nc.vector.tensor_tensor(aTl[:, r, :], PS[:, X_T, D:2 * D], aTh[:, r, :].bitcast(F32),
                                            ALU.subtract).then_inc(S2["cnT_lo"], 1)
                if tile := s.tile(0):
                    values(*tile)
                if tile := s.tile(2):
                    ln_norm_step(dve, 2, *tile, xn)
                if s.ring == 1 and s.tile(0):
                    clip(*s.tile(0))
                if s.ring == 0 and s.tile(-1):
                    normalise(*s.tile(-1))
                if tile := s.tile(-2):
                    delta(*tile)
                if tile := s.tile(2):
                    xT_lo_step(dve, 2, *tile, X_T)
                if tile := s.tile(-2):
                    t, r = tile
                    after(dve, S2["d_rstd"], t)
                    after(dve, x_done[2], t, 2)
                    nc.vector.tensor_scalar(dn[:, r, :], dl[:, r, :], mv2[:, r, 0:1], rstd2[:, r:r + 1],
                                            ALU.subtract, ALU.mult).then_inc(S2["dn"], 1)
                if s.ring == 1 and s.tile(-1):
                    normalise(*s.tile(-1))

            slots(dve, TILES, -2, TILES + 1, slot2)
            dve.wait_ge(x_done[2], TILES)

            def slot3(s):
                if tile := s.tile(1):
                    for k in range(2):
                        ln_stats_step(dve, 3, tile[0] * 2 + k, k)
                    for k in range(2):
                        ln_norm_step(dve, 3, tile[0] * 2 + k, k, mx16)
                if tile := s.tile(0):
                    g, r = tile
                    for i in range(4):
                        after(dve, S3["gelu"], g, per=8, extra=2 * i - 6)
                        after(dve, S3["o_psum"], g, 2)
                        nc.vector.tensor_copy(mD[r][:, 2 * i:2 * i + 2, :],
                                              md16[:, r, 2 * i:2 * i + 2, :]).then_inc(S3["d_ready"], 1)
                if tile := s.tile(-1):
                    g, r = tile
                    after(dve, S3["o_psum"], g)
                    after(dve, S3["o_ready"], g, 1)
                    nc.vector.tensor_tensor(me16, PS[:, M_O, :].rearrange("p (k n) -> p k n", k=2),
                                            rows[:, 4, :].unsqueeze(1).to_broadcast([P, 2, D]),
                                            ALU.add).then_inc(S3["e16"], 1)
                    after(dve, S3["e16"], g)
                    if not (isinstance(g, int) and g < 2):
                        dve.wait_ge(stored[r], g * 8 + (-8 * r))
                    nc.vector.tensor_tensor(mo[:, r, :, :], x[:, bass.ds(g * 2, 2), :], me16,
                                            ALU.add).then_inc(S3["o_ready"], 1)

            slots(dve, GROUPS, -1, GROUPS, slot3)

        @block.tensor
        def _(pe):
            pe.wait_ge(const_in, 16 * 3)

            def slot0(s):
                if tile := s.tile(0):
                    t, r = tile
                    after(pe, ctx_lo, t)
                    after(pe, ctx_hi, t)
                    if isinstance(t, int) and t == 0:
                        pe.wait_ge(w0_lo, 1)
                    after(pe, S0["v_ready"], t, 1)
                    for c in range(KC):
                        last = product(PS[:, B_KV, :], cT(r, c), [w[:, c, :] for w in kvw], c == 0, c == KC - 1)
                    last.then_inc(S0["kv_psum"], 1)
                if tile := s.tile(-2):
                    t, r = tile
                    after(pe, S0["agT_lo"], t)
                    if next_tile := s.tile(-1):
                        after(pe, S0["gate_tanh"], next_tile[0])
                    after(pe, x_done[0], t, 1)
                    for c in range(KC):
                        last = product(PS[:, B_GO, D:2 * D], aT(r, c), [w[:, c, :] for w in ow], c == 0, c == KC - 1)
                    last.then_inc(S0["o_psum"], 1)
                if tile := s.tile(-1):
                    t, r = tile
                    after(pe, S0["q_ready"], (s.pair, s.pair - 1)[s.ring == 0])
                    after(pe, S0["s_ready"], t)
                    after(pe, S0["az"], t, 1)
                    for b in range(2):
                        for c in range(KC):
                            at = c * 2 * P + r * P + SEQ * b
                            last = nc.tensor.matmul(PS[SEQ * b:SEQ * (b + 1), B_A, c * VC:(c + 1) * VC],
                                                    qq[:, at:at + SEQ], smat[:, r, b, c * VC:(c + 1) * VC],
                                                    start=True, stop=True)
                    last.then_inc(S0["attn_psum"], 1)
                if s.ring == 0 and s.tile(0):
                    after(pe, xT_lo, s.at, -1)
                    after(pe, S0["q_exp"], s.pair, 1)
                    after(pe, S0["q_relu"], s.pair, 1)
                    if isinstance(s.at, int) and s.at == 0:
                        pe.wait_ge(w0_lo, 2)
                    for m in range(KC):
                        for c in range(KC):
                            last = product(PS[:, B_Q, m * 2 * P:(m + 1) * 2 * P],
                                           [w[:, c, m * P:(m + 1) * P] for w in qw], pair((xTh, xTl), c),
                                           c == 0, c == KC - 1)
                    last.then_inc(S0["q_psum"], 1)
                if tile := s.tile(0):
                    t, r = tile
                    after(pe, xT_lo, t)
                    after(pe, S0["gate_tanh"], t, 1)
                    after(pe, x_done[0], t, 2)
                    if isinstance(t, int) and t == 0:
                        pe.wait_ge(setup_v, 2)
                    for c in range(KC):
                        product(PS[:, B_GO, 0:D], xT(r, c), [w[:, c, :] for w in gw], c == 0, False)
                    nc.tensor.matmul(PS[:, B_GO, 0:D], one_row[:, :], bgh[:, :], start=False, stop=False)
                    nc.tensor.matmul(PS[:, B_GO, 0:D], one_row[:, :], bgl[:, :], start=False,
                                     stop=True).then_inc(S0["g_psum"], 1)
                if tile := s.tile(2):
                    transpose_x(pe, 0, *tile, B_T)
                if tile := s.tile(0):
                    t, r = tile
                    after(pe, S0["k_ready"], t)
                    after(pe, S0["v_ready"], t)
                    after(pe, S0["s_ready"], t, 1)
                    for b in range(2):
                        for c in range(KC):
                            last = nc.tensor.matmul(PS[:, B_S + b, c * VC:(c + 1) * VC],
                                                    kk[SEQ * b:SEQ * (b + 1), r, c * P:(c + 1) * P],
                                                    vx[r][SEQ * b:SEQ * (b + 1), c, :], start=True, stop=True)
                    last.then_inc(S0["ktv_psum"], 1)
                if tile := s.tile(-1):
                    t, r = tile
                    after(pe, S0["ag_ready"], t)
                    after(pe, S0["agT_lo"], t, 1)
                    for c in range(KC):
                        last = nc.tensor.transpose(PS[:, B_TA, c * P:(c + 1) * P], ag[:, r, c * P:(c + 1) * P],
                                                   ident[:, :])
                    last.then_inc(S0["agT_psum"], 1)

            slots(pe, TILES, -2, TILES + 1, slot0)

            pe.wait_ge(x_done[0], TILES)
            pe.wait_ge(w_lo, TILES)
            R0 = 2 * EXPERTS * EH + 2 * SH

            def expert_in(t, r, bank, at):
                for c in range(KC):
                    last = product(PS[:, bank, :], xT(r, c), [w[:, c, at:at + 512] for w in f1w], c == 0, c == KC - 1)
                return last

            def hidden_T(first, n, bank):
                for i in range(n):
                    last = nc.tensor.transpose(PS[:, bank, i * P:(i + 1) * P],
                                               fh[:, (first + i) * P:(first + i + 1) * P], ident[:, :])
                last.then_inc(S1["hT_psum"], 1)

            def expert_out(first, n, start, stop):
                for i in range(first, first + n):
                    last = product(PS[:, F_O, 0:D], [w[:, i * P:(i + 1) * P] for w in (fTh, fTl)],
                                   [w[:, i, :] for w in f2w], start and i == first, stop and i == first + n - 1)
                last.then_inc(S1["down"], 1)
                return last

            def slot1(s):
                here, before, ahead = s.tile(0), s.tile(-1), s.tile(1)
                if here:
                    t, r = here
                    after(pe, xT_lo, t, base=TILES)
                    for c in range(KC):
                        last = product(PS[:, F_T, D:D + 10], xT(r, c), [w[:, c, R0:R0 + 10] for w in f1w], c == 0,
                                       c == KC - 1)
                    last.then_inc(S1["router_psum"], 1)
                    after(pe, S1["h"], t, 1, per=3)
                    expert_in(t, r, F_G0, 0)
                    expert_in(t, r, F_U0, 512).then_inc(S1["g_psum"], 1)
                if ahead:
                    if here:
                        after(pe, S1["scores"], t)
                    transpose_x(pe, 1, *ahead, F_T)
                if before:
                    after(pe, S1["h"], before[0], per=3)
                    after(pe, S1["hT_lo"], before[0], per=3, extra=-2)
                    hidden_T(8, 2, F_H)
                    after(pe, S1["hT_lo"], before[0], per=3, extra=-1)
                    expert_out(4, 4, False, False)
                if here:
                    after(pe, S1["h"], t, 1, per=3, extra=-1)
                    expert_in(t, r, F_G1, 1024)
                    expert_in(t, r, F_U1, 1536).then_inc(S1["g_psum"], 1)
                    after(pe, S1["h"], t, per=3, extra=-2)
                    after(pe, S1["hT_lo"], t, 1, per=3)
                    hidden_T(0, 4, F_H)
                if before:
                    after(pe, S1["hT_lo"], before[0], per=3)
                    expert_out(8, 2, False, True)
                if here:
                    expert_in(t, r, F_G0, 2048).then_inc(S1["g_psum"], 1)
                    after(pe, S1["hT_lo"], t, per=3, extra=-2)
                    after(pe, x_done[1], t, 1)
                    expert_out(0, 4, True, False)
                    after(pe, S1["h"], t, per=3, extra=-1)
                    hidden_T(4, 4, F_H + 1)

            slots(pe, TILES, -1, TILES, slot1, low=2)

            pe.wait_ge(x_done[1], TILES)
            pe.wait_ge(w_lo, 2 * TILES)

            def by_feature(bank, weights, right):
                for m in range(KC):
                    for c in range(KC):
                        last = product(PS[:, bank, m * 2 * P:(m + 1) * 2 * P],
                                       [w[:, c, m * P:(m + 1) * P] for w in weights], pair(right, c),
                                       c == 0, c == KC - 1)
                return last

            def weighted_values(t, r):
                after(pe, S2["probs"], t)
                after(pe, S2["vb_ready"], t)
                after(pe, S2["cn_ready"], t, 1)
                for b in range(2):
                    for g in range(PAIRS):
                        c, i, j = g // PPC, g // 2 % 2, g % 2
                        last = nc.tensor.matmul(PS[SEQ * b:SEQ * (b + 1), X_C, g * PVC:(g + 1) * PVC],
                                                pp[r][:, b, i, (c * 2 + j) * SEQ:(c * 2 + j + 1) * SEQ],
                                                vb[r][:, b, g, :], start=True, stop=True)
                last.then_inc(S2["pv_psum"], 1)

            def output(t, r):
                after(pe, S2["cnT_lo"], t)
                after(pe, S2["delta"], t, 1)
                for c in range(KC):
                    last = product(PS[:, X_O, 0:D], aT(r, c), [w[:, c, :] for w in o1w], c == 0, c == KC - 1)
                last.then_inc(S2["o_psum"], 1)

            def scores(t, r, pair_at):
                after(pe, S2["kb_ready"], pair_at, per=4)
                after(pe, S2["q_ready"], pair_at, per=4)
                after(pe, S2["clipped"], t, 1, per=2)
                for b in range(2):
                    for c in range(KC):
                        for i in range(2):
                            f = slice(P // 2 * i, P // 2 * (i + 1))
                            last = nc.tensor.matmul(
                                PS[:, X_S + i, (b * KC + c) * P:(b * KC + c + 1) * P],
                                kb[f, r, c, b, :, :].rearrange("p h k -> p (h k)"),
                                qb[f, r, c, b, :, :].rearrange("p j q -> p (j q)"), start=True, stop=True)
                last.then_inc(S2["scores_psum"], 1)

            def slot2(s):
                if s.ring == 0 and s.tile(0):
                    after(pe, ctx_lo, s.at, -1, base=TILES)
                    after(pe, S2["kb_ready"], s.pair, 1, per=4)
                    by_feature(X_K, k1w, (cTh, cTl)).then_inc(S2["k_psum"], 1)
                if tile := s.tile(0):
                    t, r = tile
                    after(pe, ctx_lo, t, base=TILES)
                    after(pe, S2["vb_ready"], t, 1)
                    for c in range(KC):
                        last = product(PS[:, X_V, 0:D], cT(r, c), [w[:, c, :] for w in v1w], c == 0, c == KC - 1)
                    last.then_inc(S2["v_psum"], 1)
                if tile := s.tile(-2):
                    t, r = tile
                    after(pe, S2["cn_ready"], t)
                    if t_ahead := s.tile(1):
                        after(pe, xT_lo, t_ahead[0], base=2 * TILES)
                    for c in range(KC):
                        last = nc.tensor.transpose(PS[:, X_T, D + c * P:D + (c + 1) * P], cn[:, r, c * P:(c + 1) * P],
                                                   ident[:, :])
                    last.then_inc(S2["cnT_psum"], 1)
                if s.ring == 0:
                    if s.tile(0):
                        after(pe, xT_lo, s.at, -1, base=2 * TILES)
                        after(pe, S2["q_ready"], s.pair, 1, per=4)
                        by_feature(X_Q, q1w, (xTh, xTl)).then_inc(S2["q_psum"], 1)
                    if s.tile(-1):
                        weighted_values(*s.tile(-1))
                if s.ring == 1 and s.tile(0):
                    scores(*s.tile(0), s.pair)
                if s.tile(-2):
                    output(*s.tile(-2))
                if tile := s.tile(2):
                    if before := s.tile(-2):
                        after(pe, S2["cnT_lo"], before[0])
                    transpose_x(pe, 2, *tile, X_T)
                if s.ring == 0 and s.tile(0):
                    scores(*s.tile(0), s.pair)
                if s.ring == 1 and s.tile(-1):
                    weighted_values(*s.tile(-1))

            slots(pe, TILES, -2, TILES + 1, slot2)

            pe.wait_ge(x_done[2], TILES)
            pe.wait_ge(setup_v, 6)

            def slot3(s):
                if tile := s.tile(0):
                    g, r = tile
                    after(pe, S3["x_ready"], g, per=2)
                    for n in range(NFF):
                        if n % 2 == 0:
                            after(pe, S3["gelu"], g, 1, per=8, extra=n - 6)
                        for c in range(KC):
                            for w in range(2):
                                last = nc.tensor.matmul(PS[:, M_H + n // 2, (n % 2) * D:(n % 2 + 1) * D],
                                                        m0w[w][:, c, n * P:(n + 1) * P], mX[r][:, c, :],
                                                        start=c + w == 0, stop=c + w == 2)
                        if n % 2:
                            last.then_inc(S3["h_psum"], 1)
                if tile := s.tile(-1):
                    g, r = tile
                    after(pe, S3["d_ready"], g, per=4)
                    after(pe, S3["e16"], g, 1)
                    for k in range(2):
                        for n in range(NFF):
                            for w in range(2):
                                last = nc.tensor.matmul(PS[:, M_O, k * D:(k + 1) * D],
                                                        mD[r][:, n, k * P:(k + 1) * P], m1w[w][:, n, :],
                                                        start=n + w == 0, stop=n + w == NFF)
                    last.then_inc(S3["o_psum"], 1)
                if tile := s.tile(1):
                    g, r = tile
                    after(pe, S3["x_ready"], g, 1, per=2)
                    for k in range(2):
                        after(pe, xn_ready, g, per=2, base=3 * TILES, extra=k - 1)
                        for c in range(KC):
                            last = nc.tensor.transpose(
                                PS[:, M_T, k * P + c * SEQ:k * P + (c + 1) * SEQ].bitcast(F16),
                                mx16[:, k, c * P:(c + 1) * P], ident16[:, :])
                        last.then_inc(xT_psum, 1)

            slots(pe, GROUPS, -1, GROUPS, slot3, low=2)


def by_contraction(w):
    n, k = w.shape
    return np.ascontiguousarray(w.T.reshape(k // P, P, n).transpose(1, 0, 2)).reshape(P, -1)


def laid_out(i):
    i = {k: np.asarray(v) for k, v in i.items()}
    f = np.float32
    lane = np.arange(P)
    a = {"x": i["x"].reshape(TOKENS, D)}
    a["ctxT"] = i["ctx_2048"].reshape(TILES, P, KC, P).transpose(0, 3, 2, 1).reshape(TILES, P, D)
    a["w_l0"] = np.concatenate([by_contraction(i["L0_xattn_" + n]) for n in ("Wkv", "Wq", "Wg", "Wo")], 1)
    gates, ups = (i["L0_ffn_" + n].reshape(2, 4 * EH, D) for n in ("w_gate", "w_up"))
    w1 = np.concatenate([gates[0], ups[0], gates[1], ups[1], i["L0_ffn_sh_gate"], i["L0_ffn_sh_up"],
                         i["L0_ffn_gate_w"], i["L0_ffn_se_gate_w"], np.zeros((1, D), f)])
    ffn = np.concatenate([by_contraction(w1), i["L0_ffn_w_down"].transpose(2, 0, 1).reshape(P, -1),
                          by_contraction(i["L0_ffn_sh_down"]), np.zeros((P, FFN_COLS - FFN_USED), f)], 1)
    a["w_ffn"] = ffn.reshape(P, TILES, FFN_CHUNK).transpose(1, 0, 2)
    l1 = np.concatenate([by_contraction(i[n]) for n in ("L1_xattn_Wq", "L1_xattn_Wk", "L1_xattn_Wv", "L1_xattn_Wo",
                                                        "L1_ffn_W0", "L1_ffn_W1")], 1)
    a["w_l1"] = l1.reshape(P, TILES, L1_CHUNK).transpose(1, 0, 2)
    a["rows"] = np.broadcast_to(np.stack([i[n] for n in ("L1_xattn_bv", "L1_xattn_bo", "L1_xattn_ln_gamma",
                                                         "L1_xattn_ln_beta", "L1_ffn_bias1")]), (P, 5, D))
    a["cols"] = np.concatenate([i[n].reshape(-1, P).T for n in ("L1_xattn_bq", "L1_xattn_bk", "L1_ffn_bias0")], 1)
    a["bg"] = i["L0_xattn_bg"].reshape(1, D)
    a["rs"] = np.broadcast_to(i["L1_xattn_residual_scale"].reshape(1, 1), (P, 1))
    mask = i["mask_BxS2_ik0"].T
    a["mask"] = np.concatenate([mask, mask], 0)
    a["ident"] = np.eye(P, dtype=f)
    own = (lane[:, None] // HD == np.arange(VC)[None, :] // HD)
    own[:, P:] = lane[:, None] // HD == np.arange(HPC)[None, :]
    a["blockmask"] = np.concatenate([own, own], 1).astype(f)
    a["headmask"] = np.concatenate([0.25 * (lane[:, None] // HD % 2 == np.arange(2)),
                                    lane[:, None] // (2 * HD) % 2 == np.arange(2)], 1).astype(f)
    a["iota8"] = np.tile(np.arange(EXPERTS, dtype=f), (P, 1))
    return {k: np.ascontiguousarray(v) for k, v in a.items()}


def kernel(**inputs):
    import concourse.bacc as _bacc
    from concourse.bass_utils import run_bass_kernel_spmd as _run

    nc = _bacc.Bacc("TRN2", target_bir_lowering=False, num_devices=1, dynamic_dma_scratch_size=2048)
    arrays = laid_out(inputs)
    args = {n: nc.dram_tensor("in_" + n, a.shape, mybir.dt.from_np(a.dtype), kind="ExternalInput").ap()
            for n, a in arrays.items()}
    out = nc.dram_tensor("out", (TOKENS, D), F32, kind="ExternalOutput").ap()
    build(nc, args, out)
    r = _run(nc, [{"in_" + n: a for n, a in arrays.items()}], core_ids=[0])
    return r.results[0]["out"].reshape(BATCHES, SEQ, D)
```

```python
from contextlib import ExitStack

import numpy as np

import concourse.bass as bass
from concourse import mybir

F32 = mybir.dt.float32
F32R = mybir.dt.float32r
F16 = mybir.dt.float16
I32 = mybir.dt.int32
U32 = mybir.dt.uint32
ALU = mybir.AluOpType
ACT = mybir.ActivationFunctionType

P = 128
BATCHES, SEQ, D = 32, 64, 256
TOKENS = BATCHES * SEQ
TILES = TOKENS // P
PER_TILE = P // SEQ
KC = D // P
HEADS, HD = 16, 16
HPC = P // HD
PAIRS = HEADS // 2
PPC = P // (2 * HD)
EXPERTS, EH = 8, 128
SH = 256
FF = 1024
NFF = FF // P
PER_GROUP = 2
GROUPS = TILES // PER_GROUP
EARLY, LATE = range(6), range(6, NFF)
VC = P + HPC
PVC = 2 * HD + 2

L0_KV, L0_Q, L0_G, L0_O = 0, 2 * 512, 2 * 512 + 2 * D, 2 * 512 + 4 * D
L0_COLS = L0_O + 2 * D
W1_COLS = 2 * EXPERTS * EH + 2 * SH + EXPERTS + 2
FFN_USED = KC * W1_COLS + (EXPERTS + SH // P) * D
FFN_CHUNK = -(-FFN_USED // TILES // 2) * 2
FFN_COLS = FFN_CHUNK * TILES
L1_Q, L1_K, L1_V, L1_O = 0, 2 * D, 4 * D, 6 * D
L1_W0 = 8 * D
L1_W1 = L1_W0 + KC * FF
L1_COLS = L1_W1 + NFF * D
L1_CHUNK = L1_COLS // TILES

GROUP_A, GROUP_B, GROUP_C = slice(0, 512), slice(512, 1024), slice(1024, 1280)

ARENA_R = 5120
ARENA_F = 6784

B_T, B_Q, B_GO, B_KV, B_A, B_S, B_TA = 0, 1, 2, 3, 4, 5, 7
F_T, F_G0, F_U0, F_G1, F_U1, F_O, F_H = 0, 1, 3, 4, 2, 5, 6
X_T, X_Q, X_K, X_V, X_O, X_C, X_S = 0, 1, 2, 3, 4, 5, 6
M_T, M_H, M_O = 0, 1, 5


class Slot:

    def __init__(self, at, ring, count, pair=None):
        self.at, self.ring, self.count = at, ring, count
        self.pair = at // 2 if isinstance(at, int) else pair

    def tile(self, ahead):
        t = self.at + ahead
        if isinstance(t, int) and not 0 <= t < self.count:
            return None
        return t, (self.ring + ahead) % 2


    def next(self, ahead, over=2):
        t = self.at + ahead
        if isinstance(t, int) and not 0 <= t < self.count + over:
            return None
        return t, (self.ring + ahead) % 2

    def is_at(self, at):
        return isinstance(self.at, int) and self.at == at


def slots(eng, count, first, last, body, low=4):
    high = (count - 1) // 2 * 2
    for s in range(first, low):
        body(Slot(s, s % 2, count))
    with eng.Fori(low // 2, high // 2) as i:
        body(Slot(i * 2, 0, count, i))
        body(Slot(i * 2 + 1, 1, count, i))
    for s in range(high, last + 1):
        body(Slot(s, s % 2, count))


def after(eng, sem, t, back=0, base=0, per=1, extra=0):
    if isinstance(t, int) and t - back < 0:
        if base:
            eng.wait_ge(sem, base)
        return
    eng.wait_ge(sem, t * per + (base + per * (1 - back) + extra))


def after_plain(eng, held, sem, t, base=0):
    value = t + (base + 1)
    if not isinstance(t, int):
        value = eng.to_reg(value)
    eng.wait_ge(*held)
    eng.wait_ge(sem, value)


def build(nc, A, out):
    with ExitStack() as ctx:
        def sb(name, shape, dt=F32):
            return ctx.enter_context(nc.sbuf_tensor(name, shape, dt))

        def sem(name):
            return ctx.enter_context(nc.semaphore(name))

        x = sb("x", [P, TILES, D])
        raw = sb("raw", [P, L0_COLS])
        w0h, w0l = sb("w0h", [P, L0_COLS], F32R), sb("w0l", [P, L0_COLS], F32R)
        wfh, wfl = sb("wfh", [P, FFN_COLS], F32R), sb("wfl", [P, FFN_COLS], F32R)
        w1h, w1l = sb("w1h", [P, L1_COLS], F32R), sb("w1l", [P, L1_COLS], F32R)
        ar = sb("arena_r", [P, ARENA_R], F32R)
        af = sb("arena_f", [P, ARENA_F])
        ctx_raw = sb("ctx_raw", [P, 2, D])
        ident = sb("ident", [P, P])
        ident16 = sb("ident16", [P, P], F16)
        blockmask = sb("blockmask", [P, 2 * VC])
        headmask = sb("headmask", [P, 4])
        iota8 = sb("iota8", [P, EXPERTS])
        rows = sb("rows", [P, 5, D])
        bo_rs = rows[:, 1, :]
        cols = sb("cols", [P, 2 * KC + NFF])
        bkm, bqm = sb("bkm", [P, KC, 2]), sb("bqm", [P, KC, 2])
        rs = sb("rs", [P, 1])
        bg_raw = sb("bg_raw", [1, D])
        bgh, bgl = sb("bgh", [1, D], F32R), sb("bgl", [1, D], F32R)
        one_raw = sb("one_raw", [1, P])
        one_row = sb("one_row", [1, P], F32R)
        mask_i = sb("mask_i", [P, BATCHES], I32)
        lim = sb("lim", [P, BATCHES])
        st = sb("st", [P, 2, 6])
        mv = sb("mv", [P, 2, 2])
        ve = sb("ve", [P, 2])
        rstd = sb("rstd", [P, 2])
        st2 = sb("st2", [P, 2, 6])
        mv2 = sb("mv2", [P, 2, 2])
        ve2 = sb("ve2", [P, 2])
        rstd2 = sb("rstd2", [P, 2])
        mhalf = sb("mhalf", [P, 1])
        eps = sb("eps", [P, 1])
        tiny = sb("tiny", [P, 2, 80])
        tinyi = sb("tinyi", [P, 2, 8], U32)
        PS = ctx.enter_context(nc.psum_tensor("PS", [P, 8, 512], F32))

        def carve(arena, sizes):
            at, parts = 0, []
            for n in sizes:
                parts.append(arena[:, at:at + n])
                at += n
            assert at <= arena.shape[1], at
            return parts

        def ring(ap):
            return ap.rearrange("p (r n) -> p r n", r=2)

        xTh, xTl, aTh, aTl = map(ring, carve(ar, [512] * 4))
        fTh, fTl, cTh, cTl = carve(ar, [1024, 1280, 1280, 512, 512])[1:]
        cTh, cTl = ring(cTh), ring(cTl)
        mX, mD = map(ring, carve(ar, [1024, 4096]))
        (xn,) = map(ring, carve(af, [512]))
        _, ek, rk, eq, rq, kk, qq, thg, ag, vx, smat, az = carve(af, [512] * 9 + [2 * 2 * VC, 4 * 2 * VC, D])
        ek, rk, kk, thg, ag, vx = map(ring, (ek, rk, kk, thg, ag, vx))
        vx = [vx[:, r, :].rearrange("p (c n) -> p c n", c=2) for r in range(2)]
        smat = smat.rearrange("p (r b n) -> p r b n", r=2, b=2)
        _, fth, fa, fh = carve(af, [512, 1280, 1280, 1280])
        _, kb, pp, cn, _, vb, dl, dn = map(ring, carve(af, [512, 1024, 2048, 512, 256, 4 * PAIRS * PVC, 512, 512]))
        assert 512 + 3 * 1280 <= 512 + 1024 + 2048 + 512 + 256
        assert 2 * FFN_CHUNK <= 1024 <= L0_COLS - 1024
        qb = raw[:, 1024:2048]
        qb = qb.rearrange("p (r c b j q) -> p r c b j q", r=2, c=KC, b=2, j=2)
        kb = kb.rearrange("p r (c b h k) -> p r c b h k", c=KC, b=2, h=2)
        vb = [vb[:, r, :].rearrange("p (b g n) -> p b g n", b=2, g=PAIRS) for r in range(2)]
        pp = [pp[:, r, :].rearrange("p (b i n) -> p b i n", b=2, i=2) for r in range(2)]
        mx16 = raw[:, 2048:2304]
        md16, me16, mo = carve(af, [512, 2048, 256, 1024])[1:]
        mx16 = mx16.bitcast(F16).rearrange("p (r n) -> p r n", r=2)
        md16 = md16.bitcast(F16).rearrange("p (r n t) -> p r n t", r=2, n=NFF)
        me16 = me16.bitcast(F16).rearrange("p (k n) -> p k n", k=2)
        mo = mo.rearrange("p (r k n) -> p r k n", r=2, k=2)
        mX = [mX[:, r, :].rearrange("p (c t) -> p c t", c=KC) for r in range(2)]
        mD = [mD[:, r, :].rearrange("p (n t) -> p n t", n=NFF) for r in range(2)]

        def wmat(h, l, at, k, n):
            return [w[:, at:at + k * n].rearrange("p (k n) -> p k n", k=k) for w in (h, l)]

        kvw, qw, gw, ow = (wmat(w0h, w0l, at, KC, n) for at, n in ((L0_KV, 512), (L0_Q, D), (L0_G, D), (L0_O, D)))
        f1w = wmat(wfh, wfl, 0, KC, W1_COLS)
        f2w = wmat(wfh, wfl, KC * W1_COLS, EXPERTS + SH // P, D)
        q1w, k1w, v1w, o1w = (wmat(w1h, w1l, at, KC, D) for at in (L1_Q, L1_K, L1_V, L1_O))
        m0w = wmat(w1h, w1l, L1_W0, KC, FF)
        m1w = wmat(w1h, w1l, L1_W1, NFF, D)

        x_in = [sem("x_in_first"), sem("x_in_rest")]
        ident_in, const_in, late_in = sem("ident_in"), sem("const_in"), sem("late_in")
        w0_in = [sem(f"w0_in{i}") for i in range(3)]
        w0_hi, w0_lo = sem("w0_hi"), sem("w0_lo")
        ctx_in = [sem("ctx_in0"), sem("ctx_in1")]
        w_in = [sem("w_in0"), sem("w_in1")]
        setup_v, setup_p = sem("setup_vector"), sem("setup_pool")
        w_hi, w_lo = sem("weights_hi"), sem("weights_lo")
        ln_stats, ln_aggr, ln_var, ln_rstd = sem("ln_stats"), sem("ln_aggr"), sem("ln_var"), sem("ln_rstd")
        xn_ready, xT_psum, xT_hi, xT_lo = sem("xn_ready"), sem("xT_psum"), sem("xT_hi"), sem("xT_lo")
        ctx_hi, ctx_lo = sem("ctx_hi"), sem("ctx_lo")
        x_done = [sem(f"x_done{i}") for i in range(3)]

        block = ctx.enter_context(nc.Block())

        def product(out_ap, left, right, first=True, last=True):
            (lh, ll), (rh, rl) = left, right
            nc.tensor.matmul(out_ap, lh, rh, start=first, stop=False)
            nc.tensor.matmul(out_ap, lh, rl, start=False, stop=False)
            return nc.tensor.matmul(out_ap, ll, rh, start=False, stop=last)

        def at_tile(t):
            return t % TILES if isinstance(t, int) else t

        def ln_stats_step(dve, stage, t, r):
            base = TILES * stage
            after(dve, ln_var, t, 2, base)
            after(dve, xn_ready, t, 2, base)
            if isinstance(t, int) and t >= TILES:
                dve.wait_ge(x_done[stage], t - TILES + 1)
            nc.vector.bn_stats(st[:, r, :], x[:, at_tile(t), :]).then_inc(ln_stats, 1)

        def ln_aggr_step(dve, stage, t, r):
            after_plain(dve, (x_in[0], 16), ln_stats, t, TILES * stage)
            nc.vector.bn_aggr(mv[:, r, :], st[:, r, :]).then_inc(ln_aggr, 1)

        def ln_rstd_step(pool, stage, t, r):
            base = TILES * stage
            after(pool, ln_aggr, t, 0, base)
            nc.gpsimd.tensor_tensor(ve[:, r:r + 1], mv[:, r, 1:2], eps[:, 0:1], ALU.add).then_inc(ln_var, 1)
            after(pool, ln_var, t, 0, base)
            after(pool, xn_ready, t, 2, base)
            nc.gpsimd.tensor_tensor(rstd[:, r:r + 1], ve[:, r:r + 1], mhalf[:, 0:1], ALU.pow).then_inc(ln_rstd, 1)

        def ln_norm_step(dve, stage, t, r, dst):
            base = TILES * stage
            after(dve, ln_rstd, t, 0, base)
            after(dve, ln_aggr, t, 0, base)
            after(dve, xT_psum, t, 2, base)
            nc.vector.tensor_scalar(dst[:, r, :], x[:, at_tile(t), :], mv[:, r, 0:1], rstd[:, r:r + 1],
                                    ALU.subtract, ALU.mult).then_inc(xn_ready, 1)

        def transpose_x(pe, stage, t, r, bank):
            base = TILES * stage
            after(pe, xn_ready, t, 0, base)
            after(pe, xT_lo, t, 1, base)
            for c in range(KC):
                last = nc.tensor.transpose(PS[:, bank, c * P:(c + 1) * P], xn[:, r, c * P:(c + 1) * P], ident[:, :])
            last.then_inc(xT_psum, 1)

        def xT_hi_step(act, stage, t, r, bank):
            base = TILES * stage
            after(act, xT_psum, t, 0, base)
            after(act, xT_lo, t, 2, base)
            nc.scalar.activation(xTh[:, :, r * P:(r + 1) * P], PS[:, bank, 0:D].rearrange("p (c t) -> p c t", c=KC),
                                 ACT.Copy).then_inc(xT_hi, 1)

        def xT_lo_step(dve, stage, t, r, bank):
            after(dve, xT_hi, t, 0, TILES * stage)
            at = slice(r * P, (r + 1) * P)
            nc.vector.tensor_tensor(xTl[:, :, at], PS[:, bank, 0:D].rearrange("p (c t) -> p c t", c=KC),
                                    xTh[:, :, at].bitcast(F32), ALU.subtract).then_inc(xT_lo, 1)

        def xT(r, c):
            return [w[:, c, r * P:(r + 1) * P] for w in (xTh, xTl)]

        def cT(r, c):
            return [w[:, c, r * P:(r + 1) * P] for w in (cTh, cTl)]

        def scores_bank(r):
            return (X_S, X_Q)[r]

        def pair(parts, c):
            return [w[:, c, :] for w in parts]

        def aT(r, c):
            return [w[:, r, c * P:(c + 1) * P] for w in (aTh, aTl)]

        def in_ring(eng, sems, t, r, before=0):
            eng.wait_ge(sems[r], t * 8 + (16 - 8 * r + 16 * before))

        def ctx_hi_step(act, turn, t, r, used):
            base = TILES * turn
            in_ring(act, ctx_in, t, r, 8 * turn)
            after(act, used, t, 2)
            after(act, ctx_lo, t, 2, base)
            nc.scalar.activation(cTh[:, :, r * P:(r + 1) * P], ctx_raw[:, r, :].rearrange("p (c t) -> p c t", c=KC),
                                 ACT.Copy).then_inc(ctx_hi, 1)

        def ctx_lo_step(pool, turn, t, r, used):
            after(pool, ctx_hi, t, 0, TILES * turn)
            after(pool, used, t, 2)
            at = slice(r * P, (r + 1) * P)
            nc.gpsimd.tensor_tensor(cTl[:, :, at], ctx_raw[:, r, :].rearrange("p (c t) -> p c t", c=KC),
                                    cTh[:, :, at].bitcast(F32), ALU.subtract).then_inc(ctx_lo, 1)

        def weights_hi_step(act, turn, t, r):
            wh, n = ((wfh, FFN_CHUNK), (w1h, L1_CHUNK))[turn]
            in_ring(act, w_in, t, r, 8 * turn)
            nc.scalar.activation(wh[:, bass.ts(t, n)], raw[:, r * FFN_CHUNK:r * FFN_CHUNK + n],
                                 ACT.Copy).then_inc(w_hi, 1)

        def weights_lo_step(pool, turn, t, r):
            wh, wl, n = ((wfh, wfl, FFN_CHUNK), (w1h, w1l, L1_CHUNK))[turn]
            after(pool, w_hi, t, 0, TILES * turn)
            nc.gpsimd.tensor_tensor(wl[:, bass.ts(t, n)], raw[:, r * FFN_CHUNK:r * FFN_CHUNK + n],
                                    wh[:, bass.ts(t, n)].bitcast(F32), ALU.subtract).then_inc(w_lo, 1)

        def ahead_of(s):
            return None if s.is_at(0) else s.next(1)

        def normalised_in(s):
            return None if s.is_at(0) else s.next(2, over=2 * PER_GROUP)

        S0 = {n: sem("s0_" + n) for n in (
            "kv_psum", "q_psum", "g_psum", "k_exp", "k_relu", "v_ready", "q_exp", "q_relu", "gate_tanh", "k_ready", "q_ready",
            "ktv_psum", "s_ready", "attn_psum", "den", "z", "az", "ag_ready", "agT_psum", "agT_hi", "agT_lo",
            "o_psum")}
        S1 = {n: sem("s1_" + n) for n in (
            "router_psum", "scores", "top", "index", "gap", "gap_exp", "denom", "weights", "w2", "indexf", "pick1",
            "pick2", "comb", "g_psum", "u_psum", "tanh", "a", "h", "hT_psum", "hT_hi", "hT_lo", "down")}
        S2 = {n: sem("s2_" + n) for n in (
            "q_psum", "k_psum", "v_psum", "q_ready", "kb_ready", "vb_ready", "scores_psum", "clipped", "probs", "pv_psum",
            "guard", "den", "rden", "cn_ready", "cnT_psum", "cnT_hi", "cnT_lo", "o_psum", "delta", "d_stats",
            "d_aggr", "d_var", "d_rstd", "dn", "scaled", "shifted")}
        S3 = {n: sem("s3_" + n) for n in (
            "x_ready", "h_psum", "gelu", "d_ready", "o_psum", "e16", "o_ready")}
        stored = [sem("stored0"), sem("stored1")]

        @block.sync
        def _(sp):
            def load(dst, src, s):
                sp.dma_start(dst, src).then_inc(s, 16)

            x_d = A["x"].rearrange("(t p) d -> p t d", p=P)
            load(x[:, 0:2, :], x_d[:, 0:2, :], x_in[0])
            load(ctx_raw[:, 0, :], A["ctxT"][0], ctx_in[0])
            load(ident[:, :], A["ident"], ident_in)
            load(raw[:, 0:L0_Q], A["w_l0"][:, 0:L0_Q], w0_in[0])
            load(raw[:, L0_Q:L0_O], A["w_l0"][:, L0_Q:L0_O], w0_in[1])
            load(ctx_raw[:, 1, :], A["ctxT"][1], ctx_in[1])
            load(raw[:, L0_O:], A["w_l0"][:, L0_O:], w0_in[2])
            load(bg_raw[:, :], A["bg"], const_in)
            load(blockmask[:, :], A["blockmask"], const_in)
            load(x[:, 2:TILES, :], x_d[:, 2:TILES, :], x_in[1])
            for dst, name in ((headmask, "headmask"), (iota8, "iota8"), (cols, "cols"), (rs, "rs"), (mask_i, "mask")):
                load(dst[:, :], A[name], late_in)
            load(rows[:, :, :], A["rows"], late_in)

            def load_ctx(turn, t, r):
                after(sp, ctx_lo, t, 2, TILES * turn)
                load(ctx_raw[:, r, :], A["ctxT"][t], ctx_in[r])

            def load_w(turn, t, r):
                src, n = ((A["w_ffn"], FFN_CHUNK), (A["w_l1"], L1_CHUNK))[turn]
                after(sp, w_lo, t, 2, TILES * turn)
                load(raw[:, r * FFN_CHUNK:r * FFN_CHUNK + n], src[t], w_in[r])

            for t in range(2, 4):
                load_ctx(0, t, t - 2)
            sp.wait_ge(w0_lo, 3)
            for t in range(2):
                load_w(0, t, t)
            with sp.Fori(1, TILES // 2 - 1) as i:
                for r in range(2):
                    load_ctx(0, i * 2 + (2 + r), r)
                    load_w(0, i * 2 + r, r)
            for r in range(2):
                load_w(0, TILES - 2 + r, r)
            for t in range(2):
                load_ctx(1, t, t)
            for t in range(2):
                load_w(1, t, t)
            with sp.Fori(1, TILES // 2) as i:
                for r in range(2):
                    load_w(1, i * 2 + r, r)
            with sp.Fori(1, TILES // 2) as i:
                for r in range(2):
                    load_ctx(1, i * 2 + r, r)

            out_d = out.rearrange("(g k p) d -> g p k d", p=P, k=2)
            with sp.Fori(0, GROUPS // 2) as i:
                for r in range(2):
                    sp.wait_ge(S3["o_ready"], i * 2 + (r + 1))
                    load(out_d[i * 2 + r], mo[:, r, :, :], stored[r])
            for r in range(2):
                sp.wait_ge(stored[r], 16 * GROUPS // 2)

        @block.gpsimd
        def _(pool):
            nc.gpsimd.memset(mhalf[:, :], -0.5).then_inc(setup_p, 1)
            nc.gpsimd.memset(eps[:, :], 1e-5).then_inc(setup_p, 1)
            nc.gpsimd.memset(one_raw[:, :], 1.0).then_inc(setup_p, 1)
            for r in range(2):
                nc.gpsimd.memset(vx[r][:, :, P:VC], 1.0).then_inc(setup_p, 1)

            def slot0(s):
                if tile := s.next(2):
                    ln_rstd_step(pool, 0, *tile)
                if tile := s.tile(2):
                    ctx_lo_step(pool, 0, *tile, S0["kv_psum"])
                if tile := s.tile(0):
                    weights_lo_step(pool, 0, *tile)

            pool.wait_ge(setup_p, 5)
            for t in range(2):
                ln_rstd_step(pool, 0, t, t)
            for t in range(2):
                ctx_lo_step(pool, 0, t, t, S0["kv_psum"])
            slots(pool, TILES, 0, TILES - 1, slot0)

            def values_setup():
                pool.wait_ge(x_done[0], TILES)
                for r in range(2):
                    nc.gpsimd.memset(vb[r][:, :, :, :], 0.0).then_inc(setup_p, 1)
                pool.wait_ge(setup_p, 7)
                for r in range(2):
                    for h in range(2):
                        nc.gpsimd.memset(vb[r][SEQ * h:SEQ * (h + 1), :, :, 2 * HD + h:2 * HD + h + 1],
                                         1.0).then_inc(setup_p, 1)
                pool.wait_ge(setup_p, 11)

            def slot1(s):
                ln_rstd_step(pool, 1, *s.next(2, over=3))
                if tile := s.tile(0):
                    weights_lo_step(pool, 1, *tile)
                if s.is_at(0):
                    values_setup()
                for t in range(2):
                    if s.is_at(TILES - 2 + t):
                        ctx_lo_step(pool, 1, t, t, S2["v_psum"])

            slots(pool, TILES, 0, TILES, slot1, low=2)

            def slot2(s):
                if tile := normalised_in(s):
                    ln_rstd_step(pool, 2, *tile)
                if tile := s.tile(2):
                    ctx_lo_step(pool, 1, *tile, S2["v_psum"])
                if tile := s.tile(-3):
                    t, r = tile
                    after(pool, S2["dn"], t)
                    nc.gpsimd.tensor_tensor(dn[:, r, :], dn[:, r, :], rows[:, 2, :], ALU.mult).then_inc(S2["scaled"], 1)
                    after(pool, S2["scaled"], t)
                    nc.gpsimd.tensor_tensor(dn[:, r, :], dn[:, r, :], rows[:, 3, :], ALU.add).then_inc(S2["shifted"], 1)
                    after(pool, S2["shifted"], t)
                    nc.gpsimd.tensor_tensor(x[:, t, :], x[:, t, :], dn[:, r, :], ALU.add).then_inc(x_done[2], 1)
                if tile := s.tile(-2):
                    t, r = tile
                    after(pool, S2["d_aggr"], t)
                    nc.gpsimd.tensor_tensor(ve2[:, r:r + 1], mv2[:, r, 1:2], eps[:, 0:1], ALU.add).then_inc(S2["d_var"], 1)
                    after(pool, S2["d_var"], t)
                    after(pool, S2["dn"], t, 2)
                    nc.gpsimd.tensor_tensor(rstd2[:, r:r + 1], ve2[:, r:r + 1], mhalf[:, 0:1],
                                            ALU.pow).then_inc(S2["d_rstd"], 1)

            slots(pool, TILES, 0, TILES + 2, slot2, low=6)

            def slot3(s):
                if tile := s.tile(2):
                    for k in range(2):
                        ln_rstd_step(pool, 3, tile[0] * 2 + k, k)

            slots(pool, GROUPS, 0, GROUPS - 3, slot3, low=2)

        @block.scalar
        def _(act):
            def split_hi(i, a, b):
                act.wait_ge(w0_in[i], 16)
                nc.scalar.activation(w0h[:, a:b], raw[:, a:b], ACT.Copy).then_inc(w0_hi, 1)

            ctx_hi_step(act, 0, 0, 0, S0["kv_psum"])
            split_hi(0, L0_KV, L0_Q)
            xT_hi_step(act, 0, 0, 0, B_T)
            split_hi(1, L0_Q, L0_O)
            ctx_hi_step(act, 0, 1, 1, S0["kv_psum"])
            xT_hi_step(act, 0, 1, 1, B_T)
            split_hi(2, L0_O, L0_COLS)

            def slot0(s):
                if tile := s.tile(0):
                    t, r = tile
                    after(act, S0["kv_psum"], t)
                    after(act, S0["k_ready"], t, 2)
                    nc.scalar.activation(ek[:, r, :], PS[:, B_KV, 0:D], ACT.Exp).then_inc(S0["k_exp"], 1)
                    nc.scalar.activation(rk[:, r, :], PS[:, B_KV, 0:D], ACT.Relu).then_inc(S0["k_relu"], 1)
                    after(act, S0["ktv_psum"], t, 2)
                    act.wait_ge(setup_p, 5)
                    nc.scalar.activation(vx[r][:, :, 0:P], PS[:, B_KV, D:2 * D].rearrange("p (c n) -> p c n", c=2),
                                         ACT.Copy).then_inc(S0["v_ready"], 1)
                if tile := s.tile(2):
                    ctx_hi_step(act, 0, *tile, S0["kv_psum"])
                if s.ring == 0 and s.tile(0):
                    after(act, S0["q_psum"], s.pair)
                    after(act, S0["q_ready"], s.pair, 1)
                    nc.scalar.activation(eq, PS[:, B_Q, :], ACT.Exp).then_inc(S0["q_exp"], 1)
                    nc.scalar.activation(rq, PS[:, B_Q, :], ACT.Relu).then_inc(S0["q_relu"], 1)
                if tile := s.tile(0):
                    t, r = tile
                    after(act, S0["g_psum"], t)
                    after(act, S0["ag_ready"], t, 2)
                    nc.scalar.activation(thg[:, r, :], PS[:, B_GO, 0:D], ACT.Tanh,
                                         scale=0.5).then_inc(S0["gate_tanh"], 1)
                if tile := s.next(2):
                    after(act, S0["g_psum"], tile[0], 2)
                    xT_hi_step(act, 0, *tile, B_T)
                if tile := s.tile(0):
                    weights_hi_step(act, 0, *tile)
                if tile := s.tile(-1):
                    t, r = tile
                    after(act, S0["agT_psum"], t)
                    after(act, S0["o_psum"], t, 2)
                    after(act, S0["agT_lo"], t, 2)
                    nc.scalar.activation(aTh[:, r, :], PS[:, B_TA, 0:D], ACT.Copy).then_inc(S0["agT_hi"], 1)

            slots(act, TILES, 0, TILES, slot0)

            down = S1["down"]

            def hidden_hi(t, group, at, bank):
                after(act, S1["hT_psum"], t, per=3, extra=group - 2)
                after(act, down, t, 1, per=3, extra=group - 2)
                nc.scalar.activation(fTh[:, at], PS[:, bank, 0:at.stop - at.start], ACT.Copy).then_inc(S1["hT_hi"], 1)

            def gate_tanh(t, group, at, bank):
                after(act, S1["g_psum"], t, per=3, extra=group - 2)
                after(act, S1["a"], t, 1, per=3, extra=group - 2)
                nc.scalar.activation(fth[:, at], PS[:, bank, 0:at.stop - at.start], ACT.Tanh,
                                     scale=0.5).then_inc(S1["tanh"], 1)

            def slot1(s):
                here, before, ahead = s.tile(0), s.tile(-1), ahead_of(s)
                if before:
                    hidden_hi(before[0], 1, GROUP_B, F_H + 1)
                if here:
                    t, r = here
                    after(act, S1["gap"], t)
                    after(act, S1["w2"], t, 2)
                    nc.scalar.activation(tiny[:, r, 34:36], tiny[:, r, 32:34], ACT.Exp).then_inc(S1["gap_exp"], 1)
                    gate_tanh(t, 0, GROUP_A, F_G0)
                if before:
                    hidden_hi(before[0], 2, GROUP_C, F_H)
                if ahead:
                    after(act, S1["g_psum"], ahead[0], 2, per=3)
                    xT_hi_step(act, 1, *ahead, F_T)
                if here:
                    weights_hi_step(act, 1, t, r)
                    gate_tanh(t, 1, GROUP_B, F_G1)
                    hidden_hi(t, 0, GROUP_A, F_H)
                    gate_tanh(t, 2, GROUP_C, F_G0)
                for t in range(2):
                    if s.is_at(TILES - 2 + t):
                        ctx_hi_step(act, 1, t, t, S2["v_psum"])

            slots(act, TILES, 0, TILES, slot1, low=2)

            act.wait_ge(setup_v, 6)

            def ffn_gelu(g, r, features):
                for n in features:
                    if n % 2 == 0:
                        after(act, S3["h_psum"], g, per=4, extra=n // 2 - 3)
                        after(act, S3["d_ready"], g, 2, per=4, extra=n // 2 - 3)
                    nc.scalar.activation(md16[:, r, n, :], PS[:, M_H + n // 2, (n % 2) * D:(n % 2 + 1) * D],
                                         ACT.Gelu, bias=cols[:, 2 * KC + n:2 * KC + n + 1]).then_inc(S3["gelu"], 1)

            def halves_up(g):
                r = g[1]
                after(act, xT_psum, g[0], per=2, base=3 * TILES)
                after(act, S3["h_psum"], g[0], 2, per=4)
                for k in range(2):
                    src = PS[:, M_T, k * P:(k + 1) * P].bitcast(F16).rearrange("p (c t) -> p c t", c=KC)
                    nc.scalar.activation(mX[r][:, :, k * P:(k + 1) * P], src, ACT.Copy).then_inc(S3["x_ready"], 1)

            def exp_scores(t, r):
                after(act, S2["clipped"], t, per=2)
                flat = pp[r].rearrange("p b i n -> p (b i n)")
                nc.scalar.activation(flat, flat, ACT.Exp).then_inc(S2["probs"], 1)

            def slot2(s):
                if s.ring == 0 and s.tile(0):
                    after(act, S2["k_psum"], s.pair)
                    after(act, S2["scores_psum"], s.at, 1)
                    for c in range(KC):
                        for h in range(2):
                            nc.scalar.activation(
                                kb[:, :, c, :, h, :],
                                PS[:, X_K, c * 2 * P:(c + 1) * 2 * P].rearrange("p (r b k) -> p r b k", r=2, b=2),
                                ACT.Identity, bias=bkm[:, c, h:h + 1], scale=headmask[:, h:h + 1],
                            ).then_inc(S2["kb_ready"], 1)
                if tile := s.tile(-2):
                    t, r = tile
                    after(act, S2["cnT_psum"], t)
                    after(act, S2["o_psum"], t, 2)
                    after(act, S2["cnT_lo"], t, 2)
                    nc.scalar.activation(aTh[:, r, :], PS[:, X_T, D:2 * D], ACT.Copy).then_inc(S2["cnT_hi"], 1)
                if s.ring == 1 and s.tile(-1):
                    exp_scores(*s.tile(-1))
                if s.ring == 0 and s.tile(0):
                    after(act, S2["q_psum"], s.pair)
                    after(act, S2["scores_psum"], s.at, 1)
                    for c in range(KC):
                        for j in range(2):
                            nc.scalar.activation(
                                qb[:, :, c, :, j, :],
                                PS[:, X_Q, c * 2 * P:(c + 1) * 2 * P].rearrange("p (r b q) -> p r b q", r=2, b=2),
                                ACT.Identity, bias=bqm[:, c, j:j + 1], scale=headmask[:, 2 + j:3 + j],
                            ).then_inc(S2["q_ready"], 1)
                if tile := s.tile(2):
                    ctx_hi_step(act, 1, *tile, S2["v_psum"])
                    after(act, S2["q_psum"], s.pair)
                    xT_hi_step(act, 2, *tile, X_T)
                if s.is_at(TILES - 1):
                    halves_up((0, 0))
                if s.ring == 1 and s.tile(0):
                    exp_scores(*s.tile(0))
                if s.is_at(TILES):
                    ffn_gelu(0, 0, EARLY)

            slots(act, TILES, 0, TILES + 1, slot2)

            def slot3(s):
                if tile := s.tile(0):
                    ffn_gelu(*tile, LATE if s.is_at(0) else range(NFF))
                if tile := s.tile(1):
                    halves_up(tile)

            slots(act, GROUPS, 0, GROUPS - 1, slot3, low=2)

        @block.vector
        def _(dve):
            def split_w0(i, a, b):
                dve.wait_ge(w0_hi, i + 1)
                nc.vector.tensor_tensor(w0l[:, a:b], raw[:, a:b], w0h[:, a:b].bitcast(F32),
                                        ALU.subtract).then_inc(w0_lo, 1)

            def setup():
                dve.wait_ge(const_in, 16 * 2)
                dve.wait_ge(setup_p, 3)
                nc.vector.tensor_copy(bgh[:, :], bg_raw[:, :]).then_inc(setup_v, 1)
                nc.vector.tensor_copy(one_row[:, :], one_raw[:, :])
                dve.wait_ge(setup_v, 1)
                nc.vector.tensor_tensor(bgl[:, :], bg_raw[:, :], bgh[:, :].bitcast(F32),
                                        ALU.subtract).then_inc(setup_v, 1)

            def setup_late():
                dve.wait_ge(late_in, 16 * 6)
                dve.wait_ge(ident_in, 16)
                nc.vector.tensor_copy(ident16[:, :], ident[:, :]).then_inc(setup_v, 1)
                for c in range(KC):
                    nc.vector.tensor_scalar(bqm[:, c, :], headmask[:, 2:4], cols[:, c:c + 1], None, ALU.mult)
                    nc.vector.tensor_scalar(bkm[:, c, :], headmask[:, 0:2], cols[:, KC + c:KC + c + 1], None, ALU.mult)
                nc.vector.tensor_scalar(rs[:, :], rs[:, :], 0.0, 0.3, ALU.max, ALU.min).then_inc(setup_v, 1)
                nc.vector.tensor_scalar(lim[:, :], mask_i[:, :], 0.5, 100.0, ALU.is_gt, ALU.mult).then_inc(setup_v, 1)
                dve.wait_ge(setup_v, 5)
                nc.vector.tensor_scalar(rows[:, 1, :], rows[:, 1, :], rs[:, 0:1], None, ALU.mult)
                nc.vector.tensor_scalar(lim[:, :], lim[:, :], -50.0, None, ALU.add).then_inc(setup_v, 1)

            dve.wait_ge(x_in[0], 16)
            for t in range(2):
                ln_stats_step(dve, 0, t, t)
                ln_aggr_step(dve, 0, t, t)
            for t in range(2):
                ln_norm_step(dve, 0, t, t, xn)
            split_w0(0, L0_KV, L0_Q)
            xT_lo_step(dve, 0, 0, 0, B_T)
            split_w0(1, L0_Q, L0_O)
            xT_lo_step(dve, 0, 1, 1, B_T)
            setup()
            split_w0(2, L0_O, L0_COLS)

            def slot0(s):
                if tile := s.next(2):
                    t, r = tile
                    if s.is_at(0):
                        dve.wait_ge(x_in[1], 16)
                    ln_stats_step(dve, 0, t, r)
                    ln_aggr_step(dve, 0, t, r)
                if tile := s.tile(0):
                    t, r = tile
                    after(dve, S0["k_exp"], t)
                    after(dve, S0["k_relu"], t)
                    after(dve, S0["ktv_psum"], t, 2)
                    nc.vector.scalar_tensor_tensor(out=kk[:, r, :], in0=ek[:, r, :], scalar=1.0, in1=rk[:, r, :],
                                                   op0=ALU.min, op1=ALU.add).then_inc(S0["k_ready"], 1)
                if tile := s.next(2):
                    ln_norm_step(dve, 0, *tile, xn)
                if tile := s.tile(-1):
                    t, r = tile
                    at = PS[:, B_A, 0:2 * VC].rearrange("p (c n) -> p c n", c=2)
                    den, hz = (tiny[:, r, a:a + HEADS].rearrange("p (c h) -> p c h", c=2) for a in (0, HEADS))
                    after(dve, S0["attn_psum"], t)
                    nc.vector.tensor_scalar(den, at[:, :, P:VC], 1e-6, 2.0, ALU.add, ALU.mult).then_inc(S0["den"], 1)
                    after(dve, S0["den"], t)
                    nc.vector.reciprocal(hz, den).then_inc(S0["z"], 1)
                    after(dve, S0["z"], t)
                    nc.vector.tensor_tensor(
                        az.rearrange("p (c h e) -> p c h e", c=2, h=HPC),
                        at[:, :, 0:P].rearrange("p c (h e) -> p c h e", h=HPC),
                        hz.unsqueeze(3).to_broadcast([P, 2, HPC, HD]), ALU.mult).then_inc(S0["az"], 1)
                    after(dve, S0["az"], t)
                    after(dve, S0["gate_tanh"], t)
                    after(dve, S0["agT_psum"], t, 2)
                    nc.vector.scalar_tensor_tensor(out=ag[:, r, :], in0=thg[:, r, :], scalar=1.0, in1=az,
                                                   op0=ALU.add, op1=ALU.mult).then_inc(S0["ag_ready"], 1)
                if s.ring == 0 and s.tile(0):
                    after(dve, S0["q_exp"], s.pair)
                    after(dve, S0["q_relu"], s.pair)
                    after(dve, S0["attn_psum"], s.at, 1)
                    nc.vector.scalar_tensor_tensor(out=qq, in0=eq, scalar=1.0, in1=rq,
                                                   op0=ALU.min, op1=ALU.add).then_inc(S0["q_ready"], 1)
                if tile := s.tile(0):
                    t, r = tile
                    after(dve, S0["ktv_psum"], t)
                    after(dve, S0["attn_psum"], t, 2)
                    for b in range(2):
                        last = nc.vector.tensor_tensor(smat[:, r, b, :], PS[:, B_S + b, 0:2 * VC], blockmask[:, :],
                                                       ALU.mult)
                    last.then_inc(S0["s_ready"], 1)
                if tile := s.tile(-2):
                    t, r = tile
                    after(dve, S0["o_psum"], t)
                    nc.vector.tensor_tensor(x[:, t, :], PS[:, B_GO, D:2 * D], x[:, t, :], ALU.add).then_inc(x_done[0], 1)
                if tile := s.next(2):
                    xT_lo_step(dve, 0, *tile, B_T)
                if tile := s.tile(-1):
                    t, r = tile
                    after(dve, S0["agT_hi"], t)
                    after(dve, S0["o_psum"], t, 2)
                    nc.vector.tensor_tensor(aTl[:, r, :], PS[:, B_TA, 0:D], aTh[:, r, :].bitcast(F32),
                                            ALU.subtract).then_inc(S0["agT_lo"], 1)
                if s.is_at(2):
                    setup_late()

            slots(dve, TILES, 0, TILES + 1, slot0)

            def router(t, r):
                sc, mx8, gap, e2, w3, c1, c2, comb, dn2, ixf = (
                    tiny[:, r, a:a + n] for a, n in (
                        (0, 10), (16, 8), (32, 2), (34, 2), (36, 3), (40, 8), (48, 8), (56, 8), (64, 2), (66, 2)))
                ix = tinyi[:, r, :]
                after(dve, S1["router_psum"], t)
                nc.vector.tensor_copy(sc, PS[:, F_T, D:D + 10]).then_inc(S1["scores"], 1)
                after_plain(dve, (late_in, 16 * 6), S1["scores"], t)
                nc.vector.max(mx8, sc[:, 0:8]).then_inc(S1["top"], 1)
                nc.vector.tensor_scalar(gap[:, 1:2], sc[:, 8:9], -1.0, None, ALU.mult)
                after(dve, S1["top"], t)
                nc.vector.tensor_tensor(gap[:, 0:1], mx8[:, 1:2], mx8[:, 0:1], ALU.subtract).then_inc(S1["gap"], 1)
                nc.vector.max_index(ix, mx8, sc[:, 0:8]).then_inc(S1["index"], 1)
                after(dve, S1["index"], t)
                nc.vector.tensor_copy(ixf, ix[:, 0:2]).then_inc(S1["indexf"], 1)
                after(dve, S1["gap_exp"], t)
                nc.vector.tensor_scalar(dn2, e2, 2.0, 2.0, ALU.mult, ALU.add).then_inc(S1["denom"], 1)
                after(dve, S1["denom"], t)
                nc.vector.reciprocal(w3[:, 0:2], dn2).then_inc(S1["weights"], 1)
                after(dve, S1["weights"], t)
                nc.vector.tensor_tensor(w3[:, 2:3], w3[:, 0:1], e2[:, 0:1], ALU.mult).then_inc(S1["w2"], 1)
                after(dve, S1["indexf"], t)
                nc.vector.tensor_scalar(c1, iota8[:, :], ixf[:, 0:1], w3[:, 0:1], ALU.is_equal,
                                        ALU.mult).then_inc(S1["pick1"], 1)
                after(dve, S1["w2"], t)
                nc.vector.tensor_scalar(c2, iota8[:, :], ixf[:, 1:2], w3[:, 2:3], ALU.is_equal,
                                        ALU.mult).then_inc(S1["pick2"], 1)
                after(dve, S1["pick1"], t)
                after(dve, S1["pick2"], t)
                nc.vector.tensor_tensor(comb, c1, c2, ALU.add).then_inc(S1["comb"], 1)
                return comb, w3[:, 1:2]

            def hidden_lo(t, group, at, bank):
                after(dve, S1["hT_hi"], t, per=3, extra=group - 2)
                nc.vector.tensor_tensor(fTl[:, at], PS[:, bank, 0:at.stop - at.start], fTh[:, at].bitcast(F32),
                                        ALU.subtract).then_inc(S1["hT_lo"], 1)

            def gate_factor(t, group, at, bank):
                after(dve, S1["tanh"], t, per=3, extra=group - 2)
                nc.vector.scalar_tensor_tensor(out=fa[:, at], in0=fth[:, at], scalar=1.0,
                                               in1=PS[:, bank, 0:at.stop - at.start],
                                               op0=ALU.add, op1=ALU.mult).then_inc(S1["a"], 1)

            def hidden(t, group, parts, bank, first):
                after(dve, S1["a"], t, per=3, extra=group - 2)
                after(dve, S1["comb"], t)
                if group < 2:
                    after(dve, S1["u_psum"], t, per=2, extra=group - 1)
                after(dve, S1["hT_psum"], t, 1, per=3, extra=group - 2)
                for c, weight in parts:
                    u = first + c.start - parts[0][0].start
                    last = nc.vector.scalar_tensor_tensor(
                        out=fh[:, c], in0=fa[:, c], scalar=weight, in1=PS[:, bank, u:u + c.stop - c.start],
                        op0=ALU.mult, op1=ALU.mult)
                last.then_inc(S1["h"], 1)

            def slot1(s):
                here, before, ahead = s.tile(0), s.tile(-1), ahead_of(s)
                if before:
                    hidden_lo(before[0], 1, GROUP_B, F_H + 1)
                if here:
                    t, r = here
                    comb, shared_gate = router(t, r)
                    experts = [(slice(EH * e, EH * (e + 1)), comb[:, e:e + 1]) for e in range(EXPERTS)]
                if here:
                    gate_factor(t, 0, GROUP_A, F_G0)
                    ln_stats_step(dve, 1, *s.next(2))
                    hidden(t, 0, experts[:4], F_U0, 0)
                    ln_aggr_step(dve, 1, *s.next(2))
                if before:
                    hidden_lo(before[0], 2, GROUP_C, F_H)
                if ahead:
                    xT_lo_step(dve, 1, *ahead, F_T)
                if s.is_at(TILES):
                    for step in (ln_stats_step, ln_aggr_step):
                        step(dve, 1, *s.next(2, over=3))
                    ln_norm_step(dve, 1, *s.next(2, over=3), xn)
                if here:
                    ln_norm_step(dve, 1, *s.next(2), xn)
                    gate_factor(t, 1, GROUP_B, F_G1)
                if before:
                    after(dve, S1["down"], before[0], per=3)
                    nc.vector.tensor_tensor(x[:, before[0], :], PS[:, F_O, 0:D], x[:, before[0], :],
                                            ALU.add).then_inc(x_done[1], 1)
                if here:
                    hidden_lo(t, 0, GROUP_A, F_H)
                    hidden(t, 1, experts[4:], F_U1, 0)
                    gate_factor(t, 2, GROUP_C, F_G0)
                    hidden(t, 2, [(GROUP_C, shared_gate)], F_G0, SH)

            slots(dve, TILES, 0, TILES, slot1, low=2)

            def values(t, r):
                after(dve, S2["v_psum"], t)
                after(dve, S2["pv_psum"], t, 2)
                dve.wait_ge(setup_p, 11)

                def heads(ap, b, h):
                    return ap[SEQ * b:SEQ * (b + 1)].rearrange("p (g h e) -> p g h e", g=PAIRS, h=2)[:, :, h, :]

                for b in range(2):
                    for h in range(2):
                        last = nc.vector.tensor_tensor(
                            vb[r][SEQ * h:SEQ * (h + 1), b, :, HD * h:HD * (h + 1)],
                            heads(PS[:, X_V, 0:D], b, h), heads(rows[:, 0, :], b, h), ALU.add)
                last.then_inc(S2["vb_ready"], 1)

            def delta(t, r):
                after(dve, S2["o_psum"], t)
                after(dve, S2["dn"], t, 2)
                nc.vector.scalar_tensor_tensor(out=dl[:, r, :], in0=PS[:, X_O, 0:D], scalar=rs[:, 0:1],
                                               in1=bo_rs, op0=ALU.mult, op1=ALU.add).then_inc(S2["delta"], 1)
                after(dve, S2["delta"], t)
                after(dve, S2["d_var"], t, 2)
                nc.vector.bn_stats(st2[:, r, :], dl[:, r, :]).then_inc(S2["d_stats"], 1)

            def delta_aggr(t, r):
                after_plain(dve, (x_in[0], 16), S2["d_stats"], t)
                nc.vector.bn_aggr(mv2[:, r, :], st2[:, r, :]).then_inc(S2["d_aggr"], 1)

            def delta_norm(t, r):
                after(dve, S2["d_rstd"], t)
                after(dve, x_done[2], t, 2)
                nc.vector.tensor_scalar(dn[:, r, :], dl[:, r, :], mv2[:, r, 0:1], rstd2[:, r:r + 1],
                                        ALU.subtract, ALU.mult).then_inc(S2["dn"], 1)

            cx = PS[:, X_C, 0:PAIRS * PVC].rearrange("p (g n) -> p g n", g=PAIRS)
            sums = cx[:, :, 2 * HD:PVC]

            def sums_place(r, i):
                return tiny[:, r, i * HEADS:(i + 1) * HEADS].rearrange("p (g h) -> p g h", h=2)

            def sums_guard(t, r):
                after(dve, S2["pv_psum"], t)
                nc.vector.tensor_scalar(sums_place(r, 0), sums, 1e-8, None, ALU.mult).then_inc(S2["guard"], 1)

            def sums_guarded(t, r):
                after(dve, S2["guard"], t)
                nc.vector.tensor_tensor(sums_place(r, 1), sums, sums_place(r, 0), ALU.add).then_inc(S2["den"], 1)

            def sums_inverse(t, r):
                after(dve, S2["den"], t)
                nc.vector.reciprocal(sums_place(r, 2), sums_place(r, 1)).then_inc(S2["rden"], 1)

            def normalise(t, r):
                after(dve, S2["rden"], t)
                after(dve, S2["cnT_psum"], t, 2)
                nc.vector.tensor_tensor(
                    cn[:, r, :].rearrange("p (g h e) -> p g h e", g=PAIRS, h=2),
                    cx[:, :, 0:2 * HD].rearrange("p g (h e) -> p g h e", h=2),
                    sums_place(r, 2).unsqueeze(3).to_broadcast([P, PAIRS, 2, HD]), ALU.mult).then_inc(S2["cn_ready"], 1)

            def clip(t, r):
                after(dve, S2["scores_psum"], t)
                after(dve, S2["pv_psum"], t, 2)
                for b in range(2):
                    bank = scores_bank(r)
                    nc.vector.tensor_scalar(pp[r][:, b, :, :], PS[:, bank:bank + 2, b * 2 * P:(b + 1) * 2 * P], -50.0,
                                            lim[:, bass.ds(t * 2 + b, 1)], ALU.max, ALU.min).then_inc(S2["clipped"], 1)

            def slot2(s):
                even, odd = s.ring == 0, s.ring == 1
                here, before, leaving, ahead = s.tile(0), s.tile(-1), s.tile(-2), normalised_in(s)
                if ahead:
                    ln_stats_step(dve, 2, *ahead)
                if odd and before:
                    clip(*before)
                if ahead:
                    ln_aggr_step(dve, 2, *ahead)
                if leaving:
                    t, r = leaving
                    after(dve, S2["cnT_hi"], t)
                    after(dve, S2["o_psum"], t, 2)
                    nc.vector.tensor_tensor(aTl[:, r, :], PS[:, X_T, D:2 * D], aTh[:, r, :].bitcast(F32),
                                            ALU.subtract).then_inc(S2["cnT_lo"], 1)
                if here:
                    values(*here)
                if ahead:
                    ln_norm_step(dve, 2, *ahead, xn if s.tile(2) else mx16)
                if tile := s.tile(-3):
                    delta_norm(*tile)
                if odd and here:
                    clip(*here)
                if even and before:
                    sums_guard(*before)
                    sums_guarded(*before)
                    sums_inverse(*before)
                    normalise(*before)
                if leaving:
                    delta(*leaving)
                if s.tile(2):
                    xT_lo_step(dve, 2, *s.tile(2), X_T)
                if odd and before:
                    sums_guard(*before)
                if leaving:
                    delta_aggr(*leaving)
                if odd and before:
                    sums_guarded(*before)
                    sums_inverse(*before)
                    normalise(*before)

            slots(dve, TILES, 0, TILES + 2, slot2, low=6)

            def slot3(s):
                if tile := s.tile(0):
                    g, r = tile
                    for i in range(4):
                        after(dve, S3["gelu"], g, per=8, extra=2 * i - 6)
                        after(dve, S3["o_psum"], g, 2)
                        nc.vector.tensor_copy(mD[r][:, 2 * i:2 * i + 2, :],
                                              md16[:, r, 2 * i:2 * i + 2, :]).then_inc(S3["d_ready"], 1)
                if s.is_at(0):
                    dve.wait_ge(x_done[2], 3 * PER_GROUP)
                if s.is_at(1):
                    dve.wait_ge(x_done[2], TILES)
                if tile := s.tile(2):
                    for step in (ln_stats_step, ln_aggr_step):
                        for k in range(2):
                            step(dve, 3, tile[0] * 2 + k, k)
                    for k in range(2):
                        ln_norm_step(dve, 3, tile[0] * 2 + k, k, mx16)
                if tile := s.tile(-1):
                    g, r = tile
                    after(dve, S3["o_psum"], g)
                    after(dve, S3["o_ready"], g, 1)
                    nc.vector.tensor_tensor(me16, PS[:, M_O, :].rearrange("p (k n) -> p k n", k=2),
                                            rows[:, 4, :].unsqueeze(1).to_broadcast([P, 2, D]),
                                            ALU.add).then_inc(S3["e16"], 1)
                    after(dve, S3["e16"], g)
                    if not (isinstance(g, int) and g < 2):
                        dve.wait_ge(stored[r], g * 8 + (-8 * r))
                    nc.vector.tensor_tensor(mo[:, r, :, :], x[:, bass.ds(g * 2, 2), :], me16,
                                            ALU.add).then_inc(S3["o_ready"], 1)

            slots(dve, GROUPS, 0, GROUPS, slot3)

        @block.tensor
        def _(pe):
            pe.wait_ge(ident_in, 16)

            R0 = 2 * EXPERTS * EH + 2 * SH

            def expert_in(t, r, bank, at):
                for c in range(KC):
                    last = product(PS[:, bank, :], xT(r, c), [w[:, c, at:at + 512] for w in f1w], c == 0, c == KC - 1)
                return last

            def route(t, r):
                after(pe, xT_lo, t, base=TILES)
                if isinstance(t, int) and t == 0:
                    pe.wait_ge(xT_lo, TILES + 2)
                for c in range(KC):
                    last = product(PS[:, F_T, D:D + 10], xT(r, c), [w[:, c, R0:R0 + 10] for w in f1w], c == 0,
                                   c == KC - 1)
                last.then_inc(S1["router_psum"], 1)

            def first_experts(t, r):
                after(pe, S1["h"], t, 1, per=3)
                expert_in(t, r, F_G0, 0).then_inc(S1["g_psum"], 1)
                expert_in(t, r, F_U0, 512).then_inc(S1["u_psum"], 1)

            def slot0(s):
                if tile := s.tile(0):
                    t, r = tile
                    after(pe, ctx_lo, t)
                    after(pe, ctx_hi, t)
                    if isinstance(t, int) and t == 0:
                        pe.wait_ge(w0_lo, 1)
                    after(pe, S0["v_ready"], t, 1)
                    for c in range(KC):
                        last = product(PS[:, B_KV, :], cT(r, c), [w[:, c, :] for w in kvw], c == 0, c == KC - 1)
                    last.then_inc(S0["kv_psum"], 1)
                if tile := s.tile(-1):
                    t, r = tile
                    after(pe, S0["q_ready"], (s.pair, s.pair - 1)[s.ring == 0])
                    after(pe, S0["s_ready"], t)
                    after(pe, S0["az"], t, 1)
                    for b in range(2):
                        for c in range(KC):
                            at = c * 2 * P + r * P + SEQ * b
                            last = nc.tensor.matmul(PS[SEQ * b:SEQ * (b + 1), B_A, c * VC:(c + 1) * VC],
                                                    qq[:, at:at + SEQ], smat[:, r, b, c * VC:(c + 1) * VC],
                                                    start=True, stop=True)
                    last.then_inc(S0["attn_psum"], 1)
                if s.ring == 0 and s.tile(0):
                    after(pe, xT_lo, s.at, -1)
                    after(pe, S0["q_exp"], s.pair, 1)
                    after(pe, S0["q_relu"], s.pair, 1)
                    if isinstance(s.at, int) and s.at == 0:
                        pe.wait_ge(w0_lo, 2)
                    for m in range(KC):
                        for c in range(KC):
                            last = product(PS[:, B_Q, m * 2 * P:(m + 1) * 2 * P],
                                           [w[:, c, m * P:(m + 1) * P] for w in qw], pair((xTh, xTl), c),
                                           c == 0, c == KC - 1)
                    last.then_inc(S0["q_psum"], 1)
                if tile := s.tile(0):
                    t, r = tile
                    after(pe, xT_lo, t)
                    after(pe, S0["gate_tanh"], t, 1)
                    after(pe, x_done[0], t, 3)
                    if isinstance(t, int) and t == 0:
                        pe.wait_ge(setup_v, 2)
                    for c in range(KC):
                        product(PS[:, B_GO, 0:D], xT(r, c), [w[:, c, :] for w in gw], c == 0, False)
                    nc.tensor.matmul(PS[:, B_GO, 0:D], one_row[:, :], bgh[:, :], start=False, stop=False)
                    nc.tensor.matmul(PS[:, B_GO, 0:D], one_row[:, :], bgl[:, :], start=False,
                                     stop=True).then_inc(S0["g_psum"], 1)
                if tile := s.tile(0):
                    t, r = tile
                    after(pe, S0["k_ready"], t)
                    after(pe, S0["v_ready"], t)
                    after(pe, S0["s_ready"], t, 1)
                    for b in range(2):
                        for c in range(KC):
                            last = nc.tensor.matmul(PS[:, B_S + b, c * VC:(c + 1) * VC],
                                                    kk[SEQ * b:SEQ * (b + 1), r, c * P:(c + 1) * P],
                                                    vx[r][SEQ * b:SEQ * (b + 1), c, :], start=True, stop=True)
                    last.then_inc(S0["ktv_psum"], 1)
                if tile := s.tile(-2):
                    t, r = tile
                    after(pe, S0["agT_lo"], t)
                    if here := s.tile(0):
                        after(pe, S0["gate_tanh"], here[0])
                    after(pe, x_done[0], t, 1)
                    for c in range(KC):
                        last = product(PS[:, B_GO, D:2 * D], aT(r, c), [w[:, c, :] for w in ow], c == 0, c == KC - 1)
                    last.then_inc(S0["o_psum"], 1)
                if tile := s.next(2):
                    transpose_x(pe, 0, *tile, B_T)
                if tile := s.tile(-1):
                    t, r = tile
                    after(pe, S0["ag_ready"], t)
                    after(pe, S0["agT_lo"], t, 1)
                    for c in range(KC):
                        last = nc.tensor.transpose(PS[:, B_TA, c * P:(c + 1) * P], ag[:, r, c * P:(c + 1) * P],
                                                   ident[:, :])
                    last.then_inc(S0["agT_psum"], 1)
                if s.is_at(TILES):
                    pe.wait_ge(w_lo, TILES)
                    route(0, 0)

            slots(pe, TILES, -2, TILES + 1, slot0)

            def hidden_T(first, n, bank):
                for i in range(n):
                    last = nc.tensor.transpose(PS[:, bank, i * P:(i + 1) * P],
                                               fh[:, (first + i) * P:(first + i + 1) * P], ident[:, :])
                last.then_inc(S1["hT_psum"], 1)

            def expert_out(first, n, start, stop):
                for i in range(first, first + n):
                    last = product(PS[:, F_O, 0:D], [w[:, i * P:(i + 1) * P] for w in (fTh, fTl)],
                                   [w[:, i, :] for w in f2w], start and i == first, stop and i == first + n - 1)
                last.then_inc(S1["down"], 1)
                return last

            def by_feature(bank, weights, right):
                for m in range(KC):
                    for c in range(KC):
                        last = product(PS[:, bank, m * 2 * P:(m + 1) * 2 * P],
                                       [w[:, c, m * P:(m + 1) * P] for w in weights], pair(right, c),
                                       c == 0, c == KC - 1)
                return last

            def pair_queries(t):
                after(pe, xT_lo, t, -1, base=2 * TILES)
                by_feature(X_Q, q1w, (xTh, xTl)).then_inc(S2["q_psum"], 1)

            def pair_keys(t):
                after(pe, ctx_lo, t, -1, base=TILES)
                after(pe, S2["clipped"], t, 1, per=2)
                by_feature(X_K, k1w, (cTh, cTl)).then_inc(S2["k_psum"], 1)

            def slot1(s):
                here, before, ahead = s.tile(0), s.tile(-1), ahead_of(s)
                if here:
                    t, r = here
                    if not s.is_at(0):
                        route(t, r)
                    first_experts(t, r)
                if ahead:
                    if here:
                        after(pe, S1["scores"], t)
                    transpose_x(pe, 1, *ahead, F_T)
                if before:
                    after(pe, S1["h"], before[0], per=3)
                    after(pe, S1["hT_lo"], before[0], per=3, extra=-2)
                    hidden_T(8, 2, F_H)
                    if s.is_at(TILES):
                        pe.wait_ge(w_lo, 2 * TILES)
                        pair_keys(0)
                    after(pe, S1["hT_lo"], before[0], per=3, extra=-1)
                    expert_out(4, 4, False, False)
                    if s.is_at(TILES):
                        pair_queries(0)
                if here:
                    after(pe, S1["h"], t, 1, per=3, extra=-1)
                    if s.is_at(0):
                        pe.wait_ge(x_done[0], TILES)
                    expert_in(t, r, F_G1, 1024).then_inc(S1["g_psum"], 1)
                    expert_in(t, r, F_U1, 1536).then_inc(S1["u_psum"], 1)
                    after(pe, S1["h"], t, per=3, extra=-2)
                    after(pe, S1["hT_lo"], t, 1, per=3)
                    hidden_T(0, 4, F_H)
                if before:
                    after(pe, S1["hT_lo"], before[0], per=3)
                    expert_out(8, 2, False, True)
                if here:
                    expert_in(t, r, F_G0, 2048).then_inc(S1["g_psum"], 1)
                    after(pe, S1["hT_lo"], t, per=3, extra=-2)
                    after(pe, x_done[1], t, 1)
                    expert_out(0, 4, True, False)
                    after(pe, S1["h"], t, per=3, extra=-1)
                    hidden_T(4, 4, F_H + 1)

            slots(pe, TILES, 0, TILES, slot1, low=2)

            def halves_T(g):
                after(pe, S3["x_ready"], g, 1, per=2)
                for k in range(2):
                    after(pe, xn_ready, g, per=2, base=3 * TILES, extra=k - 1)
                    for c in range(KC):
                        last = nc.tensor.transpose(
                            PS[:, M_T, k * P + c * SEQ:k * P + (c + 1) * SEQ].bitcast(F16),
                            mx16[:, k, c * P:(c + 1) * P], ident16[:, :])
                    last.then_inc(xT_psum, 1)

            def ffn_hidden(g, r, features):
                after(pe, S3["x_ready"], g, per=2)
                for n in features:
                    if n % 2 == 0:
                        after(pe, S3["gelu"], g, 1, per=8, extra=n - 6)
                        if isinstance(g, int) and g == 0 and M_H + n // 2 == X_O:
                            pe.wait_ge(S2["delta"], TILES)
                    for c in range(KC):
                        for w in range(2):
                            last = nc.tensor.matmul(PS[:, M_H + n // 2, (n % 2) * D:(n % 2 + 1) * D],
                                                    m0w[w][:, c, n * P:(n + 1) * P], mX[r][:, c, :],
                                                    start=c + w == 0, stop=c + w == 2)
                    if n % 2:
                        last.then_inc(S3["h_psum"], 1)

            def weighted_values(t, r):
                after(pe, S2["probs"], t)
                after(pe, S2["vb_ready"], t)
                after(pe, S2["cn_ready"], t, 1)
                if isinstance(t, int) and t == 0:
                    pe.wait_ge(x_done[1], TILES)
                for b in range(2):
                    for g in range(PAIRS):
                        c, i, j = g // PPC, g // 2 % 2, g % 2
                        last = nc.tensor.matmul(PS[SEQ * b:SEQ * (b + 1), X_C, g * PVC:(g + 1) * PVC],
                                                pp[r][:, b, i, (c * 2 + j) * SEQ:(c * 2 + j + 1) * SEQ],
                                                vb[r][:, b, g, :], start=True, stop=True)
                last.then_inc(S2["pv_psum"], 1)

            def output(t, r):
                after(pe, S2["cnT_lo"], t)
                after(pe, S2["delta"], t, 1)
                for c in range(KC):
                    last = product(PS[:, X_O, 0:D], aT(r, c), [w[:, c, :] for w in o1w], c == 0, c == KC - 1)
                last.then_inc(S2["o_psum"], 1)

            def scores(t, r, pair_at):
                after(pe, S2["kb_ready"], pair_at, per=4)
                after(pe, S2["q_ready"], pair_at, per=4)
                after(pe, S2["clipped"], t, 2, per=2)
                for b in range(2):
                    for c in range(KC):
                        for i in range(2):
                            f = slice(P // 2 * i, P // 2 * (i + 1))
                            last = nc.tensor.matmul(
                                PS[:, scores_bank(r) + i, (b * KC + c) * P:(b * KC + c + 1) * P],
                                kb[f, r, c, b, :, :].rearrange("p h k -> p (h k)"),
                                qb[f, r, c, b, :, :].rearrange("p j q -> p (j q)"), start=True, stop=True)
                last.then_inc(S2["scores_psum"], 1)

            def slot2(s):
                if s.ring == 0 and s.tile(0):
                    if not s.is_at(0):
                        pair_keys(s.at)
                if tile := s.tile(0):
                    t, r = tile
                    after(pe, ctx_lo, t, base=TILES)
                    after(pe, S2["vb_ready"], t, 1)
                    for c in range(KC):
                        last = product(PS[:, X_V, 0:D], cT(r, c), [w[:, c, :] for w in v1w], c == 0, c == KC - 1)
                    last.then_inc(S2["v_psum"], 1)
                if s.is_at(TILES):
                    pe.wait_ge(S2["clipped"], 2 * TILES)
                    ffn_hidden(0, 0, EARLY)
                if tile := s.tile(-2):
                    t, r = tile
                    after(pe, S2["cn_ready"], t)
                    if t_ahead := s.tile(1):
                        after(pe, xT_lo, t_ahead[0], base=2 * TILES)
                    if s.is_at(TILES):
                        pe.wait_ge(S3["x_ready"], PER_GROUP)
                    for c in range(KC):
                        last = nc.tensor.transpose(PS[:, X_T, D + c * P:D + (c + 1) * P], cn[:, r, c * P:(c + 1) * P],
                                                   ident[:, :])
                    last.then_inc(S2["cnT_psum"], 1)
                if s.ring == 0:
                    if s.tile(0) and not s.is_at(0):
                        pair_queries(s.at)
                    if s.tile(-1):
                        weighted_values(*s.tile(-1))
                if s.ring == 1 and s.tile(0):
                    scores(*s.tile(0), s.pair)
                if s.tile(-2):
                    output(*s.tile(-2))
                if tile := s.tile(2):
                    if before := s.tile(-2):
                        after(pe, S2["cnT_lo"], before[0])
                    transpose_x(pe, 2, *tile, X_T)
                if s.ring == 0 and s.tile(0):
                    scores(*s.tile(0), s.pair)
                if s.is_at(TILES - 1):
                    pe.wait_ge(setup_v, 6)
                    pe.wait_ge(S2["cnT_lo"], TILES - 2)
                    halves_T(0)
                if s.ring == 1 and s.tile(-1):
                    weighted_values(*s.tile(-1))

            slots(pe, TILES, 0, TILES + 1, slot2)

            def slot3(s):
                if tile := s.tile(0):
                    ffn_hidden(*tile, LATE if s.is_at(0) else range(NFF))
                if tile := s.tile(1):
                    halves_T(tile[0])
                if tile := s.tile(-1):
                    g, r = tile
                    after(pe, S3["d_ready"], g, per=4)
                    after(pe, S3["e16"], g, 1)
                    for k in range(2):
                        for n in range(NFF):
                            for w in range(2):
                                last = nc.tensor.matmul(PS[:, M_O, k * D:(k + 1) * D],
                                                        mD[r][:, n, k * P:(k + 1) * P], m1w[w][:, n, :],
                                                        start=n + w == 0, stop=n + w == NFF)
                    last.then_inc(S3["o_psum"], 1)

            slots(pe, GROUPS, 0, GROUPS, slot3, low=2)


def by_contraction(w):
    n, k = w.shape
    return np.ascontiguousarray(w.T.reshape(k // P, P, n).transpose(1, 0, 2)).reshape(P, -1)


def laid_out(i):
    i = {k: np.asarray(v) for k, v in i.items()}
    f = np.float32
    lane = np.arange(P)
    a = {"x": i["x"].reshape(TOKENS, D)}
    a["ctxT"] = i["ctx_2048"].reshape(TILES, P, KC, P).transpose(0, 3, 2, 1).reshape(TILES, P, D)
    a["w_l0"] = np.concatenate([by_contraction(i["L0_xattn_" + n]) for n in ("Wkv", "Wq", "Wg", "Wo")], 1)
    gates, ups = (i["L0_ffn_" + n].reshape(2, 4 * EH, D) for n in ("w_gate", "w_up"))
    w1 = np.concatenate([gates[0], ups[0], gates[1], ups[1], i["L0_ffn_sh_gate"], i["L0_ffn_sh_up"],
                         i["L0_ffn_gate_w"], i["L0_ffn_se_gate_w"], np.zeros((1, D), f)])
    ffn = np.concatenate([by_contraction(w1), i["L0_ffn_w_down"].transpose(2, 0, 1).reshape(P, -1),
                          by_contraction(i["L0_ffn_sh_down"]), np.zeros((P, FFN_COLS - FFN_USED), f)], 1)
    a["w_ffn"] = ffn.reshape(P, TILES, FFN_CHUNK).transpose(1, 0, 2)
    l1 = np.concatenate([by_contraction(i[n]) for n in ("L1_xattn_Wq", "L1_xattn_Wk", "L1_xattn_Wv", "L1_xattn_Wo",
                                                        "L1_ffn_W0", "L1_ffn_W1")], 1)
    a["w_l1"] = l1.reshape(P, TILES, L1_CHUNK).transpose(1, 0, 2)
    a["rows"] = np.broadcast_to(np.stack([i[n] for n in ("L1_xattn_bv", "L1_xattn_bo", "L1_xattn_ln_gamma",
                                                         "L1_xattn_ln_beta", "L1_ffn_bias1")]), (P, 5, D))
    a["cols"] = np.concatenate([i[n].reshape(-1, P).T for n in ("L1_xattn_bq", "L1_xattn_bk", "L1_ffn_bias0")], 1)
    a["bg"] = i["L0_xattn_bg"].reshape(1, D)
    a["rs"] = np.broadcast_to(i["L1_xattn_residual_scale"].reshape(1, 1), (P, 1))
    mask = i["mask_BxS2_ik0"].T
    a["mask"] = np.concatenate([mask, mask], 0)
    a["ident"] = np.eye(P, dtype=f)
    own = (lane[:, None] // HD == np.arange(VC)[None, :] // HD)
    own[:, P:] = lane[:, None] // HD == np.arange(HPC)[None, :]
    a["blockmask"] = np.concatenate([own, own], 1).astype(f)
    a["headmask"] = np.concatenate([0.25 * (lane[:, None] // HD % 2 == np.arange(2)),
                                    lane[:, None] // (2 * HD) % 2 == np.arange(2)], 1).astype(f)
    a["iota8"] = np.tile(np.arange(EXPERTS, dtype=f), (P, 1))
    return {k: np.ascontiguousarray(v) for k, v in a.items()}


def kernel(**inputs):
    import concourse.bacc as _bacc
    from concourse.bass_utils import run_bass_kernel_spmd as _run

    nc = _bacc.Bacc("TRN2", target_bir_lowering=False, num_devices=1, dynamic_dma_scratch_size=2048)
    arrays = laid_out(inputs)
    args = {n: nc.dram_tensor("in_" + n, a.shape, mybir.dt.from_np(a.dtype), kind="ExternalInput").ap()
            for n, a in arrays.items()}
    out = nc.dram_tensor("out", (TOKENS, D), F32, kind="ExternalOutput").ap()
    build(nc, args, out)
    r = _run(nc, [{"in_" + n: a for n, a in arrays.items()}], core_ids=[0])
    return r.results[0]["out"].reshape(BATCHES, SEQ, D)
```
